# Optimizing a Trainium2 kernel written in Bass

```python
import numpy as np
import jax
import jax.numpy as jnp

def _softmax(x, axis=-1):
    return jax.nn.softmax(x, axis=axis)

def _gelu(x):
    return jax.nn.gelu(x, approximate=True)

def _silu(x):
    return jax.nn.silu(x)

def _sigmoid(x):
    return jax.nn.sigmoid(x)

def _layernorm(x, axis=-1, eps=1e-05):
    m = jnp.mean(x, axis=axis, keepdims=True)
    v = jnp.var(x, axis=axis, keepdims=True)
    return (x - m) / jnp.sqrt(v + eps)

def _scatter_add(tgt, idx, src, axis=0):
    return tgt.at[idx].add(src)

def _segment_sum(src, seg, n):
    return jax.ops.segment_sum(src, seg, n)
kernel_name = 'mk_gnn_preln_d2_gnn_r8_b901d6'

def setup_inputs(seed: int=0):
    np.random.seed(seed)
    _w = jnp.asarray

    def _rec_inputs():
        import jax
        import jax.numpy as jnp
        _gk = jax.random.key(seed)
        x = -1.686e-05 + 1 * jax.random.normal(jax.random.fold_in(_gk, 1), (6250, 160), jnp.float32)
        _s = jax.random.randint(jax.random.fold_in(_gk, 2), (50000,), 0, 6250, jnp.int32)
        _d = jax.random.randint(jax.random.fold_in(_gk, 3), (50000,), 0, 6250, jnp.int32)
        _loop = jnp.arange(6250, dtype=jnp.int32)
        src = jnp.concatenate([_s, _d, _loop])
        dst = jnp.concatenate([_d, _s, _loop])
        _o = jnp.argsort(dst, stable=True)
        src = src[_o]
        dst = dst[_o]
        edge_attr_12 = jax.random.uniform(jax.random.fold_in(_gk, 12), (106250, 12), jnp.float32, 0.0, 1)
        edge_attr_4 = 0.000486536 + 0.999406 * jax.random.normal(jax.random.fold_in(_gk, 13), (106250, 4), jnp.float32)
        edge_attr_64 = 0.000152336 + 1.00009 * jax.random.normal(jax.random.fold_in(_gk, 14), (106250, 64), jnp.float32)
        node_vec1 = jax.random.uniform(jax.random.fold_in(_gk, 15), (6250, 1), jnp.float32, 0.0, 0.999994)
        return (x, src, dst, edge_attr_12, edge_attr_4, edge_attr_64, node_vec1)
    x, src, dst, edge_attr_12, edge_attr_4, edge_attr_64, node_vec1 = _rec_inputs()

    def _L0_gnn_setup():
        import jax, jax.numpy as jnp
        import numpy as np
        N = 6250
        E = 50000
        MUL0 = 64
        MUL1 = 32
        NEF = 12
        RN = 100
        NUM_NEIGHBORS = 8.0
        WNUM = MUL0 + MUL0 + MUL1 + MUL1

        def _split(x):
            return (x[:, :MUL0], x[:, MUL0:].reshape(-1, MUL1, 3))

        def _fctp_scalar_attr(x0, x1, z, Ws, Wv):
            s = x0 @ Ws * z / np.sqrt(Ws.shape[0])
            v = jnp.einsum('nuc,uw->nwc', x1, Wv) * z[:, :, None] / np.sqrt(Wv.shape[0])
            return (s, v)
        key = jax.random.key(seed)
        ks = jax.random.split(key, 16)
        return {'node_input': jax.random.normal(ks[0], (N, MUL0 + 3 * MUL1), jnp.float32), 'node_attr': jax.random.uniform(ks[1], (N, 1), dtype=jnp.float32), 'edge_src': jax.random.randint(ks[2], (E,), 0, N), 'edge_dst': jax.random.randint(ks[3], (E,), 0, N), 'edge_attr': jax.random.normal(ks[4], (E, 4), jnp.float32), 'edge_features': jax.random.uniform(ks[5], (E, NEF), dtype=jnp.float32), 'W_sc0': jax.random.normal(ks[6], (MUL0, MUL0), jnp.float32), 'W_sc1': jax.random.normal(ks[7], (MUL1, MUL1), jnp.float32), 'W_l1_0': jax.random.normal(ks[8], (MUL0, MUL0), jnp.float32), 'W_l1_1': jax.random.normal(ks[9], (MUL1, MUL1), jnp.float32), 'W_fc1': jax.random.normal(ks[10], (NEF, RN), jnp.float32), 'W_fc2': jax.random.normal(ks[11], (RN, WNUM), jnp.float32), 'W_l2_0': jax.random.normal(ks[12], (MUL0 + MUL1, MUL0), jnp.float32), 'W_l2_1': jax.random.normal(ks[13], (MUL0 + MUL1, MUL1), jnp.float32)}
    _L0_gnn_all = _L0_gnn_setup()
    _L0_gnn_in = {k: v for k, v in _L0_gnn_all.items() if k in ('W_sc0', 'W_sc1', 'W_l1_0', 'W_l1_1', 'W_fc1', 'W_fc2', 'W_l2_0', 'W_l2_1')}
    del _L0_gnn_all

    def _L1_gnn_setup():
        import jax, jax.numpy as jnp
        import numpy as np
        N = 6250
        E = 62500
        MUL0 = 64
        MUL1 = 32
        DIM_KEY = 64
        WEIGHT_NUMEL = 64 + 64 + 32 + 32 + 32

        def _irreps_linear(s, v, w0, w1):
            so = s @ w0 * w0.shape[0] ** (-0.5)
            vo = jnp.einsum('nui,uv->nvi', v, w1) * w1.shape[0] ** (-0.5)
            return (so, vo)
        key = jax.random.key(seed)
        ks = jax.random.split(key, 12)
        x = jax.random.normal(ks[0], (N, MUL0 + 3 * MUL1), dtype=jnp.float32)
        edge_src = jax.random.randint(ks[1], (E,), 0, N, dtype=jnp.int32)
        edge_dst = jax.random.randint(ks[2], (E,), 0, N, dtype=jnp.int32)
        edge_query = jax.random.normal(ks[3], (E, DIM_KEY), dtype=jnp.float32)
        edge_sh = jax.random.normal(ks[4], (E, 4), dtype=jnp.float32)
        si_w0 = jax.random.normal(ks[5], (MUL0, MUL0), dtype=jnp.float32)
        si_w1 = jax.random.normal(ks[6], (MUL1, MUL1), dtype=jnp.float32)
        lin1_w0 = jax.random.normal(ks[7], (MUL0, MUL0), dtype=jnp.float32)
        lin1_w1 = jax.random.normal(ks[8], (MUL1, MUL1), dtype=jnp.float32)
        tp_weight = jax.random.normal(ks[9], (DIM_KEY, WEIGHT_NUMEL), dtype=jnp.float32)
        lin2_w0 = jax.random.normal(ks[10], (MUL0 + MUL1, MUL0), dtype=jnp.float32)
        lin2_w1 = jax.random.normal(ks[11], (MUL0 + MUL1, MUL1), dtype=jnp.float32)
        return {'x': x, 'edge_src': edge_src, 'edge_dst': edge_dst, 'edge_query': edge_query, 'edge_sh': edge_sh, 'si_w0': si_w0, 'si_w1': si_w1, 'lin1_w0': lin1_w0, 'lin1_w1': lin1_w1, 'tp_weight': tp_weight, 'lin2_w0': lin2_w0, 'lin2_w1': lin2_w1}
    _L1_gnn_all = _L1_gnn_setup()
    _L1_gnn_in = {k: v for k, v in _L1_gnn_all.items() if k in ('si_w0', 'si_w1', 'lin1_w0', 'lin1_w1', 'tp_weight', 'lin2_w0', 'lin2_w1')}
    del _L1_gnn_all
    return {'x': x, 'src': src, 'dst': dst, 'edge_attr_12': edge_attr_12, 'edge_attr_4': edge_attr_4, 'edge_attr_64': edge_attr_64, 'node_vec1': node_vec1, 'L0_gnn_W_sc0': _L0_gnn_in['W_sc0'], 'L0_gnn_W_sc1': _L0_gnn_in['W_sc1'], 'L0_gnn_W_l1_0': _L0_gnn_in['W_l1_0'], 'L0_gnn_W_l1_1': _L0_gnn_in['W_l1_1'], 'L0_gnn_W_fc1': _L0_gnn_in['W_fc1'], 'L0_gnn_W_fc2': _L0_gnn_in['W_fc2'], 'L0_gnn_W_l2_0': _L0_gnn_in['W_l2_0'], 'L0_gnn_W_l2_1': _L0_gnn_in['W_l2_1'], 'L1_gnn_si_w0': _L1_gnn_in['si_w0'], 'L1_gnn_si_w1': _L1_gnn_in['si_w1'], 'L1_gnn_lin1_w0': _L1_gnn_in['lin1_w0'], 'L1_gnn_lin1_w1': _L1_gnn_in['lin1_w1'], 'L1_gnn_tp_weight': _L1_gnn_in['tp_weight'], 'L1_gnn_lin2_w0': _L1_gnn_in['lin2_w0'], 'L1_gnn_lin2_w1': _L1_gnn_in['lin2_w1']}

def reference(x, src, dst, edge_attr_12, edge_attr_4, edge_attr_64, node_vec1, L0_gnn_W_sc0, L0_gnn_W_sc1, L0_gnn_W_l1_0, L0_gnn_W_l1_1, L0_gnn_W_fc1, L0_gnn_W_fc2, L0_gnn_W_l2_0, L0_gnn_W_l2_1, L1_gnn_si_w0, L1_gnn_si_w1, L1_gnn_lin1_w0, L1_gnn_lin1_w1, L1_gnn_tp_weight, L1_gnn_lin2_w0, L1_gnn_lin2_w1):
    import jax
    import jax.numpy as jnp

    def _L0_gnn_ref(node_input, node_attr, edge_src, edge_dst, edge_attr, edge_features, W_sc0, W_sc1, W_l1_0, W_l1_1, W_fc1, W_fc2, W_l2_0, W_l2_1):
        import jax, jax.numpy as jnp
        import numpy as np
        N = 6250
        E = 50000
        MUL0 = 64
        MUL1 = 32
        NEF = 12
        RN = 100
        NUM_NEIGHBORS = 8.0
        WNUM = MUL0 + MUL0 + MUL1 + MUL1

        def _split(x):
            return (x[:, :MUL0], x[:, MUL0:].reshape(-1, MUL1, 3))

        def _fctp_scalar_attr(x0, x1, z, Ws, Wv):
            s = x0 @ Ws * z / np.sqrt(Ws.shape[0])
            v = jnp.einsum('nuc,uw->nwc', x1, Wv) * z[:, :, None] / np.sqrt(Wv.shape[0])
            return (s, v)
        x0, x1 = _split(node_input)
        z = node_attr
        s0, s1 = _fctp_scalar_attr(x0, x1, z, W_sc0, W_sc1)
        h0, h1 = _fctp_scalar_attr(x0, x1, z, W_l1_0, W_l1_1)
        h = jax.nn.silu(edge_features @ W_fc1 / np.sqrt(NEF))
        w = h @ W_fc2 / np.sqrt(RN)
        w0 = w[:, :MUL0]
        w1 = w[:, MUL0:2 * MUL0]
        w2 = w[:, 2 * MUL0:2 * MUL0 + MUL1]
        w3 = w[:, 2 * MUL0 + MUL1:]
        e0 = h0[edge_src]
        e1 = h1[edge_src]
        y0 = edge_attr[:, :1]
        y1 = edge_attr[:, 1:]
        m0a = w0 * e0 * y0
        m0b = w3 * jnp.einsum('eui,ei->eu', e1, y1) / np.sqrt(3.0)
        m1a = (w1 * e0)[:, :, None] * y1[:, None, :]
        m1b = w2[:, :, None] * (e1 * y0[:, :, None])
        mid_s = jnp.concatenate([m0a, m0b], axis=1)
        mid_v = jnp.concatenate([m1a, m1b], axis=1)
        inv = 1.0 / np.sqrt(NUM_NEIGHBORS)
        ns = jax.ops.segment_sum(mid_s, edge_dst, num_segments=N) * inv
        nv = jax.ops.segment_sum(mid_v, edge_dst, num_segments=N) * inv
        o0, o1 = _fctp_scalar_attr(ns, nv, z, W_l2_0, W_l2_1)
        c_s, c_x = (np.sin(np.pi / 8), np.cos(np.pi / 8))
        out0 = c_s * s0 + c_x * o0
        out1 = c_s * s1 + c_x * o1
        return jnp.concatenate([out0, out1.reshape(N, -1)], axis=1)

    def _L1_gnn_ref(x, edge_src, edge_dst, edge_query, edge_sh, si_w0, si_w1, lin1_w0, lin1_w1, tp_weight, lin2_w0, lin2_w1):
        import jax, jax.numpy as jnp
        import numpy as np
        N = 6250
        E = 62500
        MUL0 = 64
        MUL1 = 32
        DIM_KEY = 64
        WEIGHT_NUMEL = 64 + 64 + 32 + 32 + 32

        def _irreps_linear(s, v, w0, w1):
            so = s @ w0 * w0.shape[0] ** (-0.5)
            vo = jnp.einsum('nui,uv->nvi', v, w1) * w1.shape[0] ** (-0.5)
            return (so, vo)
        n = x.shape[0]
        s_in = x[:, :MUL0]
        v_in = x[:, MUL0:].reshape(n, MUL1, 3)
        si_s, si_v = _irreps_linear(s_in, v_in, si_w0, si_w1)
        s_skip = jnp.concatenate([si_s, si_v.reshape(n, 3 * MUL1)], axis=1)
        h_s, h_v = _irreps_linear(s_in, v_in, lin1_w0, lin1_w1)
        es = h_s[edge_src]
        ev = h_v[edge_src]
        w = edge_query @ tp_weight
        w0, w1, w2a, w2b, w3 = (w[:, :64], w[:, 64:128], w[:, 128:160], w[:, 160:192], w[:, 192:224])
        sh_s = edge_sh[:, 0:1]
        sh_v = edge_sh[:, 1:4]
        out0 = w0 * es * sh_s
        out1 = (w1 * es)[:, :, None] * sh_v[:, None, :]
        out2 = 2.0 ** (-0.5) * (w2a * sh_s)[:, :, None] * ev + 0.5 * w2b[:, :, None] * jnp.cross(ev, sh_v[:, None, :])
        out3 = 3.0 ** (-0.5) * w3 * jnp.sum(ev * sh_v[:, None, :], axis=-1)
        edge_x = jnp.concatenate([out0, out1.reshape(-1, 3 * MUL0), out2.reshape(-1, 3 * MUL1), out3], axis=1)
        agg = jax.ops.segment_sum(edge_x, edge_dst, num_segments=n)
        a0 = agg[:, :64]
        a1 = agg[:, 64:256].reshape(n, 64, 3)
        a2 = agg[:, 256:352].reshape(n, 32, 3)
        a3 = agg[:, 352:384]
        scal = jnp.concatenate([a0, a3], axis=1) @ lin2_w0 * (MUL0 + MUL1) ** (-0.5)
        vec = jnp.einsum('nui,uv->nvi', jnp.concatenate([a1, a2], axis=1), lin2_w1) * (MUL0 + MUL1) ** (-0.5)
        conv_out = jnp.concatenate([scal, vec.reshape(n, 3 * MUL1)], axis=1)
        return s_skip + conv_out / 10.0
    h = jnp.maximum(_layernorm(x, axis=-1), 0.0)
    x = x + _L0_gnn_ref(h, node_vec1, src, dst, edge_attr_4, edge_attr_12, L0_gnn_W_sc0, L0_gnn_W_sc1, L0_gnn_W_l1_0, L0_gnn_W_l1_1, L0_gnn_W_fc1, L0_gnn_W_fc2, L0_gnn_W_l2_0, L0_gnn_W_l2_1)
    h = jnp.maximum(_layernorm(x, axis=-1), 0.0)
    x = x + _L1_gnn_ref(h, src, dst, edge_attr_64, edge_attr_4, L1_gnn_si_w0, L1_gnn_si_w1, L1_gnn_lin1_w0, L1_gnn_lin1_w1, L1_gnn_tp_weight, L1_gnn_lin2_w0, L1_gnn_lin2_w1)
    return x

_drawn_inputs = setup_inputs


def setup_inputs(seed=0):
    import zlib

    import numpy as np

    out = dict(_drawn_inputs(seed))
    spreads = {}
    factors = {}
    for name, (base, spread) in spreads.items():
        noise = np.random.default_rng([zlib.crc32(name.encode()), seed]).standard_normal(out[name].shape)
        drawn = base * np.exp(spread * noise) if base else spread * noise
        out[name] = jnp.asarray(drawn.astype(out[name].dtype))
    for name, factor in factors.items():
        out[name] = (out[name] * factor).astype(out[name].dtype)
    return out
```

```python
import math
from contextlib import ExitStack

import numpy as np

import concourse.bass as bass
from concourse import mybir

F32 = mybir.dt.float32
BF16 = mybir.dt.bfloat16
I32 = mybir.dt.int32
ALU = mybir.AluOpType
ACT = mybir.ActivationFunctionType
AX = mybir.AxisListType

P = 128
N, E = 6250, 106250
S0, V1 = 64, 32
F = S0 + 3 * V1
NEF, RN, DK = 12, 100, 64
EPS = 1e-5

WIN = 32
CHUNKS = 3
SUP = CHUNKS * P
QUAD = 4
NQUAD = -(-E // (SUP * QUAD))
NSUP = NQUAD * QUAD
NCH = NSUP * CHUNKS
EPAD = NSUP * SUP
FIRST_EMPTY = -(-E // SUP)

NT = 2 * -(-N // (2 * P))
NPAD = NT * P
ROWS = NPAD + P
FG = NSUP // QUAD

PARTS = 3
KST = PARTS * PARTS * NEF
SEG = 8
SPLIT_ROWS = NEF * SEG
SPLIT_LEN = EPAD // SEG
SPLIT_STEPS = 14
SPLIT_W = SPLIT_LEN // SPLIT_STEPS

C_S, C_X = math.sin(math.pi / 8), math.cos(math.pi / 8)


class Layer:
    PK0 = F

    def __init__(self, n):
        self.n = n
        self.wcols = 2 * S0 + (2 + n) * V1
        self.kin = RN if n == 0 else DK
        self.pcols = 2 * F + n * 3 * V1
        self.d_col = 2 * S0 + V1 * (1 + n)
        self.agg = self.pcols - F
        self.k1 = S0 + V1 if n == 0 else P
        self.k2 = 2 * V1 if n == 0 else P


L0, L1 = Layer(0), Layer(1)


def other_two(c):
    return [a for a in range(3) if a != c]


def wait_for(eng, sem, value):
    if not isinstance(value, int) or value > 0:
        eng.wait_ge(sem, value)


def waits_alone(eng, sem, value, least, *more):
    pairs = [(sem, value), *more]
    if isinstance(value, int):
        for s, v in pairs:
            wait_for(eng, s, v)
    else:
        pairs = [(s, eng.to_reg(v)) for s, v in pairs]
        eng.wait_ge(sem, least)
        for s, v in pairs:
            eng.wait_ge(s, v)


def within(step, first, last):
    return not isinstance(step, int) or first <= step < last


def rolled(eng, count, body):
    body(0)
    with eng.Fori(1, count - 1) as i:
        body(i)
    body(count - 1)


def gnn_kernel(nc, x, z_t, src_t, dst_t, dst_flat, base_row, y_t, rad_t, query_t,
               w_sc0, w_sc1, w_l10, w_l11, w_fc1, w_fc2, w_l20, w_l21,
               si_w0, si_w1, lin1_w0, lin1_w1, tp_w, lin2_w0, lin2_w1, out):
    ctx = ExitStack()
    with ctx:
        ctx.enter_context(nc.allow_non_contiguous_dma(reason="per-edge columns and per-channel weights, a few bytes per partition"))

        def sb(name, shape, dt=F32):
            return ctx.enter_context(nc.sbuf_tensor(name, shape, dt))

        def sem(name):
            return ctx.enter_context(nc.semaphore(name))

        def dram(name, shape, dt=F32):
            return nc.dram_tensor(name, shape, dt, kind="Internal").ap()

        table = [dram(f"table{n}", (NPAD, F)) for n in range(2)]
        acc = [dram(f"acc{n}", (2, ROWS, F)) for n in range(2)]
        meta_d = dram("meta_d", (P, NCH, 5))
        split_d = dram("split_d", (PARTS * NEF, EPAD), BF16)

        X = sb("X", [P, NT * F])
        z_sb = sb("z_sb", [P, NT])
        ident = sb("ident", [P, P])
        win_i = sb("win_i", [P, WIN], I32)
        win = sb("win", [P, WIN])
        flag = sb("flag", [1, 1], I32)
        zero = sb("zero", [P, F])
        stats = sb("stats", [P, NT * 6])
        mean = sb("mean", [P, NT])
        rstd = sb("rstd", [P, NT])
        shift = sb("shift", [P, NT])
        base_sb = sb("base_sb", [1, NSUP + 2], I32)
        ra = [sb(f"ra{n}", [S0, 2 * S0]) for n in range(2)]
        rb = [sb(f"rb{n}", [3 * V1, 6 * V1]) for n in range(2)]
        r1 = [sb(f"r1_{n}", [P, 4, F]) for n in range(2)]
        r2 = [sb(f"r2_{n}", [P, F]) for n in range(2)]
        fc1_st = sb("fc1_st", [KST, RN], BF16)
        fc2_sb = sb("fc2_sb", [RN, L0.wcols])
        tp_sb = sb("tp_sb", [DK, L1.wcols])
        hn = sb("hn", [P, 2, F])
        hT = sb("hT", [P, 2, 2, P])
        rows2 = sb("rows2", [P, 2, F])
        accin = sb("accin", [P, 2, 2, F])
        idx = sb("idx", [P, QUAD, CHUNKS], I32)
        meta = sb("meta", [P, QUAD, CHUNKS, 5])
        rad = sb("rad", [KST, QUAD, SUP], BF16)
        query = sb("query", [DK, QUAD, SUP])
        G = sb("G", [P, QUAD, CHUNKS, F])
        hid = sb("hid", [RN, 2, SUP])
        eq = sb("eq", [P, 2, CHUNKS, WIN])
        S = sb("S", [P, 2, CHUNKS, 4, WIN])
        Pr = sb("Pr", [P, 2, CHUNKS, L1.pcols])
        agg_sb = sb("agg_sb", [P, 2, F])
        T1 = sb("T1", [P, 4, QUAD, WIN])
        T2 = sb("T2", [P, QUAD, WIN])
        sums = sb("sums", [P, F])
        g_dst = sb("g_dst", [P, 1], I32)
        g_row = sb("g_row", [P, P], I32)
        g_dstf = sb("g_dstf", [P, 1])
        g_rowf = sb("g_rowf", [P, P])
        g_y = sb("g_y", [P, 4])
        g_eq = sb("g_eq", [P, P])
        g_low = sb("g_low", [P, P])
        g_dead = sb("g_dead", [P, 1])
        g_deadi = sb("g_deadi", [P, 1], I32)
        g_tmp = sb("g_tmp", [P, P])
        g_dup = sb("g_dup", [P, 2])
        g_to = sb("g_to", [P, 1], I32)
        g_S = sb("g_S", [P, 4, P])
        g_agg = sb("g_agg", [P, 4, F])

        wps = [ctx.enter_context(nc.psum_tensor(f"wps{b}", [P, 4, 256], F32)) for b in range(2)]
        aps = [ctx.enter_context(nc.psum_tensor(f"aps{b}", [P, 512], F32)) for b in range(2)]
        hps = ctx.enter_context(nc.psum_tensor("hps", [P, 512], F32))
        tps = ctx.enter_context(nc.psum_tensor("tps", [P, 512], F32))

        def x_tile(t):
            return X[:, bass.ds(t * F, F)]

        def setup():
            setup_ctx = ExitStack()
            with setup_ctx:
                def tmp(name, shape, dt=F32):
                    return setup_ctx.enter_context(nc.sbuf_tensor(name, shape, dt))

                dst_i = tmp("dst_i", [P, NCH], I32)
                dst_f = tmp("dst_f", [P, NCH])
                base_bc = tmp("base_bc", [P, NSUP], I32)
                base_f = tmp("base_f", [P, NSUP])
                y_sb = tmp("y_sb", [P, NCH * 4])
                meta_sb = tmp("meta_sb", [P, NCH, 5])
                by_sup = tmp("by_sup", [FG, QUAD * SUP], I32)
                by_sup_f = tmp("by_sup_f", [FG, QUAD, SUP])
                b_i = tmp("b_i", [FG, 2, QUAD], I32)
                b_f = tmp("b_f", [FG, 2, QUAD])
                ext = tmp("ext", [FG, 5, QUAD])
                worst = tmp("worst", [FG, 1])
                worst1 = tmp("worst1", [1, 1])
                u0 = [tmp(f"u0_{n}", [P, S0]) for n in range(2)]
                u1 = [tmp(f"u1_{n}", [P, V1]) for n in range(2)]
                v1 = [tmp(f"v1_{n}", [P, V1]) for n in range(2)]
                w12 = tmp("w12", [NEF, RN])
                w12r = tmp("w12r", [NEF, RN])
                w12p = tmp("w12p", [NEF, PARTS, RN], BF16)
                rad_f = tmp("rad_f", [SPLIT_ROWS, 2, SPLIT_W])
                rad_r = tmp("rad_r", [SPLIT_ROWS, 2, SPLIT_W])
                rad_p = tmp("rad_p", [SPLIT_ROWS, 2, PARTS, SPLIT_W], BF16)

                x_in = sem("x_in")
                small_in = sem("small_in")
                big_in = sem("big_in")
                consts = sem("consts")
                zeroed = sem("zeroed")
                w_in = sem("w_in")
                weights = sem("weights")
                w_split = sem("w_split")
                fc1_in = sem("fc1_in")
                acc_zero = sem("acc_zero")
                y_copied = sem("y_copied")
                meta_done = sem("meta_done")
                meta_out = sem("meta_out")
                chk = sem("chk")
                chk_t = sem("chk_t")
                d_chain = sem("d_chain")
                rad_in = [sem(f"rad_in{b}") for b in range(2)]
                rad_hi = sem("rad_hi")
                rad_rest = sem("rad_rest")
                rad_mid = sem("rad_mid")
                rad_lo = sem("rad_lo")
                rad_out = [sem(f"rad_out{b}") for b in range(2)]
                stat = sem("stat")
                rad_src = rad_t.rearrange("i (s f) -> (i s) f", s=SEG)

                with nc.Block() as block:
                    @block.sync
                    def _(sp):
                        def load(s):
                            b = s % 2
                            if s >= 2:
                                sp.wait_ge(rad_hi, s - 1)
                                sp.wait_ge(rad_rest, s - 1)
                            sp.dma_start(rad_f[:, b, :], rad_src[:, s * SPLIT_W:(s + 1) * SPLIT_W]).then_inc(rad_in[b], 16)

                        def store(s):
                            b = s % 2
                            sp.wait_ge(rad_lo, s + 1)
                            sp.wait_ge(rad_mid, s + 1)
                            for a in range(PARTS):
                                dst = split_d[a * NEF:(a + 1) * NEF, :].rearrange("i (s f) -> (i s) f", s=SEG)
                                sp.dma_start(dst[:, s * SPLIT_W:(s + 1) * SPLIT_W], rad_p[:, b, a, :]).then_inc(rad_out[b], 16)

                        load(0)
                        sp.dma_start(X[:, :].rearrange("p (t f) -> p t f", f=F), x.rearrange("(t p) f -> p t f", p=P)).then_inc(x_in, 16)
                        load(1)
                        for s in range(SPLIT_STEPS):
                            store(s)
                            if s + 2 < SPLIT_STEPS:
                                load(s + 2)
                            if s == 2:
                                sp.wait_ge(meta_done, 1)
                                sp.wait_ge(y_copied, 1)
                                sp.dma_start(meta_d, meta_sb[:, :, :]).then_inc(meta_out, 16)
                        for b in range(2):
                            sp.wait_ge(rad_out[b], 16 * PARTS * SPLIT_STEPS // 2)
                        sp.wait_ge(meta_out, 16)

                    @block.gpsimd
                    def _(pool):
                        pool.memset(ident[:, :], 0.0).then_inc(consts, 1)
                        pool.memset(g_low[:, :], 1.0).then_inc(consts, 1)
                        pool.iota(win_i[:, :], [[1, WIN]], base=0, channel_multiplier=0).then_inc(consts, 1)
                        pool.iota(g_deadi[:, :], [[0, 1]], base=NPAD, channel_multiplier=1).then_inc(consts, 1)
                        pool.wait_ge(consts, 4)
                        pool.affine_select(out=ident[:, :], in_=ident[:, :], compare_op=ALU.not_equal, fill=1.0,
                                           base=0, pattern=[[-1, P]], channel_multiplier=1).then_inc(consts, 1)
                        pool.affine_select(out=g_low[:, :], in_=g_low[:, :], compare_op=ALU.is_gt, fill=0.0,
                                           base=0, pattern=[[-1, P]], channel_multiplier=1).then_inc(consts, 1)
                        for s in range(SPLIT_STEPS + 1):
                            if s < SPLIT_STEPS:
                                b = s % 2
                                pool.wait_ge(rad_hi, s + 1)
                                if s >= 2:
                                    pool.wait_ge(rad_mid, s - 1)
                                    pool.wait_ge(rad_lo, s - 1)
                                pool.tensor_tensor(rad_r[:, b, :], rad_f[:, b, :], rad_p[:, b, 0, :], ALU.subtract).then_inc(rad_rest, 1)
                            if s >= 1:
                                b = (s - 1) % 2
                                pool.wait_ge(rad_rest, s)
                                pool.wait_ge(rad_mid, s)
                                pool.tensor_tensor(rad_p[:, b, 2, :], rad_r[:, b, :], rad_p[:, b, 1, :], ALU.subtract).then_inc(rad_lo, 1)

                    @block.scalar
                    def _(act):
                        act.dma_start(dst_i[:, :], dst_t).then_inc(small_in, 16)
                        act.dma_start(base_bc[:, :], base_row[0, 0:NSUP].partition_broadcast(P)).then_inc(small_in, 16)
                        act.dma_start(by_sup[:, :], dst_flat.rearrange("(g e) -> g e", g=FG)).then_inc(small_in, 16)
                        act.dma_start(b_i[:, 0, :], base_row[0, 0:NSUP].rearrange("(g q) -> g q", q=QUAD)).then_inc(small_in, 16)
                        act.dma_start(b_i[:, 1, :], base_row[0, 2:NSUP + 2].rearrange("(g q) -> g q", q=QUAD)).then_inc(small_in, 16)
                        act.dma_start(base_sb[:, :], base_row).then_inc(small_in, 16)
                        act.dma_start(z_sb[:, :], z_t).then_inc(big_in, 16)
                        act.dma_start(y_sb[:, :], y_t).then_inc(big_in, 16)
                        act.wait_ge(zeroed, 7)
                        for n, (a0, b0, a1, b1, c0, c1) in enumerate(((w_l10, w_sc0, w_l11, w_sc1, w_l20, w_l21),
                                                                      (lin1_w0, si_w0, lin1_w1, si_w1, lin2_w0, lin2_w1))):
                            act.dma_start(ra[n][:, 0:S0], a0).then_inc(w_in, 16)
                            act.dma_start(ra[n][:, S0:2 * S0], b0).then_inc(w_in, 16)
                            for c in range(3):
                                rows = slice(c, 3 * (V1 - 1) + c + 1, 3)
                                act.dma_start(rb[n][rows, c * V1:(c + 1) * V1], a1).then_inc(w_in, 16)
                                act.dma_start(rb[n][rows, (3 + c) * V1:(4 + c) * V1], b1).then_inc(w_in, 16)
                            act.dma_start(u0[n][0:S0 + V1, :], c0).then_inc(w_in, 16)
                            act.dma_start(u1[n][0:S0 + V1, :], c1).then_inc(w_in, 16)
                            act.dma_start(u1[n][S0 + V1:P, :], c1[S0:S0 + V1, :]).then_inc(w_in, 16)
                            for q in range(4):
                                act.dma_start(v1[n][q * V1:(q + 1) * V1, :], c1[S0:S0 + V1, :]).then_inc(w_in, 16)
                        act.dma_start(w12[:, :], w_fc1).then_inc(w_in, 16)
                        act.dma_start(fc2_sb[:, :], w_fc2).then_inc(w_in, 16)
                        act.dma_start(tp_sb[:, :], tp_w).then_inc(w_in, 16)
                        for n in range(2):
                            for h in range(2):
                                act.dma_start(acc[n][h].rearrange("(p t) f -> p t f", p=P),
                                              zero[:, :].unsqueeze(1).broadcast_to([P, ROWS // P, F])).then_inc(acc_zero, 16)
                        for s in range(SPLIT_STEPS + 1):
                            if s < SPLIT_STEPS:
                                b = s % 2
                                act.wait_ge(rad_in[b], 16 * (s // 2 + 1))
                                if s >= 2:
                                    act.wait_ge(rad_out[b], 16 * PARTS * (s // 2))
                                act.activation(rad_p[:, b, 0, :], rad_f[:, b, :], ACT.Copy).then_inc(rad_hi, 1)
                            if s >= 1:
                                b = (s - 1) % 2
                                act.wait_ge(rad_rest, s)
                                act.activation(rad_p[:, b, 1, :], rad_r[:, b, :], ACT.Copy).then_inc(rad_mid, 1)
                            if s == 1:
                                act.wait_ge(big_in, 32)
                                act.activation(meta_sb[:, :, 1:5], y_sb[:, :].rearrange("p (c k) -> p c k", k=4), ACT.Copy).then_inc(y_copied, 1)
                            if s == 3:
                                act.wait_ge(w_split, 3)
                                for wp in range(PARTS):
                                    for xp in range(PARTS):
                                        r0 = (wp * PARTS + xp) * NEF
                                        act.dma_start(fc1_st[r0:r0 + NEF, :], w12p[:, wp, :]).then_inc(fc1_in, 16)
                        act.wait_ge(fc1_in, 16 * PARTS * PARTS)
                        act.wait_ge(acc_zero, 64)
                        act.wait_ge(w_in, 16 * 33)

                    @block.tensor
                    def _(pe):
                        pe.wait_ge(chk, 1)
                        pe.wait_ge(consts, 6)
                        nc.tensor.transpose(tps[0:1, 0:FG], worst[:, :], ident[0:FG, 0:FG]).then_inc(chk_t, 1)

                    @block.vector
                    def _(dve):
                        steps = [0]

                        def link(ins):
                            steps[0] += 1
                            ins.then_inc(d_chain, 1)
                            dve.wait_ge(d_chain, steps[0])

                        dve.memset(zero[:, :], 0.0).then_inc(zeroed, 1)
                        for n in range(2):
                            dve.memset(rb[n][:, :], 0.0).then_inc(zeroed, 1)
                            dve.memset(r1[n][:, :, :], 0.0).then_inc(zeroed, 1)
                            dve.memset(r2[n][:, :], 0.0).then_inc(zeroed, 1)
                        dve.wait_ge(small_in, 96)
                        dve.tensor_copy(b_f[:, :, :], b_i[:, :, :])
                        link(dve.tensor_copy(by_sup_f[:, :, :], by_sup[:, :].rearrange("g (q e) -> g q e", q=QUAD)))
                        dve.tensor_reduce(out=ext[:, 0, :], in_=by_sup_f[:, :, :], op=ALU.min, axis=AX.X)
                        link(dve.tensor_reduce(out=ext[:, 1, :], in_=by_sup_f[:, :, :], op=ALU.max, axis=AX.X))
                        dve.tensor_tensor(ext[:, 2, :], b_f[:, 0, :], ext[:, 0, :], ALU.subtract)
                        dve.scalar_tensor_tensor(out=ext[:, 3, :], in0=ext[:, 1, :], scalar=float(1 - WIN), in1=b_f[:, 0, :], op0=ALU.add, op1=ALU.subtract)
                        link(dve.scalar_tensor_tensor(out=ext[:, 4, :], in0=ext[:, 1, :], scalar=1.0, in1=b_f[:, 1, :], op0=ALU.add, op1=ALU.subtract))
                        dve.tensor_reduce(out=worst[:, :], in_=ext[:, 2:5, :], op=ALU.max, axis=AX.XY).then_inc(chk, 1)
                        dve.tensor_copy(dst_f[:, :], dst_i[:, :])
                        link(dve.tensor_copy(base_f[:, :], base_bc[:, :]))
                        dve.tensor_tensor(meta_sb[:, :, 0].rearrange("p (g c) -> p g c", c=CHUNKS),
                                          dst_f[:, :].rearrange("p (g c) -> p g c", c=CHUNKS),
                                          base_f[:, :].unsqueeze(2).broadcast_to([P, NSUP, CHUNKS]), ALU.subtract).then_inc(meta_done, 1)
                        dve.wait_ge(consts, 6)
                        dve.tensor_copy(win[:, :], win_i[:, :])
                        dve.tensor_copy(g_dead[:, :], g_deadi[:, :])
                        dve.wait_ge(chk_t, 1)
                        link(dve.tensor_reduce(out=worst1[:, :], in_=tps[0:1, 0:FG], op=ALU.max, axis=AX.X))
                        dve.tensor_scalar(flag[:, :], worst1[:, :], 0.0, None, ALU.is_le)
                        dve.wait_ge(w_in, 16 * 33)
                        link(dve.tensor_copy(w12p[:, 0, :], w12[:, :]))
                        link(dve.tensor_tensor(w12r[:, :], w12[:, :], w12p[:, 0, :], ALU.subtract))
                        link(dve.tensor_copy(w12p[:, 1, :], w12r[:, :]))
                        dve.tensor_tensor(w12p[:, 2, :], w12r[:, :], w12p[:, 1, :], ALU.subtract).then_inc(w_split, 3)
                        for n in range(2):
                            skip = C_S if n == 0 else 1.0
                            dve.tensor_scalar_mul(ra[n][:, 0:S0], ra[n][:, 0:S0], S0 ** -0.5)
                            dve.tensor_scalar_mul(ra[n][:, S0:], ra[n][:, S0:], skip * S0 ** -0.5)
                            dve.tensor_scalar_mul(rb[n][:, 0:3 * V1], rb[n][:, 0:3 * V1], V1 ** -0.5)
                            dve.tensor_scalar_mul(rb[n][:, 3 * V1:], rb[n][:, 3 * V1:], skip * V1 ** -0.5)
                            f = (C_X * RN ** -0.5 * 8.0 ** -0.5 if n == 0 else 0.1) * (S0 + V1) ** -0.5
                            fv = f if n == 0 else f * 2.0 ** -0.5
                            o_s = r1[n][:, :, 0:S0]
                            o_v = r1[n][:, :, S0:].rearrange("p k (v c) -> p k v c", c=3)
                            q_v = r2[n][:, S0:].rearrange("p (v c) -> p v c", c=3)
                            sr, vr, cr = slice(0, S0), slice(S0, S0 + V1), slice(S0 + V1, P)
                            dve.tensor_scalar_mul(o_s[sr, 0, :], u0[n][sr, :], f)
                            dve.tensor_scalar_mul(o_v[vr, 0, :, 0], u1[n][vr, :], fv)
                            if n == 0:
                                dve.tensor_scalar_mul(q_v[0:V1, :, 1], v1[n][0:V1, :], fv)
                                dve.tensor_scalar_mul(q_v[V1:2 * V1, :, 2], v1[n][V1:2 * V1, :], fv)
                            else:
                                dve.tensor_scalar_mul(o_v[cr, 0, :, 1], u1[n][cr, :], fv)
                                dve.tensor_scalar_mul(q_v[0:V1, :, 2], v1[n][0:V1, :], fv)
                            for c in range(3):
                                k = c + 1
                                dve.tensor_scalar_mul(o_v[sr, k, :, c], u1[n][sr, :], f)
                                dve.tensor_scalar_mul(o_s[vr, k, :], u0[n][vr, :], f * 3.0 ** -0.5)
                                if n == 1:
                                    for part, m in enumerate(other_two(c)):
                                        to = 3 - c - m
                                        g = 0.5 * f * (1.0 if (c - m) % 3 == 1 else -1.0)
                                        if part == 0:
                                            dve.tensor_scalar_mul(o_v[cr, k, :, to], u1[n][cr, :], g)
                                        else:
                                            rr = slice(k * V1, (k + 1) * V1)
                                            dve.tensor_scalar_mul(q_v[rr, :, to], v1[n][rr, :], g)

        def node_phase(n):
            stat = sem(f"stat{n}")
            acc_in = [sem(f"acc_in{n}{b}") for b in range(2)]
            var_eps = sem(f"var_eps{n}")
            std_done = sem(f"std_done{n}")
            moments = sem(f"moments{n}")
            norm_done = sem(f"norm_done{n}")
            t_ps = sem(f"t_ps{n}")
            hT_done = sem(f"hT_done{n}")
            o_ps = sem(f"o_ps{n}")
            row_done = sem(f"row_done{n}")
            skip_done = sem(f"skip_done{n}")
            rows_out = [sem(f"rows_out{n}{b}") for b in range(2)]

            with nc.Block() as block:
                @block.sync
                def _(sp):
                    if n == 1:
                        def load(i):
                            for b in range(2):
                                t = 2 * i + b
                                src = acc[0][:, bass.ds(t * P, P), :].rearrange("h p f -> p h f")
                                wait_for(sp, stat, 4 * (i - 1) + b + 1)
                                sp.dma_start(accin[:, b, :, :], src).then_inc(acc_in[b], 16)
                        rolled(sp, NT // 2, load)

                    def store(i):
                        for b in range(2):
                            t = 2 * i + b
                            sp.wait_ge(row_done, t + 1)
                            sp.dma_start(table[n][bass.ds(t * P, P), :], rows2[:, b, :]).then_inc(rows_out[b], 16)
                    rolled(sp, NT // 2, store)
                    for b in range(2):
                        sp.wait_ge(rows_out[b], 8 * NT)

                @block.vector
                def _(dve):
                    def add_sums(i):
                        for b in range(2):
                            dve.wait_ge(acc_in[b], 16 * i + 16)
                            wait_for(dve, stat, 4 * i - 1 + b)
                            dve.tensor_tensor(hn[:, b, :], accin[:, b, 0, :], accin[:, b, 1, :], ALU.add).then_inc(stat, 1)
                        for b in range(2):
                            t = 2 * i + b
                            dve.wait_ge(stat, 4 * i + 1 + b)
                            dve.scalar_tensor_tensor(out=x_tile(t), in0=hn[:, b, :], scalar=z_sb[:, bass.ds(t, 1)], in1=x_tile(t), op0=ALU.mult, op1=ALU.add).then_inc(stat, 1)

                    def statistics(i):
                        for b in range(2):
                            t = 2 * i + b
                            dve.bn_stats(stats[:, bass.ds(t * 6, 6)], x_tile(t))

                    if n == 0:
                        with dve.Fori(0, NT // 2) as i:
                            statistics(i)
                    else:
                        add_sums(0)
                        with dve.Fori(1, NT // 2) as i:
                            add_sums(i)
                            statistics(i - 1)
                        dve.wait_ge(stat, 2 * NT)
                        statistics(NT // 2 - 1)
                    chain = [0]

                    def link(ins):
                        chain[0] += 1
                        ins.then_inc(moments, 1)
                        dve.wait_ge(moments, chain[0])

                    st = stats[:, :].rearrange("p (t s) -> p t s", s=6)
                    dve.engine_nop().then_inc(moments, 1)
                    chain[0] += 1
                    dve.wait_ge(moments, 1)
                    dve.tensor_tensor(mean[:, :], st[:, :, 1], st[:, :, 4], ALU.add)
                    dve.tensor_tensor(shift[:, :], st[:, :, 1], st[:, :, 4], ALU.subtract)
                    link(dve.tensor_tensor(rstd[:, :], st[:, :, 2], st[:, :, 5], ALU.add))
                    dve.tensor_scalar(rstd[:, :], rstd[:, :], 1.0 / F, EPS, ALU.mult, ALU.add)
                    link(dve.scalar_tensor_tensor(out=shift[:, :], in0=shift[:, :], scalar=0.25, in1=shift[:, :], op0=ALU.mult, op1=ALU.mult))
                    dve.tensor_tensor(rstd[:, :], rstd[:, :], shift[:, :], ALU.add).then_inc(var_eps, 1)
                    dve.wait_ge(std_done, 1)
                    link(dve.reciprocal(rstd[:, :], rstd[:, :]))
                    link(dve.scalar_tensor_tensor(out=shift[:, :], in0=mean[:, :], scalar=-0.5, in1=rstd[:, :], op0=ALU.mult, op1=ALU.mult))

                    def norm(t, b):
                        wait_for(dve, t_ps, t - 1)
                        dve.tensor_scalar(hn[:, b, :], x_tile(t), rstd[:, bass.ds(t, 1)], shift[:, bass.ds(t, 1)], ALU.mult, ALU.add).then_inc(norm_done, 1)

                    def add_skip(t, b):
                        dve.wait_ge(o_ps, t + 1)
                        dve.wait_ge(norm_done, t + 1)
                        o = wps[b][:, :, :].rearrange("p a c -> p (a c)")
                        x_s, x_v = X[:, bass.ds(t * F, S0)], X[:, bass.ds(t * F + S0, 3 * V1)].rearrange("p (v c) -> p v c", c=3)
                        k_s, k_v = o[:, F:F + S0], o[:, F + S0:2 * F].rearrange("p (c v) -> p v c", c=3)
                        if n == 0:
                            zc = z_sb[:, bass.ds(t, 1)]
                            dve.scalar_tensor_tensor(out=x_s, in0=k_s, scalar=zc, in1=x_s, op0=ALU.mult, op1=ALU.add)
                            dve.scalar_tensor_tensor(out=x_v, in0=k_v, scalar=zc, in1=x_v, op0=ALU.mult, op1=ALU.add).then_inc(skip_done, 1)
                        else:
                            dve.tensor_tensor(x_s, k_s, x_s, ALU.add)
                            dve.tensor_tensor(x_v, k_v, x_v, ALU.add).then_inc(skip_done, 1)

                    norm(0, 0)

                    def tiles(i):
                        for b in range(2):
                            t = 2 * i + b
                            if within(t + 1, 0, NT):
                                norm(t + 1, 1 - b)
                            add_skip(t, b)
                    rolled(dve, NT // 2, tiles)

                @block.tensor
                def _(pe):
                    def transposes(t, b):
                        pe.wait_ge(norm_done, t + 1)
                        wait_for(pe, hT_done, t - 1)
                        nc.tensor.transpose(aps[b][0:3 * V1, P:2 * P], hn[:, b, S0:F], ident[:, :])
                        nc.tensor.transpose(aps[b][0:S0, 0:P], hn[:, b, 0:S0], ident[:, :]).then_inc(t_ps, 1)

                    def project(t, b):
                        pe.wait_ge(hT_done, t + 1)
                        wait_for(pe, row_done, t - 1)
                        wait_for(pe, skip_done, t - 1)
                        o = wps[b][:, :, :].rearrange("p a c -> p (a c)")[:, 0:2 * F].rearrange("p (h f) -> p h f", h=2)
                        nc.tensor.matmul(o[:, :, 0:S0], hT[0:S0, b, 0, :], ra[n][:, :].rearrange("p (h f) -> p h f", h=2), start=True, stop=True)
                        nc.tensor.matmul(o[:, :, S0:F], hT[0:3 * V1, b, 1, :], rb[n][:, :].rearrange("p (h f) -> p h f", h=2), start=True, stop=True).then_inc(o_ps, 1)

                    transposes(0, 0)

                    def tiles(i):
                        for b in range(2):
                            t = 2 * i + b
                            if within(t + 1, 0, NT):
                                transposes(t + 1, 1 - b)
                            project(t, b)
                    rolled(pe, NT // 2, tiles)

                @block.scalar
                def _(act):
                    act.wait_ge(var_eps, 1)
                    act.activation(rstd[:, :], rstd[:, :], ACT.Sqrt).then_inc(std_done, 1)

                    def relu(t, b):
                        act.wait_ge(t_ps, t + 1)
                        wait_for(act, o_ps, t - 1)
                        act.activation(hT[0:S0, b, 0, :], aps[b][0:S0, 0:P], ACT.Relu)
                        act.activation(hT[0:3 * V1, b, 1, :], aps[b][0:3 * V1, P:2 * P], ACT.Relu).then_inc(hT_done, 1)

                    def table_row(i, t, b):
                        act.wait_ge(skip_done, t + 1)
                        wait_for(act, rows_out[b], 16 * i)
                        o = wps[b][:, :, :].rearrange("p a c -> p (a c)")[:, 0:F]
                        if n == 0:
                            act.activation(rows2[:, b, :], o, ACT.Copy, scale=z_sb[:, bass.ds(t, 1)]).then_inc(row_done, 1)
                        else:
                            act.activation(rows2[:, b, :], o, ACT.Copy).then_inc(row_done, 1)

                    relu(0, 0)

                    def tiles(i):
                        for b in range(2):
                            t = 2 * i + b
                            if within(t + 1, 0, NT):
                                relu(t + 1, 1 - b)
                            table_row(i, t, b)
                    rolled(act, NT // 2, tiles)

        def edge_phase(L):
            n = L.n
            idx_in = [sem(f"idx_in{n}{j}") for j in range(QUAD)]
            edge_in = [sem(f"edge_in{n}{j}") for j in range(QUAD)]
            gathered = [sem(f"gathered{n}{j}") for j in range(QUAD)]
            hid_ps, hid_done = sem(f"hid_ps{n}"), sem(f"hid_done{n}")
            w_ps = sem(f"w_ps{n}")
            eq_done, S_done, P_done = sem(f"eq_done{n}"), sem(f"S_done{n}"), sem(f"P_done{n}")
            agg_ps, agg_done = sem(f"agg_ps{n}"), sem(f"agg_done{n}")
            tr_ps, tr_done = sem(f"tr_ps{n}"), sem(f"tr_done{n}")
            sum_ps, sum_done = sem(f"sum_ps{n}"), sem(f"sum_done{n}")
            sum_out = [sem(f"sum_out{n}{j}") for j in range(QUAD)]
            c_in, c_gathered, c_added = sem(f"c_in{n}"), sem(f"c_gathered{n}"), sem(f"c_added{n}")
            c_hid_ps, c_hid, c_w = sem(f"c_hid_ps{n}"), sem(f"c_hid{n}"), sem(f"c_w{n}")
            c_dve, c_ready = sem(f"c_dve{n}"), sem(f"c_ready{n}")
            c_agg_ps, c_agg, c_tr_ps, c_tr = sem(f"c_agg_ps{n}"), sem(f"c_agg{n}"), sem(f"c_tr_ps{n}"), sem(f"c_tr{n}")
            c_sum_ps, c_sum = sem(f"c_sum_ps{n}"), sem(f"c_sum{n}")

            def is_windowed(eng):
                return eng.value_load(flag[0:1, 0:1], min_val=0, max_val=1) == 1

            def radial_matmul(pe, out_ap, lhs_slot, e0, w):
                return nc.tensor.matmul(out_ap, fc1_st[:, :], rad[:, lhs_slot, e0:e0 + w], start=True, stop=True)

            def weight_matmul(out_ap, par, slot, c):
                if n == 0:
                    return nc.tensor.matmul(out_ap, hid[:, par, c * P:(c + 1) * P], fc2_sb[:, :], start=True, stop=True)
                return nc.tensor.matmul(out_ap, query[:, slot, c * P:(c + 1) * P], tp_sb[:, :], start=True, stop=True)

            def products(dve, out_p, w, g, m):
                h1 = g[:, :, S0:F].rearrange("p c (d v) -> p c d v", d=3)

                def vec(col, w_col):
                    return dve.tensor_tensor(out_p[:, :, col:col + 3 * V1].rearrange("p c (d v) -> p c d v", d=3),
                                             w[:, :, w_col:w_col + V1].unsqueeze(2).broadcast_to([P, m, 3, V1]), h1, ALU.mult)
                dve.tensor_tensor(out_p[:, :, 0:2 * F].rearrange("p c (h f) -> p c h f", h=2)[:, :, :, 0:S0],
                                  w[:, :, 0:2 * S0].rearrange("p c (h f) -> p c h f", h=2),
                                  g[:, :, 0:S0].unsqueeze(2).broadcast_to([P, m, 2, S0]), ALU.mult)
                vec(S0, 2 * S0)
                if n == 1:
                    vec(2 * F, 2 * S0 + V1)
                return vec(F + S0, L.d_col)

            def aggregate_matmul(out_ap, s_ap, p_ap, k, start, stop, tile):
                cols = slice(0, F) if k == 0 else slice(F, L.pcols)
                return nc.tensor.matmul(out_ap, s_ap, p_ap[:, cols], start=start, stop=stop, tile_position=tile)

            def pack_component(act, dst, src, k, rows):
                c = k - 1
                last = act.activation(dst[rows, S0:S0 + V1], src[rows, S0 + c * V1:S0 + (c + 1) * V1], ACT.Copy)
                if n == 1:
                    m0, m1 = other_two(c)
                    b0 = S0 + 3 * V1
                    pair = src[rows, b0:b0 + 3 * V1].rearrange("p (m v) -> p m v", m=3)[:, m0:m1 + 1:m1 - m0, :]
                    last = act.activation(dst[rows, S0 + V1:F].rearrange("p (m v) -> p m v", m=2), pair, ACT.Copy)
                return last

            def sums_ps():
                return tps[:, 2 * P:2 * P + F]

            def output_matmuls():
                for k in range(4):
                    nc.tensor.matmul(sums_ps(), T1[0:L.k1, k, :, :].rearrange("p q w -> p (q w)"), r1[n][0:L.k1, k, :], start=(k == 0), stop=False)
                return nc.tensor.matmul(sums_ps(), T2[0:L.k2, :, :].rearrange("p q w -> p (q w)"), r2[n][0:L.k2, :], start=False, stop=True)

            with nc.Block() as block:
                @block.sync
                def _(sp):
                    def load_idx(i, j):
                        g = QUAD * i + j
                        wait_for(sp, gathered[j], 16 * CHUNKS * i)
                        sp.dma_start(idx[:, j, :], src_t[:, bass.ds(g * CHUNKS, CHUNKS)]).then_inc(idx_in[j], 16)

                    def load_edges(i, j):
                        g = QUAD * i + j
                        e0 = bass.ds(g * SUP, SUP)
                        wait_for(sp, P_done, g - QUAD + 1)
                        sp.dma_start(meta[:, j, :, :], meta_d[:, bass.ds(g * CHUNKS, CHUNKS), :]).then_inc(edge_in[j], 16)
                        if n == 0:
                            for a in range(PARTS):
                                r0 = a * PARTS * NEF
                                sp.dma_start(rad[r0:r0 + PARTS * NEF, j, :], split_d[:, e0]).then_inc(edge_in[j], 16)
                        else:
                            sp.dma_start(query[:, j, :], query_t[:, e0]).then_inc(edge_in[j], 16)

                    def store_sums(i, j):
                        before = 2 * (j // 2) + j % 2 - 2 if j >= 2 else j + 2
                        start = sp.value_load(base_sb[0:1, bass.ds(QUAD * i + j, 1)], min_val=0, max_val=NPAD - WIN)
                        to = acc[n][j % 2, bass.ds(start, WIN), :]
                        waits_alone(sp, sum_done, i + 1, 1)
                        waits_alone(sp, sum_out[before], 16 * (i + 1) if j >= 2 else 16 * i, 16)
                        sp.dma_start(to, sums[j * WIN:(j + 1) * WIN, :]).then_inc(sum_out[j], 16)

                    def quad(i):
                        for j in range(QUAD):
                            if j < QUAD - 1:
                                load_idx(i, j + 1)
                            elif within(i + 1, 0, NQUAD):
                                load_idx(i + 1, 0)
                            load_edges(i, j)
                            if j >= 2 and within(i - 2, 0, NQUAD):
                                store_sums(i - 2, 2 * (j - 2))
                                store_sums(i - 2, 2 * (j - 2) + 1)

                    def drain():
                        for i in (NQUAD - 2, NQUAD - 1):
                            for j in range(QUAD):
                                store_sums(i, j)
                        for j in range(QUAD):
                            sp.wait_ge(sum_out[j], 16 * NQUAD)

                    def chunk(m):
                        waits_alone(sp, c_added, 16 * m, 16)
                        e0 = bass.ds(m * P, P)
                        sp.dma_start(idx[:, 0, 0:1], src_t[:, bass.ds(m, 1)]).then_inc(c_in, 16)
                        sp.dma_start(g_dst[:, :], dst_t[:, bass.ds(m, 1)]).then_inc(c_in, 16)
                        sp.dma_start(g_row[:, :], dst_flat[e0].partition_broadcast(P)).then_inc(c_in, 16)
                        sp.dma_start(g_y[:, :], y_t[:, bass.ds(4 * m, 4)]).then_inc(c_in, 16)
                        if n == 0:
                            for a in range(PARTS):
                                r0 = a * PARTS * NEF
                                sp.dma_start(rad[r0:r0 + PARTS * NEF, 0, 0:P], split_d[:, e0]).then_inc(c_in, 16)
                        else:
                            sp.dma_start(query[:, 0, 0:P], query_t[:, e0]).then_inc(c_in, 16)

                    with sp.If(is_windowed(sp)):
                        load_idx(0, 0)
                        quad(0)
                        quad(1)
                        quad(2)
                        with sp.Fori(3, NQUAD - 1) as i:
                            quad(i)
                        quad(NQUAD - 1)
                        drain()
                    with sp.Else():
                        chunk(0)
                        with sp.Fori(1, NCH) as m:
                            chunk(m)
                        sp.wait_ge(c_added, 16 * NCH)

                loads_per_chunk = 16 * (7 if n == 0 else 5)
                edge_loads = 16 * (1 + PARTS if n == 0 else 2)

                @block.gpsimd
                def _(pool):
                    def gather(i, j):
                        g = QUAD * i + j
                        waits_alone(pool, idx_in[j], 16 * (i + 1), 16, (P_done, g - QUAD + 1))
                        for c in range(CHUNKS):
                            pool.indirect_dma_start(out=G[:, j, c, :], out_offset=None, in_=table[n][:, :],
                                                    in_offset=bass.IndirectOffsetOnAxis(ap=idx[:, j, c:c + 1], axis=0)).then_inc(gathered[j], 16)

                    def quad(i):
                        for j in range(QUAD):
                            gather(i, j)

                    def chunk(m):
                        waits_alone(pool, c_in, loads_per_chunk * (m + 1), loads_per_chunk)
                        pool.indirect_dma_start(out=G[:, 0, 0, :], out_offset=None, in_=table[n][:, :],
                                                in_offset=bass.IndirectOffsetOnAxis(ap=idx[:, 0, 0:1], axis=0)).then_inc(c_gathered, 16)
                        waits_alone(pool, c_ready, m + 1, 1)
                        pool.wait_ge(c_sum, m + 1)
                        pool.indirect_dma_start(out=acc[n][0], out_offset=bass.IndirectOffsetOnAxis(ap=g_to[:, 0:1], axis=0),
                                                in_=sums[:, :], in_offset=None, compute_op=ALU.add).then_inc(c_added, 16)

                    with pool.If(is_windowed(pool)):
                        rolled(pool, NQUAD, quad)
                    with pool.Else():
                        with pool.Fori(0, NCH) as m:
                            chunk(m)

                @block.tensor
                def _(pe):
                    def hidden(i, j):
                        g = QUAD * i + j
                        pe.wait_ge(edge_in[j], edge_loads * (i + 1))
                        wait_for(pe, hid_done, g)
                        radial_matmul(pe, hps[0:RN, 0:SUP], j, 0, SUP).then_inc(hid_ps, 1)

                    def radial_weights(i, j):
                        g = QUAD * i + j
                        if n == 0:
                            pe.wait_ge(hid_done, g + 1)
                        else:
                            pe.wait_ge(edge_in[j], edge_loads * (i + 1))
                        wait_for(pe, P_done, g - 1)
                        for c in range(CHUNKS):
                            last = weight_matmul(wps[j % 2][:, c, 0:L.wcols], j % 2, j, c)
                        last.then_inc(w_ps, 1)

                    def aggregate(i, j):
                        g = QUAD * i + j
                        b = j % 2
                        pe.wait_ge(S_done, g + 1)
                        pe.wait_ge(P_done, g + 1)
                        wait_for(pe, agg_done, g - 1)
                        for c in range(CHUNKS):
                            for k in range(4):
                                width = F if k == 0 else L.agg
                                last = aggregate_matmul(aps[b][k * WIN:(k + 1) * WIN, 0:width], S[:, b, c, k, :], Pr[:, b, c, :],
                                                        k, c == 0, c == CHUNKS - 1, (0, k * WIN))
                        last.then_inc(agg_ps, 1)

                    def transposes(g, b, quads_out=None):
                        pe.wait_ge(agg_done, g + 1)
                        if quads_out is not None:
                            wait_for(pe, sum_done, quads_out)
                        wait_for(pe, tr_done, g)
                        nc.tensor.transpose(tps[0:L.k1, 0:P], agg_sb[:, b, 0:L.k1], ident[:, :])
                        if n == 0:
                            last = nc.tensor.transpose(tps[0:2 * V1, P:P + WIN], agg_sb[0:WIN, b, L.k1:F], ident[0:WIN, 0:WIN])
                        else:
                            last = nc.tensor.transpose(tps[0:V1, P:2 * P], agg_sb[:, b, L.k1:F], ident[:, :])
                        last.then_inc(tr_ps, 1)

                    def output(i):
                        pe.wait_ge(tr_done, QUAD * (i + 1))
                        wait_for(pe, sum_done, i)
                        output_matmuls().then_inc(sum_ps, 1)

                    def quad(i):
                        for j in range(QUAD):
                            g = QUAD * i + j
                            if n == 0 and within(g + 2, 0, NSUP):
                                hidden(i + (j + 2) // QUAD, (j + 2) % QUAD)
                            if within(g + 1, 0, NSUP):
                                radial_weights(i + (j + 1) // QUAD, (j + 1) % QUAD)
                            aggregate(i, j)
                            if j == 1 and within(i - 1, 0, NQUAD):
                                output(i - 1)
                            if within(g - 1, 0, NSUP):
                                transposes(g - 1, (j - 1) % 2, i if j == 1 else None)

                    def chunk(m):
                        pe.wait_ge(c_in, loads_per_chunk * (m + 1))
                        if n == 0:
                            radial_matmul(pe, hps[0:RN, 0:P], 0, 0, P).then_inc(c_hid_ps, 1)
                            pe.wait_ge(c_hid, m + 1)
                        weight_matmul(wps[0][:, 0, 0:L.wcols], 0, 0, 0).then_inc(c_w, 1)
                        pe.wait_ge(c_ready, m + 1)
                        for k in range(4):
                            width = F if k == 0 else L.agg
                            last = aggregate_matmul(aps[k // 2][:, 256 * (k % 2):256 * (k % 2) + width], g_S[:, k, :], Pr[:, 0, 0, :], k, True, True, None)
                        last.then_inc(c_agg_ps, 1)
                        pe.wait_ge(c_agg, m + 1)
                        for k in range(4):
                            last = nc.tensor.transpose(wps[1][0:L.k1, k // 2, P * (k % 2):P * (k % 2) + P], g_agg[:, k, 0:L.k1], ident[:, :])
                        if n == 0:
                            last = nc.tensor.transpose(wps[1][0:2 * V1, 2, 0:P], g_agg[:, 0, L.k1:F], ident[:, :])
                        else:
                            for k in range(4):
                                last = nc.tensor.transpose(wps[1][0:V1, 2 + k // 2, P * (k % 2):P * (k % 2) + P], g_agg[:, k, L.k1:F], ident[:, :])
                        last.then_inc(c_tr_ps, 1)
                        pe.wait_ge(c_tr, m + 1)
                        output_matmuls().then_inc(c_sum_ps, 1)

                    with pe.If(is_windowed(pe)):
                        if n == 0:
                            hidden(0, 0)
                            hidden(0, 1)
                        radial_weights(0, 0)
                        rolled(pe, NQUAD, quad)
                        transposes(NSUP - 1, (NSUP - 1) % 2)
                        output(NQUAD - 1)
                    with pe.Else():
                        with pe.Fori(0, NCH) as m:
                            chunk(m)

                @block.scalar
                def _(act):
                    def silu(g, b):
                        act.wait_ge(hid_ps, g + 1)
                        wait_for(act, w_ps, g - 1)
                        act.activation(hid[:, b, :], hps[0:RN, 0:SUP], ACT.Silu, scale=NEF ** -0.5).then_inc(hid_done, 1)

                    def pack(g, b):
                        act.wait_ge(agg_ps, g + 1)
                        wait_for(act, tr_ps, g - 1)
                        act.activation(agg_sb[:, b, 0:S0], aps[b][:, 0:S0], ACT.Copy)
                        act.activation(agg_sb[0:WIN, b, S0:F], aps[b][0:WIN, S0:F], ACT.Copy)
                        for k in range(1, 4):
                            last = pack_component(act, agg_sb[:, b, :], aps[b], k, slice(k * WIN, (k + 1) * WIN))
                        last.then_inc(agg_done, 1)

                    def transposed(i, j):
                        g = QUAD * i + j
                        act.wait_ge(tr_ps, g + 1)
                        if j == 0:
                            wait_for(act, sum_ps, i)
                        last = act.activation(T1[0:L.k1, :, j, :], tps[0:L.k1, 0:P].rearrange("p (k w) -> p k w", k=4), ACT.Copy)
                        if n == 0:
                            last = act.activation(T2[0:2 * V1, j, :], tps[0:2 * V1, P:P + WIN], ACT.Copy)
                        else:
                            for k in range(4):
                                last = act.activation(T2[k * V1:(k + 1) * V1, j, :], tps[0:V1, P + k * WIN:P + (k + 1) * WIN], ACT.Copy)
                        last.then_inc(tr_done, 1)

                    def window_sums(i):
                        act.wait_ge(sum_ps, i + 1)
                        for j in range(QUAD):
                            wait_for(act, sum_out[j], 16 * i)
                        act.activation(sums[:, :], sums_ps(), ACT.Copy).then_inc(sum_done, 1)

                    def quad(i):
                        for j in range(QUAD):
                            g = QUAD * i + j
                            if n == 0 and within(g + 2, 0, NSUP):
                                silu(g + 2, j % 2)
                            pack(g, j % 2)
                            if j == 1 and within(i - 1, 0, NQUAD):
                                window_sums(i - 1)
                            if within(g - 1, 0, NSUP):
                                transposed(i - 1 if j == 0 else i, (j - 1) % QUAD)

                    def chunk(m):
                        if n == 0:
                            act.wait_ge(c_hid_ps, m + 1)
                            act.activation(hid[:, 0, 0:P], hps[0:RN, 0:P], ACT.Silu, scale=NEF ** -0.5).then_inc(c_hid, 1)
                        act.wait_ge(c_agg_ps, m + 1)
                        every = slice(0, P)
                        act.activation(g_agg[:, 0, :], aps[0][:, 0:F], ACT.Copy)
                        for k in range(1, 4):
                            at = aps[k // 2][:, 256 * (k % 2):256 * (k % 2) + 256]
                            act.activation(g_agg[:, k, 0:S0], at[:, 0:S0], ACT.Copy)
                            last = pack_component(act, g_agg[:, k, :], at, k, every)
                        last.then_inc(c_agg, 1)
                        act.wait_ge(c_tr_ps, m + 1)
                        for k in range(4):
                            last = act.activation(T1[0:L.k1, k, :, :].rearrange("p q w -> p (q w)"), wps[1][0:L.k1, k // 2, P * (k % 2):P * (k % 2) + P], ACT.Copy)
                        if n == 0:
                            last = act.activation(T2[0:2 * V1, :, :].rearrange("p q w -> p (q w)"), wps[1][0:2 * V1, 2, 0:P], ACT.Copy)
                        else:
                            for k in range(4):
                                last = act.activation(T2[k * V1:(k + 1) * V1, :, :].rearrange("p q w -> p (q w)"),
                                                      wps[1][0:V1, 2 + k // 2, P * (k % 2):P * (k % 2) + P], ACT.Copy)
                        last.then_inc(c_tr, 1)
                        act.wait_ge(c_sum_ps, m + 1)
                        act.activation(sums[:, :], sums_ps(), ACT.Copy).then_inc(c_sum, 1)

                    with act.If(is_windowed(act)):
                        if n == 0:
                            silu(0, 0)
                            silu(1, 1)
                        rolled(act, NQUAD, quad)
                        transposed(NQUAD - 1, QUAD - 1)
                        window_sums(NQUAD - 1)
                    with act.Else():
                        with act.Fori(0, NCH) as m:
                            chunk(m)

                @block.vector
                def _(dve):
                    def select(i, j):
                        g = QUAD * i + j
                        dve.wait_ge(edge_in[j], edge_loads * (i + 1))
                        wait_for(dve, S_done, g - 1)
                        dve.tensor_tensor(eq[:, j % 2, :, :], win[:, :].unsqueeze(1).broadcast_to([P, CHUNKS, WIN]),
                                          meta[:, j, :, 0:1].broadcast_to([P, CHUNKS, WIN]), ALU.is_equal).then_inc(eq_done, 1)

                    def scale(g, j):
                        dve.wait_ge(eq_done, g + 1)
                        wait_for(dve, agg_ps, g - 1)
                        shape = [P, CHUNKS, 4, WIN]
                        dve.tensor_tensor(S[:, j % 2, :, :, :], eq[:, j % 2, :, :].unsqueeze(2).broadcast_to(shape),
                                          meta[:, j, :, 1:5].unsqueeze(3).broadcast_to(shape), ALU.mult).then_inc(S_done, 1)

                    def multiply(i, j):
                        g = QUAD * i + j
                        dve.wait_ge(w_ps, g + 1)
                        dve.wait_ge(gathered[j], 16 * CHUNKS * (i + 1))
                        wait_for(dve, agg_ps, g - 1)
                        products(dve, Pr[:, j % 2, :, :], wps[j % 2][:, 0:CHUNKS, :], G[:, j, :, :], CHUNKS).then_inc(P_done, 1)

                    def quad(i):
                        for j in range(QUAD):
                            g = QUAD * i + j
                            more = within(g + 1, 0, NSUP)
                            if more:
                                select(i + (j + 1) // QUAD, (j + 1) % QUAD)
                            multiply(i, j)
                            if more:
                                scale(g + 1, (j + 1) % QUAD)

                    DUP_OPS = 8

                    def chunk(m):
                        s = [0]

                        def link(ins):
                            s[0] += 1
                            ins.then_inc(c_dve, 1)
                            dve.wait_ge(c_dve, DUP_OPS * m + s[0])
                        dve.wait_ge(c_in, loads_per_chunk * (m + 1))
                        link(dve.tensor_copy(g_dstf[:, :], g_dst[:, :]))
                        link(dve.tensor_copy(g_rowf[:, :], g_row[:, :]))
                        link(dve.tensor_scalar(g_eq[:, :], g_rowf[:, :], g_dstf[:, 0:1], None, ALU.is_equal))
                        shape = [P, 4, P]
                        dve.tensor_tensor(g_S[:, :, :], g_eq[:, :].unsqueeze(1).broadcast_to(shape), g_y[:, :].unsqueeze(2).broadcast_to(shape), ALU.mult)
                        link(dve.tensor_tensor(g_tmp[:, :], g_eq[:, :], g_low[:, :], ALU.mult))
                        link(dve.tensor_reduce(out=g_dup[:, 0:1], in_=g_tmp[:, :], op=ALU.max, axis=AX.X))
                        link(dve.tensor_tensor(g_dup[:, 1:2], g_dead[:, :], g_dstf[:, :], ALU.subtract))
                        link(dve.scalar_tensor_tensor(out=g_dup[:, 1:2], in0=g_dup[:, 1:2], scalar=g_dup[:, 0:1], in1=g_dstf[:, :], op0=ALU.mult, op1=ALU.add))
                        link(dve.tensor_copy(g_to[:, :], g_dup[:, 1:2]))
                        assert s[0] == DUP_OPS
                        dve.wait_ge(c_w, m + 1)
                        dve.wait_ge(c_gathered, 16 * (m + 1))
                        products(dve, Pr[:, 0, 0:1, :], wps[0][:, 0:1, :], G[:, 0, 0:1, :], 1).then_inc(c_ready, 1)

                    with dve.If(is_windowed(dve)):
                        select(0, 0)
                        scale(0, 0)
                        rolled(dve, NQUAD, quad)
                    with dve.Else():
                        with dve.Fori(0, NCH) as m:
                            chunk(m)

        def output_phase():
            acc_in = [sem(f"out_in{b}") for b in range(2)]
            added = sem("added")
            out_done = [sem(f"out_done{b}") for b in range(2)]
            with nc.Block() as block:
                @block.sync
                def _(sp):
                    def load(i):
                        for b in range(2):
                            t = 2 * i + b
                            src = acc[1][:, bass.ds(t * P, P), :].rearrange("h p f -> p h f")
                            wait_for(sp, added, 4 * (i - 1) + 2)
                            sp.dma_start(accin[:, b, :, :], src).then_inc(acc_in[b], 16)
                    rolled(sp, NT // 2, load)

                @block.scalar
                def _(act):
                    def store(i):
                        for b in range(2):
                            t = 2 * i + b
                            to = out[bass.ds(t * P, P), :]
                            act.wait_ge(added, 4 * i + 3 + b)
                            act.dma_start(to, rows2[:, b, :]).then_inc(out_done[b], 16)
                    rolled(act, NT // 2, store)
                    for b in range(2):
                        act.wait_ge(out_done[b], 8 * NT)

                @block.vector
                def _(dve):
                    def tiles(i):
                        for b in range(2):
                            dve.wait_ge(acc_in[b], 16 * (i + 1))
                            wait_for(dve, added, 4 * (i - 1) + 3 + b)
                            dve.tensor_tensor(hn[:, b, :], accin[:, b, 0, :], accin[:, b, 1, :], ALU.add).then_inc(added, 1)
                        for b in range(2):
                            dve.wait_ge(added, 4 * i + 1 + b)
                            wait_for(dve, out_done[b], 16 * i)
                            dve.tensor_tensor(rows2[:, b, :], hn[:, b, :], x_tile(2 * i + b), ALU.add).then_inc(added, 1)
                    rolled(dve, NT // 2, tiles)

        setup()
        node_phase(0)
        edge_phase(L0)
        node_phase(1)
        edge_phase(L1)
        output_phase()


def kernel(x, src, dst, edge_attr_12, edge_attr_4, edge_attr_64, node_vec1,
           L0_gnn_W_sc0, L0_gnn_W_sc1, L0_gnn_W_l1_0, L0_gnn_W_l1_1, L0_gnn_W_fc1, L0_gnn_W_fc2, L0_gnn_W_l2_0, L0_gnn_W_l2_1,
           L1_gnn_si_w0, L1_gnn_si_w1, L1_gnn_lin1_w0, L1_gnn_lin1_w1, L1_gnn_tp_weight, L1_gnn_lin2_w0, L1_gnn_lin2_w1):
    import concourse.bacc as bacc
    from concourse.bass_utils import run_bass_kernel_spmd

    def pad(a, rows, mode="constant"):
        a = np.asarray(a)
        return np.pad(a, [(0, rows - a.shape[0])] + [(0, 0)] * (a.ndim - 1), mode=mode)

    def by_chunk(a):
        a = a.reshape((NCH, P) + a.shape[1:])
        return np.ascontiguousarray(np.moveaxis(a, 0, 1).reshape(P, -1))

    dst_pad = pad(dst, EPAD, "edge")
    dst_pad[FIRST_EMPTY * SUP:] = np.repeat(np.arange(N, N + NSUP - FIRST_EMPTY, dtype=dst_pad.dtype), SUP)
    base = np.concatenate([dst_pad[::SUP], np.full(2, NPAD - 1, dst_pad.dtype)]).reshape(1, -1)
    arrays = {
        "x": pad(x, NPAD),
        "z_t": np.ascontiguousarray(pad(node_vec1, NPAD).reshape(NT, P).T),
        "src_t": by_chunk(pad(src, EPAD)),
        "dst_t": by_chunk(dst_pad),
        "dst_flat": dst_pad,
        "base_row": base,
        "y_t": by_chunk(pad(edge_attr_4, EPAD)),
        "rad_t": np.ascontiguousarray(pad(edge_attr_12, EPAD).T),
        "query_t": np.ascontiguousarray(pad(edge_attr_64, EPAD).T),
        "w_sc0": L0_gnn_W_sc0, "w_sc1": L0_gnn_W_sc1, "w_l10": L0_gnn_W_l1_0, "w_l11": L0_gnn_W_l1_1,
        "w_fc1": L0_gnn_W_fc1, "w_fc2": L0_gnn_W_fc2, "w_l20": L0_gnn_W_l2_0, "w_l21": L0_gnn_W_l2_1,
        "si_w0": L1_gnn_si_w0, "si_w1": L1_gnn_si_w1, "lin1_w0": L1_gnn_lin1_w0, "lin1_w1": L1_gnn_lin1_w1,
        "tp_w": L1_gnn_tp_weight, "lin2_w0": L1_gnn_lin2_w0, "lin2_w1": L1_gnn_lin2_w1,
    }
    arrays = {k: np.ascontiguousarray(v) for k, v in arrays.items()}
    nc = bacc.Bacc("TRN2", target_bir_lowering=False, num_devices=1)
    aps = {k: nc.dram_tensor(k, v.shape, mybir.dt.from_np(v.dtype), kind="ExternalInput").ap() for k, v in arrays.items()}
    out = nc.dram_tensor("out", (NPAD, F), F32, kind="ExternalOutput").ap()
    gnn_kernel(nc, out=out, **aps)
    r = run_bass_kernel_spmd(nc, [arrays], core_ids=[0])
    return r.results[0]["out"][:N]
```

```python
import math
from contextlib import ExitStack

import numpy as np

import concourse.bass as bass
from concourse import mybir

F32 = mybir.dt.float32
BF16 = mybir.dt.bfloat16
I32 = mybir.dt.int32
ALU = mybir.AluOpType
ACT = mybir.ActivationFunctionType
AX = mybir.AxisListType

P = 128
N, E = 6250, 106250
S0, V1 = 64, 32
F = S0 + 3 * V1
NEF, RN, DK = 12, 100, 64
EPS = 1e-5

WIN = 32
CHUNKS = 3
SUP = CHUNKS * P
QUAD = 4
NSUP = -(-E // SUP)
NCH = NSUP * CHUNKS
NQUAD = -(-NSUP // QUAD)
LAST = NSUP - (NQUAD - 1) * QUAD
ALLSUP = NQUAD * QUAD
EPAD = ALLSUP * SUP

BATCH = 5
NT = 2 * BATCH * -(-N // (2 * BATCH * P))
NBATCH = NT // BATCH
NPAD = NT * P
ROWS = NPAD + P
FG = NQUAD

PARTS = 3
KST = PARTS * PARTS * NEF
SEG = 10
SPLIT_ROWS = NEF * SEG
SPLIT_LEN = EPAD // SEG
SPLIT_STEPS = 14
SPLIT_SLOTS = 4
SPLIT_W = SPLIT_LEN // SPLIT_STEPS

C_S, C_X = math.sin(math.pi / 8), math.cos(math.pi / 8)


class Layer:
    PK0 = F

    def __init__(self, n):
        self.n = n
        self.wcols = 2 * S0 + (2 + n) * V1
        self.kin = RN if n == 0 else DK
        self.pcols = 2 * F + n * 3 * V1
        self.d_col = 2 * S0 + V1 * (1 + n)
        self.agg = self.pcols - F
        self.k1 = S0 + V1 if n == 0 else P
        self.k2 = 2 * V1 if n == 0 else P


L0, L1 = Layer(0), Layer(1)


def other_two(c):
    return [a for a in range(3) if a != c]


def wait_for(eng, sem, value):
    if not isinstance(value, int) or value > 0:
        eng.wait_ge(sem, value)


def waits_alone(eng, sem, value, least, *more):
    pairs = [(sem, value), *more]
    if isinstance(value, int):
        for s, v in pairs:
            wait_for(eng, s, v)
    else:
        pairs = [(s, eng.to_reg(v)) for s, v in pairs]
        eng.wait_ge(sem, least)
        for s, v in pairs:
            eng.wait_ge(s, v)


def within(step, first, last):
    return not isinstance(step, int) or first <= step < last


def rolled(eng, count, body, tail=1):
    body(0)
    with eng.Fori(1, count - tail) as i:
        body(i)
    for i in range(count - tail, count):
        body(i)


def gnn_kernel(nc, x, z_t, src_t, dst_t, dst_flat, base_row, y_t, rad_t, query_t,
               w_sc0, w_sc1, w_l10, w_l11, w_fc1, w_fc2, w_l20, w_l21,
               si_w0, si_w1, lin1_w0, lin1_w1, tp_w, lin2_w0, lin2_w1, out):
    ctx = ExitStack()
    with ctx:
        ctx.enter_context(nc.allow_non_contiguous_dma(reason="per-edge columns and per-channel weights, a few bytes per partition"))

        def sb(name, shape, dt=F32):
            return ctx.enter_context(nc.sbuf_tensor(name, shape, dt))

        def sem(name):
            return ctx.enter_context(nc.semaphore(name))

        def dram(name, shape, dt=F32):
            return nc.dram_tensor(name, shape, dt, kind="Internal").ap()

        table = [dram(f"table{n}", (NPAD, F)) for n in range(2)]
        acc = [dram(f"acc{n}", (2, ROWS, F)) for n in range(2)]
        split_d = dram("split_d", (PARTS * NEF, EPAD), BF16)

        X = sb("X", [P, NT * F])
        z_sb = sb("z_sb", [P, NT])
        ident = sb("ident", [P, P])
        win_i = sb("win_i", [P, WIN], I32)
        win = sb("win", [P, WIN])
        flag = sb("flag", [1, 1], I32)
        zero = sb("zero", [P, F])
        src_sb = sb("src_sb", [P, NCH], I32)
        meta_sb = sb("meta_sb", [P, NCH, 5])
        stats = sb("stats", [P, NT * 6])
        mean = sb("mean", [P, NT])
        rstd = sb("rstd", [P, NT])
        shift = sb("shift", [P, NT])
        base_sb = sb("base_sb", [1, ALLSUP + 2], I32)
        u0 = [sb(f"u0_{n}", [P, S0]) for n in range(2)]
        u1 = [sb(f"u1_{n}", [P, V1]) for n in range(2)]
        v1 = [sb(f"v1_{n}", [P, V1]) for n in range(2)]
        ra = [sb(f"ra{n}", [S0, 2 * S0]) for n in range(2)]
        rb = [sb(f"rb{n}", [3 * V1, 6 * V1]) for n in range(2)]
        r1 = [sb(f"r1_{n}", [P, 4, F]) for n in range(2)]
        r2 = [sb(f"r2_{n}", [P, F]) for n in range(2)]
        fc1_st = sb("fc1_st", [KST, RN], BF16)
        fc2_sb = sb("fc2_sb", [RN, L0.wcols])
        tp_sb = sb("tp_sb", [DK, L1.wcols])
        hn = sb("hn", [P, 2, F])
        hT = sb("hT", [P, 2, 2, P])
        rows2 = sb("rows2", [P, 2, F])
        idx = sb("idx", [P, QUAD, CHUNKS], I32)
        rad = sb("rad", [KST, 2, 2 * SUP], BF16)
        query = sb("query", [DK, 2, 2 * SUP])
        G = sb("G", [P, QUAD, CHUNKS, F])
        hid = sb("hid", [RN, 2, SUP])
        eq = sb("eq", [P, 2, CHUNKS, WIN])
        S = sb("S", [P, 2, CHUNKS, 4, WIN])
        Pr = sb("Pr", [P, 2, CHUNKS, L1.pcols])
        agg_sb = sb("agg_sb", [P, 2, F])
        T1 = sb("T1", [P, 4, QUAD, WIN])
        T2 = sb("T2", [P, QUAD, WIN])
        sums = sb("sums", [P, F])
        g_dst = sb("g_dst", [P, 1], I32)
        g_row = sb("g_row", [P, P], I32)
        g_dstf = sb("g_dstf", [P, 1])
        g_rowf = sb("g_rowf", [P, P])
        g_y = sb("g_y", [P, 4])
        g_eq = sb("g_eq", [P, P])
        g_low = sb("g_low", [P, P])
        g_dead = sb("g_dead", [P, 1])
        g_deadi = sb("g_deadi", [P, 1], I32)
        g_tmp = sb("g_tmp", [P, P])
        g_dup = sb("g_dup", [P, 2])
        g_to = sb("g_to", [P, 1], I32)
        g_S = sb("g_S", [P, 4, P])
        g_agg = sb("g_agg", [P, 4, F])

        wps = [ctx.enter_context(nc.psum_tensor(f"wps{b}", [P, 4, 256], F32)) for b in range(2)]
        aps = [ctx.enter_context(nc.psum_tensor(f"aps{b}", [P, 512], F32)) for b in range(2)]
        hps = ctx.enter_context(nc.psum_tensor("hps", [P, 512], F32))
        tps = ctx.enter_context(nc.psum_tensor("tps", [P, 512], F32))

        def x_tile(t):
            return X[:, bass.ds(t * F, F)]

        def load_weights(eng, n, w_in):
            a0, b0, a1, b1, c0, c1 = ((w_l10, w_sc0, w_l11, w_sc1, w_l20, w_l21),
                                      (lin1_w0, si_w0, lin1_w1, si_w1, lin2_w0, lin2_w1))[n]
            eng.dma_start(ra[n][:, 0:S0], a0).then_inc(w_in, 16)
            eng.dma_start(ra[n][:, S0:2 * S0], b0).then_inc(w_in, 16)
            for c in range(3):
                rows = slice(c, 3 * (V1 - 1) + c + 1, 3)
                eng.dma_start(rb[n][rows, c * V1:(c + 1) * V1], a1).then_inc(w_in, 16)
                eng.dma_start(rb[n][rows, (3 + c) * V1:(4 + c) * V1], b1).then_inc(w_in, 16)
            eng.dma_start(u0[n][0:S0 + V1, :], c0).then_inc(w_in, 16)
            eng.dma_start(u1[n][0:S0 + V1, :], c1).then_inc(w_in, 16)
            eng.dma_start(u1[n][S0 + V1:P, :], c1[S0:S0 + V1, :]).then_inc(w_in, 16)
            for q in range(4):
                eng.dma_start(v1[n][q * V1:(q + 1) * V1, :], c1[S0:S0 + V1, :]).then_inc(w_in, 16)

        W_LOADS = 15

        def scale_weights(dve, n):
            skip = C_S if n == 0 else 1.0
            dve.tensor_scalar_mul(ra[n][:, 0:S0], ra[n][:, 0:S0], S0 ** -0.5)
            dve.tensor_scalar_mul(ra[n][:, S0:], ra[n][:, S0:], skip * S0 ** -0.5)
            dve.tensor_scalar_mul(rb[n][:, 0:3 * V1], rb[n][:, 0:3 * V1], V1 ** -0.5)
            dve.tensor_scalar_mul(rb[n][:, 3 * V1:], rb[n][:, 3 * V1:], skip * V1 ** -0.5)
            f = (C_X * RN ** -0.5 * 8.0 ** -0.5 if n == 0 else 0.1) * (S0 + V1) ** -0.5
            fv = f if n == 0 else f * 2.0 ** -0.5
            o_s = r1[n][:, :, 0:S0]
            o_v = r1[n][:, :, S0:].rearrange("p k (v c) -> p k v c", c=3)
            q_v = r2[n][:, S0:].rearrange("p (v c) -> p v c", c=3)
            sr, vr, cr = slice(0, S0), slice(S0, S0 + V1), slice(S0 + V1, P)
            dve.tensor_scalar_mul(o_s[sr, 0, :], u0[n][sr, :], f)
            dve.tensor_scalar_mul(o_v[vr, 0, :, 0], u1[n][vr, :], fv)
            if n == 0:
                dve.tensor_scalar_mul(q_v[0:V1, :, 1], v1[n][0:V1, :], fv)
                dve.tensor_scalar_mul(q_v[V1:2 * V1, :, 2], v1[n][V1:2 * V1, :], fv)
            else:
                dve.tensor_scalar_mul(o_v[cr, 0, :, 1], u1[n][cr, :], fv)
                dve.tensor_scalar_mul(q_v[0:V1, :, 2], v1[n][0:V1, :], fv)
            for c in range(3):
                k = c + 1
                last = dve.tensor_scalar_mul(o_v[sr, k, :, c], u1[n][sr, :], f)
                last = dve.tensor_scalar_mul(o_s[vr, k, :], u0[n][vr, :], f * 3.0 ** -0.5)
                if n == 1:
                    for part, m in enumerate(other_two(c)):
                        to = 3 - c - m
                        g = 0.5 * f * (1.0 if (c - m) % 3 == 1 else -1.0)
                        if part == 0:
                            last = dve.tensor_scalar_mul(o_v[cr, k, :, to], u1[n][cr, :], g)
                        else:
                            rr = slice(k * V1, (k + 1) * V1)
                            last = dve.tensor_scalar_mul(q_v[rr, :, to], v1[n][rr, :], g)
            return last

        def first_phase():
            setup_ctx = ExitStack()
            with setup_ctx:
                def tmp(name, shape, dt=F32):
                    return setup_ctx.enter_context(nc.sbuf_tensor(name, shape, dt))

                dst_i = tmp("dst_i", [P, ALLSUP * CHUNKS], I32)
                dst_f = tmp("dst_f", [P, NCH])
                base_bc = tmp("base_bc", [P, NSUP], I32)
                base_f = tmp("base_f", [P, NSUP])
                y_sb = tmp("y_sb", [P, NCH * 4])
                by_sup = tmp("by_sup", [FG, QUAD * SUP], I32)
                by_sup_f = tmp("by_sup_f", [FG, QUAD, SUP])
                b_i = tmp("b_i", [FG, 2, QUAD], I32)
                b_f = tmp("b_f", [FG, 2, QUAD])
                ext = tmp("ext", [FG, 5, QUAD])
                worst = tmp("worst", [FG, 1])
                worst1 = tmp("worst1", [1, 1])
                w12 = tmp("w12", [NEF, RN])
                w12r = tmp("w12r", [NEF, RN])
                w12p = tmp("w12p", [NEF, PARTS, RN], BF16)
                rad_f = tmp("rad_f", [SPLIT_ROWS, SPLIT_SLOTS, SPLIT_W])
                rad_r = tmp("rad_r", [SPLIT_ROWS, SPLIT_SLOTS, SPLIT_W])
                rad_p = tmp("rad_p", [SPLIT_ROWS, SPLIT_SLOTS, PARTS, SPLIT_W], BF16)

                x_in = sem("x_in")
                small_in = sem("small_in")
                big_in = sem("big_in")
                consts = sem("consts")
                zeroed = sem("zeroed")
                w_in = [sem("w_in0"), sem("w_in1")]
                w_split = sem("w_split")
                fc1_in = sem("fc1_in")
                acc_zero = sem("acc_zero")
                chk = sem("chk")
                chk_t = sem("chk_t")
                d_chain = sem("d_chain")
                rad_in = [sem(f"rad_in{b}") for b in range(SPLIT_SLOTS)]
                rad_hi = sem("rad_hi")
                rad_rest = sem("rad_rest")
                rad_mid = sem("rad_mid")
                rad_lo = sem("rad_lo")
                rad_out = [sem(f"rad_out{b}") for b in range(SPLIT_SLOTS)]
                rad_src = rad_t.rearrange("i (s f) -> (i s) f", s=SEG)
                split_dst = split_d.rearrange("(a i) (s f) -> (i s) a f", a=PARTS, s=SEG)

                def sync_setup(sp):
                    def load(s):
                        b = s % SPLIT_SLOTS
                        if s >= SPLIT_SLOTS:
                            sp.wait_ge(rad_rest, s - SPLIT_SLOTS + 1)
                        sp.dma_start(rad_f[:, b, :], rad_src[:, s * SPLIT_W:(s + 1) * SPLIT_W]).then_inc(rad_in[b], 16)

                    def store(s):
                        b = s % SPLIT_SLOTS
                        sp.wait_ge(rad_lo, s + 1)
                        sp.dma_start(split_dst[:, :, s * SPLIT_W:(s + 1) * SPLIT_W], rad_p[:, b, :, :]).then_inc(rad_out[b], 16)

                    load(0)
                    load(1)
                    sp.dma_start(X[:, :].rearrange("p (t f) -> p t f", f=F), x.rearrange("(t p) f -> p t f", p=P)).then_inc(x_in, 16)
                    load(2)
                    load(3)
                    for s in range(SPLIT_STEPS):
                        if s + SPLIT_SLOTS < SPLIT_STEPS:
                            load(s + SPLIT_SLOTS)
                        store(s)

                def sync_end(sp):
                    for b in range(SPLIT_SLOTS):
                        sp.wait_ge(rad_out[b], 16 * len(range(b, SPLIT_STEPS, SPLIT_SLOTS)))

                def gpsimd_setup(pool):
                    pool.memset(ident[:, :], 0.0).then_inc(consts, 1)
                    pool.memset(g_low[:, :], 1.0).then_inc(consts, 1)
                    pool.iota(win_i[:, :], [[1, WIN]], base=0, channel_multiplier=0).then_inc(consts, 1)
                    pool.iota(g_deadi[:, :], [[0, 1]], base=NPAD, channel_multiplier=1).then_inc(consts, 1)
                    pool.wait_ge(consts, 4)
                    pool.affine_select(out=ident[:, :], in_=ident[:, :], compare_op=ALU.not_equal, fill=1.0,
                                       base=0, pattern=[[-1, P]], channel_multiplier=1).then_inc(consts, 1)
                    pool.affine_select(out=g_low[:, :], in_=g_low[:, :], compare_op=ALU.is_gt, fill=0.0,
                                       base=0, pattern=[[-1, P]], channel_multiplier=1).then_inc(consts, 1)
                    for s in range(SPLIT_STEPS):
                        b = s % SPLIT_SLOTS
                        pool.wait_ge(rad_hi, s + 1)
                        if s >= SPLIT_SLOTS:
                            pool.wait_ge(rad_lo, s - SPLIT_SLOTS + 1)
                        pool.tensor_tensor(rad_r[:, b, :], rad_f[:, b, :], rad_p[:, b, 0, :], ALU.subtract).then_inc(rad_rest, 1)
                    pool.wait_ge(zeroed, 7)
                    load_weights(pool, 1, w_in[1])
                    for n in range(2):
                        for h in range(2):
                            pool.dma_start(acc[n][h].rearrange("(p t) f -> p t f", p=P),
                                           zero[:, :].unsqueeze(1).broadcast_to([P, ROWS // P, F])).then_inc(acc_zero, 16)
                    pool.wait_ge(w_in[1], 16 * W_LOADS)
                    pool.wait_ge(acc_zero, 64)

                def scalar_setup(act):
                    act.dma_start(by_sup[:, :], dst_flat.rearrange("(g e) -> g e", g=FG)).then_inc(small_in, 16)
                    act.dma_start(b_i[:, 0, :], base_row[0, 0:ALLSUP].rearrange("(g q) -> g q", q=QUAD)).then_inc(small_in, 16)
                    act.dma_start(b_i[:, 1, :], base_row[0, 2:ALLSUP + 2].rearrange("(g q) -> g q", q=QUAD)).then_inc(small_in, 16)
                    act.dma_start(dst_i[:, :], dst_t).then_inc(small_in, 16)
                    act.dma_start(base_bc[:, :], base_row[0, 0:NSUP].partition_broadcast(P)).then_inc(small_in, 16)
                    act.dma_start(y_sb[:, :], y_t[:, 0:NCH * 4]).then_inc(big_in, 16)
                    act.dma_start(z_sb[:, :], z_t).then_inc(big_in, 16)
                    act.dma_start(base_sb[:, :], base_row).then_inc(big_in, 16)
                    act.dma_start(src_sb[:, :], src_t[:, 0:NCH]).then_inc(big_in, 16)
                    act.wait_ge(zeroed, 7)
                    load_weights(act, 0, w_in[0])
                    act.dma_start(w12[:, :], w_fc1).then_inc(w_in[0], 16)
                    act.dma_start(fc2_sb[:, :], w_fc2).then_inc(w_in[0], 16)
                    act.dma_start(tp_sb[:, :], tp_w).then_inc(w_in[0], 16)
                    for s in range(SPLIT_STEPS + 1):
                        if s < SPLIT_STEPS:
                            b = s % SPLIT_SLOTS
                            act.wait_ge(rad_in[b], 16 * (s // SPLIT_SLOTS + 1))
                            if s >= SPLIT_SLOTS:
                                act.wait_ge(rad_out[b], 16 * (s // SPLIT_SLOTS))
                            act.activation(rad_p[:, b, 0, :], rad_f[:, b, :], ACT.Copy).then_inc(rad_hi, 1)
                        if s >= 1:
                            b = (s - 1) % SPLIT_SLOTS
                            act.wait_ge(rad_rest, s)
                            act.activation(rad_p[:, b, 1, :], rad_r[:, b, :], ACT.Copy).then_inc(rad_mid, 1)
                    act.wait_ge(big_in, 64)
                    act.activation(meta_sb[:, :, 1:5], y_sb[:, :].rearrange("p (c k) -> p c k", k=4), ACT.Copy)
                    act.wait_ge(w_split, 3)
                    for wp in range(PARTS):
                        for xp in range(PARTS):
                            r0 = (wp * PARTS + xp) * NEF
                            act.dma_start(fc1_st[r0:r0 + NEF, :], w12p[:, wp, :]).then_inc(fc1_in, 16)

                def scalar_end(act):
                    act.wait_ge(fc1_in, 16 * PARTS * PARTS)

                def tensor_setup(pe):
                    pe.wait_ge(chk, 1)
                    pe.wait_ge(consts, 6)
                    nc.tensor.transpose(tps[0:1, 0:FG], worst[:, :], ident[0:FG, 0:FG]).then_inc(chk_t, 1)
                    pe.wait_ge(zeroed, 8)

                def vector_setup(dve):
                    steps = [0]

                    def link(ins):
                        steps[0] += 1
                        ins.then_inc(d_chain, 1)
                        dve.wait_ge(d_chain, steps[0])

                    dve.memset(zero[:, :], 0.0).then_inc(zeroed, 1)
                    for n in range(2):
                        dve.memset(rb[n][:, :], 0.0).then_inc(zeroed, 1)
                        dve.memset(r1[n][:, :, :], 0.0).then_inc(zeroed, 1)
                        dve.memset(r2[n][:, :], 0.0).then_inc(zeroed, 1)
                    dve.wait_ge(small_in, 80)
                    dve.tensor_copy(b_f[:, :, :], b_i[:, :, :])
                    link(dve.tensor_copy(by_sup_f[:, :, :], by_sup[:, :].rearrange("g (q e) -> g q e", q=QUAD)))
                    dve.tensor_reduce(out=ext[:, 0, :], in_=by_sup_f[:, :, :], op=ALU.min, axis=AX.X)
                    link(dve.tensor_reduce(out=ext[:, 1, :], in_=by_sup_f[:, :, :], op=ALU.max, axis=AX.X))
                    dve.tensor_tensor(ext[:, 2, :], b_f[:, 0, :], ext[:, 0, :], ALU.subtract)
                    dve.scalar_tensor_tensor(out=ext[:, 3, :], in0=ext[:, 1, :], scalar=float(1 - WIN), in1=b_f[:, 0, :], op0=ALU.add, op1=ALU.subtract)
                    link(dve.scalar_tensor_tensor(out=ext[:, 4, :], in0=ext[:, 1, :], scalar=1.0, in1=b_f[:, 1, :], op0=ALU.add, op1=ALU.subtract))
                    dve.tensor_reduce(out=worst[:, :], in_=ext[:, 2:5, :], op=ALU.max, axis=AX.XY).then_inc(chk, 1)
                    dve.tensor_copy(dst_f[:, :], dst_i[:, 0:NCH])
                    link(dve.tensor_copy(base_f[:, :], base_bc[:, :]))
                    dve.tensor_tensor(meta_sb[:, :, 0].rearrange("p (g c) -> p g c", c=CHUNKS),
                                      dst_f[:, :].rearrange("p (g c) -> p g c", c=CHUNKS),
                                      base_f[:, :].unsqueeze(2).broadcast_to([P, NSUP, CHUNKS]), ALU.subtract)
                    dve.wait_ge(consts, 6)
                    dve.tensor_copy(win[:, :], win_i[:, :])
                    dve.tensor_copy(g_dead[:, :], g_deadi[:, :])
                    dve.wait_ge(chk_t, 1)
                    link(dve.tensor_reduce(out=worst1[:, :], in_=tps[0:1, 0:FG], op=ALU.max, axis=AX.X))
                    dve.tensor_scalar(flag[:, :], worst1[:, :], 0.0, None, ALU.is_le)
                    dve.wait_ge(w_in[0], 16 * (W_LOADS + 3))
                    link(dve.tensor_copy(w12p[:, 0, :], w12[:, :]))
                    link(dve.tensor_tensor(w12r[:, :], w12[:, :], w12p[:, 0, :], ALU.subtract))
                    link(dve.tensor_copy(w12p[:, 1, :], w12r[:, :]))
                    dve.tensor_tensor(w12p[:, 2, :], w12r[:, :], w12p[:, 1, :], ALU.subtract).then_inc(w_split, 3)
                    scale_weights(dve, 0).then_inc(zeroed, 1)
                    dve.wait_ge(x_in, 16)
                    per_step = -(-NT // SPLIT_STEPS)
                    for s in range(SPLIT_STEPS):
                        for t in range(s * per_step, min(NT, (s + 1) * per_step)):
                            dve.bn_stats(stats[:, t * 6:(t + 1) * 6], X[:, t * F:(t + 1) * F])
                        b = s % SPLIT_SLOTS
                        dve.wait_ge(rad_mid, s + 1)
                        dve.tensor_tensor(rad_p[:, b, 2, :], rad_r[:, b, :], rad_p[:, b, 1, :], ALU.subtract).then_inc(rad_lo, 1)

                node_phase(0, {"sync": sync_setup, "sync_end": sync_end, "gpsimd": gpsimd_setup, "scalar": scalar_setup,
                               "scalar_end": scalar_end, "tensor": tensor_setup, "vector": vector_setup})

        def node_phase(n, beside):
            stat = sem(f"stat{n}")
            scaled = sem(f"scaled{n}")
            acc_in = [sem(f"acc_in{n}{b}") for b in range(2)]
            var_eps = sem(f"var_eps{n}")
            std_done = sem(f"std_done{n}")
            moments = sem(f"moments{n}")
            norm_done = sem(f"norm_done{n}")
            t_ps = sem(f"t_ps{n}")
            hT_done = sem(f"hT_done{n}")
            o_ps = sem(f"o_ps{n}")
            row_done = sem(f"row_done{n}")
            skip_done = sem(f"skip_done{n}")
            rows_out = [sem(f"rows_out{n}{b}") for b in range(2)]

            phase_ctx = ExitStack()
            if n == 1:
                accin = phase_ctx.enter_context(nc.sbuf_tensor("accin", [P, 2, 2, BATCH, F], F32))
            with phase_ctx, nc.Block() as block:
                @block.sync
                def _(sp):
                    if n == 0:
                        beside["sync"](sp)
                    else:
                        def load(i):
                            for b in range(2):
                                q = 2 * i + b
                                for h in range(2):
                                    src = acc[0][h, bass.ds(q * BATCH * P, BATCH * P), :].rearrange("(t p) f -> p t f", p=P)
                                    if h == 0:
                                        wait_for(sp, stat, 2 * q - 2)
                                    sp.dma_start(accin[:, b, h, :, :], src).then_inc(acc_in[b], 16)
                        rolled(sp, NBATCH // 2, load)

                    def store(i):
                        for b in range(2):
                            t = 2 * i + b
                            sp.wait_ge(row_done, t + 1)
                            sp.dma_start(table[n][bass.ds(t * P, P), :], rows2[:, b, :]).then_inc(rows_out[b], 16)
                    rolled(sp, NT // 2, store)
                    for b in range(2):
                        sp.wait_ge(rows_out[b], 8 * NT)
                    if n == 0:
                        beside["sync_end"](sp)

                if n == 0:
                    block.gpsimd(beside["gpsimd"])

                @block.vector
                def _(dve):
                    def add_sums(i, b):
                        q = 2 * i + b
                        dve.wait_ge(acc_in[b], 32 * i + 32)
                        dve.tensor_tensor(accin[:, b, 0, :, :], accin[:, b, 0, :, :], accin[:, b, 1, :, :], ALU.add).then_inc(stat, 1)
                        dve.wait_ge(stat, 2 * q + 1)
                        for r in range(BATCH):
                            t = q * BATCH + r
                            last = dve.scalar_tensor_tensor(out=x_tile(t), in0=accin[:, b, 0, r, :], scalar=z_sb[:, bass.ds(t, 1)], in1=x_tile(t), op0=ALU.mult, op1=ALU.add)
                        last.then_inc(stat, 1)

                    def statistics(q):
                        for r in range(BATCH):
                            t = q * BATCH + r
                            dve.bn_stats(stats[:, bass.ds(t * 6, 6)], x_tile(t))

                    if n == 0:
                        beside["vector"](dve)
                    else:
                        scale_weights(dve, 1).then_inc(scaled, 1)

                        def batches(i):
                            for b in range(2):
                                add_sums(i, b)
                                if within(2 * i + b - 1, 0, NBATCH):
                                    statistics(2 * i + b - 1)
                        rolled(dve, NBATCH // 2, batches)
                        dve.wait_ge(stat, 2 * NBATCH)
                        statistics(NBATCH - 1)
                    chain = [0]

                    def link(ins):
                        chain[0] += 1
                        ins.then_inc(moments, 1)
                        dve.wait_ge(moments, chain[0])

                    st = stats[:, :].rearrange("p (t s) -> p t s", s=6)
                    dve.engine_nop().then_inc(moments, 1)
                    chain[0] += 1
                    dve.wait_ge(moments, 1)
                    dve.tensor_tensor(mean[:, :], st[:, :, 1], st[:, :, 4], ALU.add)
                    dve.tensor_tensor(shift[:, :], st[:, :, 1], st[:, :, 4], ALU.subtract)
                    link(dve.tensor_tensor(rstd[:, :], st[:, :, 2], st[:, :, 5], ALU.add))
                    dve.tensor_scalar(rstd[:, :], rstd[:, :], 1.0 / F, EPS, ALU.mult, ALU.add)
                    link(dve.scalar_tensor_tensor(out=shift[:, :], in0=shift[:, :], scalar=0.25, in1=shift[:, :], op0=ALU.mult, op1=ALU.mult))
                    dve.tensor_tensor(rstd[:, :], rstd[:, :], shift[:, :], ALU.add).then_inc(var_eps, 1)
                    dve.wait_ge(std_done, 1)
                    link(dve.reciprocal(rstd[:, :], rstd[:, :]))
                    link(dve.scalar_tensor_tensor(out=shift[:, :], in0=mean[:, :], scalar=-0.5, in1=rstd[:, :], op0=ALU.mult, op1=ALU.mult))

                    def norm(t, b):
                        wait_for(dve, t_ps, t - 1)
                        dve.tensor_scalar(hn[:, b, :], x_tile(t), rstd[:, bass.ds(t, 1)], shift[:, bass.ds(t, 1)], ALU.mult, ALU.add).then_inc(norm_done, 1)

                    def add_skip(t, b):
                        dve.wait_ge(o_ps, t + 1)
                        dve.wait_ge(norm_done, t + 1)
                        o = wps[b][:, :, :].rearrange("p a c -> p (a c)")
                        x_s, x_v = X[:, bass.ds(t * F, S0)], X[:, bass.ds(t * F + S0, 3 * V1)].rearrange("p (v c) -> p v c", c=3)
                        k_s, k_v = o[:, F:F + S0], o[:, F + S0:2 * F].rearrange("p (c v) -> p v c", c=3)
                        if n == 0:
                            zc = z_sb[:, bass.ds(t, 1)]
                            dve.scalar_tensor_tensor(out=x_s, in0=k_s, scalar=zc, in1=x_s, op0=ALU.mult, op1=ALU.add)
                            dve.scalar_tensor_tensor(out=x_v, in0=k_v, scalar=zc, in1=x_v, op0=ALU.mult, op1=ALU.add).then_inc(skip_done, 1)
                        else:
                            dve.tensor_tensor(x_s, k_s, x_s, ALU.add)
                            dve.tensor_tensor(x_v, k_v, x_v, ALU.add).then_inc(skip_done, 1)

                    norm(0, 0)
                    norm(1, 1)

                    def tiles(i):
                        for b in range(2):
                            t = 2 * i + b
                            if within(t + 2, 0, NT):
                                norm(t + 2, b)
                            add_skip(t, b)
                    rolled(dve, NT // 2, tiles)

                @block.tensor
                def _(pe):
                    def transposes(t, b):
                        pe.wait_ge(norm_done, t + 1)
                        wait_for(pe, hT_done, t - 1)
                        nc.tensor.transpose(aps[b][0:3 * V1, P:2 * P], hn[:, b, S0:F], ident[:, :])
                        nc.tensor.transpose(aps[b][0:S0, 0:P], hn[:, b, 0:S0], ident[:, :]).then_inc(t_ps, 1)

                    def project(t, b):
                        pe.wait_ge(hT_done, t + 1)
                        wait_for(pe, row_done, t - 1)
                        wait_for(pe, skip_done, t - 1)
                        o = wps[b][:, :, :].rearrange("p a c -> p (a c)")[:, 0:2 * F].rearrange("p (h f) -> p h f", h=2)
                        nc.tensor.matmul(o[:, :, 0:S0], hT[0:S0, b, 0, :], ra[n][:, :].rearrange("p (h f) -> p h f", h=2), start=True, stop=True)
                        nc.tensor.matmul(o[:, :, S0:F], hT[0:3 * V1, b, 1, :], rb[n][:, :].rearrange("p (h f) -> p h f", h=2), start=True, stop=True).then_inc(o_ps, 1)

                    if n == 0:
                        beside["tensor"](pe)
                    else:
                        pe.wait_ge(scaled, 1)
                    transposes(0, 0)

                    def tiles(i):
                        for b in range(2):
                            t = 2 * i + b
                            if within(t + 1, 0, NT):
                                transposes(t + 1, 1 - b)
                            project(t, b)
                    rolled(pe, NT // 2, tiles)

                @block.scalar
                def _(act):
                    if n == 0:
                        beside["scalar"](act)
                    act.wait_ge(var_eps, 1)
                    act.activation(rstd[:, :], rstd[:, :], ACT.Sqrt).then_inc(std_done, 1)

                    def relu(t, b):
                        act.wait_ge(t_ps, t + 1)
                        wait_for(act, o_ps, t - 1)
                        act.activation(hT[0:S0, b, 0, :], aps[b][0:S0, 0:P], ACT.Relu)
                        act.activation(hT[0:3 * V1, b, 1, :], aps[b][0:3 * V1, P:2 * P], ACT.Relu).then_inc(hT_done, 1)

                    def table_row(i, t, b):
                        act.wait_ge(skip_done, t + 1)
                        wait_for(act, rows_out[b], 16 * i)
                        o = wps[b][:, :, :].rearrange("p a c -> p (a c)")[:, 0:F]
                        if n == 0:
                            act.activation(rows2[:, b, :], o, ACT.Copy, scale=z_sb[:, bass.ds(t, 1)]).then_inc(row_done, 1)
                        else:
                            act.activation(rows2[:, b, :], o, ACT.Copy).then_inc(row_done, 1)

                    relu(0, 0)

                    def tiles(i):
                        for b in range(2):
                            t = 2 * i + b
                            if within(t + 1, 0, NT):
                                relu(t + 1, 1 - b)
                            table_row(i, t, b)
                    rolled(act, NT // 2, tiles)
                    if n == 0:
                        beside["scalar_end"](act)

        def edge_phase(L):
            n = L.n
            idx_done = sem(f"idx_done{n}")
            edge_in = [sem(f"edge_in{n}{h}") for h in range(2)]
            gathered = [sem(f"gathered{n}{j}") for j in range(QUAD)]
            hid_ps, hid_done = sem(f"hid_ps{n}"), sem(f"hid_done{n}")
            w_ps = sem(f"w_ps{n}")
            eq_done, S_done, P_done = sem(f"eq_done{n}"), sem(f"S_done{n}"), sem(f"P_done{n}")
            agg_ps, agg_done = sem(f"agg_ps{n}"), sem(f"agg_done{n}")
            tr_ps, tr_done = sem(f"tr_ps{n}"), sem(f"tr_done{n}")
            sum_ps, sum_done = sem(f"sum_ps{n}"), sem(f"sum_done{n}")
            sum_out = [sem(f"sum_out{n}{j}") for j in range(QUAD)]
            c_in, c_gathered, c_added = sem(f"c_in{n}"), sem(f"c_gathered{n}"), sem(f"c_added{n}")
            c_hid_ps, c_hid, c_w = sem(f"c_hid_ps{n}"), sem(f"c_hid{n}"), sem(f"c_w{n}")
            c_dve, c_ready = sem(f"c_dve{n}"), sem(f"c_ready{n}")
            c_agg_ps, c_agg, c_tr_ps, c_tr = sem(f"c_agg_ps{n}"), sem(f"c_agg{n}"), sem(f"c_tr_ps{n}"), sem(f"c_tr{n}")
            c_sum_ps, c_sum = sem(f"c_sum_ps{n}"), sem(f"c_sum{n}")

            def is_windowed(eng):
                return eng.value_load(flag[0:1, 0:1], min_val=0, max_val=1) == 1

            def radial_matmul(out_ap, lhs_slot, e0, w):
                return nc.tensor.matmul(out_ap, fc1_st[:, :], rad[:, lhs_slot, e0:e0 + w], start=True, stop=True)

            def weight_matmul(out_ap, j, c):
                if n == 0:
                    return nc.tensor.matmul(out_ap, hid[:, j % 2, c * P:(c + 1) * P], fc2_sb[:, :], start=True, stop=True)
                e0 = j % 2 * SUP + c * P
                return nc.tensor.matmul(out_ap, query[:, j // 2, e0:e0 + P], tp_sb[:, :], start=True, stop=True)

            def products(dve, out_p, w, g, m):
                h1 = g[:, :, S0:F].rearrange("p c (d v) -> p c d v", d=3)

                def vec(col, w_col):
                    return dve.tensor_tensor(out_p[:, :, col:col + 3 * V1].rearrange("p c (d v) -> p c d v", d=3),
                                             w[:, :, w_col:w_col + V1].unsqueeze(2).broadcast_to([P, m, 3, V1]), h1, ALU.mult)
                dve.tensor_tensor(out_p[:, :, 0:2 * F].rearrange("p c (h f) -> p c h f", h=2)[:, :, :, 0:S0],
                                  w[:, :, 0:2 * S0].rearrange("p c (h f) -> p c h f", h=2),
                                  g[:, :, 0:S0].unsqueeze(2).broadcast_to([P, m, 2, S0]), ALU.mult)
                vec(S0, 2 * S0)
                if n == 1:
                    vec(2 * F, 2 * S0 + V1)
                return vec(F + S0, L.d_col)

            def aggregate_matmul(out_ap, s_ap, p_ap, k, start, stop, tile):
                cols = slice(0, F) if k == 0 else slice(F, L.pcols)
                return nc.tensor.matmul(out_ap, s_ap, p_ap[:, cols], start=start, stop=stop, tile_position=tile)

            def pack_component(act, dst, src, k, rows):
                c = k - 1
                last = act.activation(dst[rows, S0:S0 + V1], src[rows, S0 + c * V1:S0 + (c + 1) * V1], ACT.Copy)
                if n == 1:
                    m0, m1 = other_two(c)
                    b0 = S0 + 3 * V1
                    pair = src[rows, b0:b0 + 3 * V1].rearrange("p (m v) -> p m v", m=3)[:, m0:m1 + 1:m1 - m0, :]
                    last = act.activation(dst[rows, S0 + V1:F].rearrange("p (m v) -> p m v", m=2), pair, ACT.Copy)
                return last

            def sums_ps():
                return tps[:, 2 * P:2 * P + F]

            def output_matmuls():
                for k in range(4):
                    nc.tensor.matmul(sums_ps(), T1[0:L.k1, k, :, :].rearrange("p q w -> p (q w)"), r1[n][0:L.k1, k, :], start=(k == 0), stop=False)
                return nc.tensor.matmul(sums_ps(), T2[0:L.k2, :, :].rearrange("p q w -> p (q w)"), r2[n][0:L.k2, :], start=False, stop=True)

            with nc.Block() as block:
                @block.sync
                def _(sp):
                    def load_edges(i, h):
                        e0 = bass.ds(i * QUAD * SUP + h * 2 * SUP, 2 * SUP)
                        wait_for(sp, hid_ps if n == 0 else w_ps, QUAD * (i - 1) + 2 * h + 2)
                        if n == 0:
                            for a in range(PARTS):
                                r0 = a * PARTS * NEF
                                sp.dma_start(rad[r0:r0 + PARTS * NEF, h, :], split_d[:, e0]).then_inc(edge_in[h], 16)
                        else:
                            sp.dma_start(query[:, h, :], query_t[:, e0]).then_inc(edge_in[h], 16)

                    def store_sums(i, j):
                        before = 2 * (j // 2) + j % 2 - 2 if j >= 2 else j + 2
                        start = sp.value_load(base_sb[0:1, bass.ds(QUAD * i + j, 1)], min_val=0, max_val=NPAD - WIN)
                        to = acc[n][j % 2, bass.ds(start, WIN), :]
                        waits_alone(sp, sum_done, i + 1, 1)
                        waits_alone(sp, sum_out[before], 16 * (i + 1) if j >= 2 else 16 * i, 16)
                        sp.dma_start(to, sums[j * WIN:(j + 1) * WIN, :]).then_inc(sum_out[j], 16)

                    def quad(i):
                        if within(i + 1, 0, NQUAD):
                            load_edges(i + 1, 0)
                            if not isinstance(i, int) or (i + 1) * QUAD + 2 < NSUP:
                                load_edges(i + 1, 1)
                        if within(i - 1, 0, NQUAD):
                            for j in range(QUAD):
                                store_sums(i - 1, j)

                    def drain():
                        for j in range(LAST):
                            store_sums(NQUAD - 1, j)
                        for j in range(QUAD):
                            sp.wait_ge(sum_out[j], 16 * (NQUAD if j < LAST else NQUAD - 1))

                    def chunk(m):
                        waits_alone(sp, c_added, 16 * m, 16)
                        e0 = bass.ds(m * P, P)
                        sp.dma_start(idx[:, 0, 0:1], src_t[:, bass.ds(m, 1)]).then_inc(c_in, 16)
                        sp.dma_start(g_dst[:, :], dst_t[:, bass.ds(m, 1)]).then_inc(c_in, 16)
                        sp.dma_start(g_row[:, :], dst_flat[e0].partition_broadcast(P)).then_inc(c_in, 16)
                        sp.dma_start(g_y[:, :], y_t[:, bass.ds(4 * m, 4)]).then_inc(c_in, 16)
                        if n == 0:
                            for a in range(PARTS):
                                r0 = a * PARTS * NEF
                                sp.dma_start(rad[r0:r0 + PARTS * NEF, 0, 0:P], split_d[:, e0]).then_inc(c_in, 16)
                        else:
                            sp.dma_start(query[:, 0, 0:P], query_t[:, e0]).then_inc(c_in, 16)

                    with sp.If(is_windowed(sp)):
                        load_edges(0, 0)
                        load_edges(0, 1)
                        quad(0)
                        quad(1)
                        with sp.Fori(2, NQUAD - 2) as i:
                            quad(i)
                        quad(NQUAD - 2)
                        quad(NQUAD - 1)
                        drain()
                    with sp.Else():
                        chunk(0)
                        with sp.Fori(1, NCH) as m:
                            chunk(m)
                        sp.wait_ge(c_added, 16 * NCH)

                loads_per_chunk = 16 * (7 if n == 0 else 5)
                edge_loads = 16 * (PARTS if n == 0 else 1)

                @block.gpsimd
                def _(pool):
                    def gather(i, j):
                        g = QUAD * i + j
                        waits_alone(pool, idx_done, g + 1, 1)
                        for c in range(CHUNKS):
                            pool.indirect_dma_start(out=G[:, j, c, :], out_offset=None, in_=table[n][:, :],
                                                    in_offset=bass.IndirectOffsetOnAxis(ap=idx[:, j, c:c + 1], axis=0)).then_inc(gathered[j], 16)

                    def quad(i):
                        for j in range(QUAD):
                            if within(QUAD * i + j, 0, NSUP):
                                gather(i, j)

                    def chunk(m):
                        waits_alone(pool, c_in, loads_per_chunk * (m + 1), loads_per_chunk)
                        pool.indirect_dma_start(out=G[:, 0, 0, :], out_offset=None, in_=table[n][:, :],
                                                in_offset=bass.IndirectOffsetOnAxis(ap=idx[:, 0, 0:1], axis=0)).then_inc(c_gathered, 16)
                        waits_alone(pool, c_ready, m + 1, 1)
                        pool.wait_ge(c_sum, m + 1)
                        pool.indirect_dma_start(out=acc[n][0], out_offset=bass.IndirectOffsetOnAxis(ap=g_to[:, 0:1], axis=0),
                                                in_=sums[:, :], in_offset=None, compute_op=ALU.add).then_inc(c_added, 16)

                    with pool.If(is_windowed(pool)):
                        rolled(pool, NQUAD, quad)
                    with pool.Else():
                        with pool.Fori(0, NCH) as m:
                            chunk(m)

                @block.tensor
                def _(pe):
                    def hidden(i, j):
                        g = QUAD * i + j
                        pe.wait_ge(edge_in[j // 2], edge_loads * (i + 1))
                        wait_for(pe, hid_done, g)
                        radial_matmul(hps[0:RN, 0:SUP], j // 2, j % 2 * SUP, SUP).then_inc(hid_ps, 1)

                    def radial_weights(i, j):
                        g = QUAD * i + j
                        if n == 0:
                            pe.wait_ge(hid_done, g + 1)
                        else:
                            pe.wait_ge(edge_in[j // 2], edge_loads * (i + 1))
                        wait_for(pe, P_done, g - 1)
                        for c in range(CHUNKS):
                            last = weight_matmul(wps[j % 2][:, c, 0:L.wcols], j, c)
                        last.then_inc(w_ps, 1)

                    def aggregate(i, j):
                        g = QUAD * i + j
                        b = j % 2
                        pe.wait_ge(S_done, g + 1)
                        pe.wait_ge(P_done, g + 1)
                        wait_for(pe, agg_done, g - 1)
                        for c in range(CHUNKS):
                            for k in range(4):
                                width = F if k == 0 else L.agg
                                last = aggregate_matmul(aps[b][k * WIN:(k + 1) * WIN, 0:width], S[:, b, c, k, :], Pr[:, b, c, :],
                                                        k, c == 0, c == CHUNKS - 1, (0, k * WIN))
                        last.then_inc(agg_ps, 1)

                    def transposes(g, b, quads_out=None):
                        pe.wait_ge(agg_done, g + 1)
                        if quads_out is not None:
                            wait_for(pe, sum_done, quads_out)
                        wait_for(pe, tr_done, g)
                        nc.tensor.transpose(tps[0:L.k1, 0:P], agg_sb[:, b, 0:L.k1], ident[:, :])
                        if n == 0:
                            last = nc.tensor.transpose(tps[0:2 * V1, P:P + WIN], agg_sb[0:WIN, b, L.k1:F], ident[0:WIN, 0:WIN])
                        else:
                            last = nc.tensor.transpose(tps[0:V1, P:2 * P], agg_sb[:, b, L.k1:F], ident[:, :])
                        last.then_inc(tr_ps, 1)

                    def output(i):
                        pe.wait_ge(tr_done, min(NSUP, QUAD * (i + 1)) if isinstance(i, int) else QUAD * (i + 1))
                        wait_for(pe, sum_done, i)
                        output_matmuls().then_inc(sum_ps, 1)

                    def quad(i):
                        for j in range(QUAD):
                            g = QUAD * i + j
                            if not within(g, 0, NSUP):
                                break
                            if n == 0 and within(g + 2, 0, NSUP):
                                hidden(i + (j + 2) // QUAD, (j + 2) % QUAD)
                            if within(g + 1, 0, NSUP):
                                radial_weights(i + (j + 1) // QUAD, (j + 1) % QUAD)
                            aggregate(i, j)
                            if j == 1 and within(i - 1, 0, NQUAD):
                                output(i - 1)
                            if within(g - 1, 0, NSUP):
                                transposes(g - 1, (j - 1) % 2, i if j == 1 else None)

                    def chunk(m):
                        pe.wait_ge(c_in, loads_per_chunk * (m + 1))
                        if n == 0:
                            radial_matmul(hps[0:RN, 0:P], 0, 0, P).then_inc(c_hid_ps, 1)
                            pe.wait_ge(c_hid, m + 1)
                        weight_matmul(wps[0][:, 0, 0:L.wcols], 0, 0).then_inc(c_w, 1)
                        pe.wait_ge(c_ready, m + 1)
                        for k in range(4):
                            width = F if k == 0 else L.agg
                            last = aggregate_matmul(aps[k // 2][:, 256 * (k % 2):256 * (k % 2) + width], g_S[:, k, :], Pr[:, 0, 0, :], k, True, True, None)
                        last.then_inc(c_agg_ps, 1)
                        pe.wait_ge(c_agg, m + 1)
                        for k in range(4):
                            last = nc.tensor.transpose(wps[1][0:L.k1, k // 2, P * (k % 2):P * (k % 2) + P], g_agg[:, k, 0:L.k1], ident[:, :])
                        if n == 0:
                            last = nc.tensor.transpose(wps[1][0:2 * V1, 2, 0:P], g_agg[:, 0, L.k1:F], ident[:, :])
                        else:
                            for k in range(4):
                                last = nc.tensor.transpose(wps[1][0:V1, 2 + k // 2, P * (k % 2):P * (k % 2) + P], g_agg[:, k, L.k1:F], ident[:, :])
                        last.then_inc(c_tr_ps, 1)
                        pe.wait_ge(c_tr, m + 1)
                        output_matmuls().then_inc(c_sum_ps, 1)

                    with pe.If(is_windowed(pe)):
                        if n == 0:
                            hidden(0, 0)
                            hidden(0, 1)
                        radial_weights(0, 0)
                        rolled(pe, NQUAD, quad, tail=2)
                        if LAST == 1:
                            output(NQUAD - 2)
                        transposes(NSUP - 1, (NSUP - 1) % 2, NQUAD - 1)
                        output(NQUAD - 1)
                    with pe.Else():
                        with pe.Fori(0, NCH) as m:
                            chunk(m)

                @block.scalar
                def _(act):
                    def silu(g, b):
                        act.wait_ge(hid_ps, g + 1)
                        wait_for(act, w_ps, g - 1)
                        act.activation(hid[:, b, :], hps[0:RN, 0:SUP], ACT.Silu, scale=NEF ** -0.5).then_inc(hid_done, 1)

                    def pack(g, b):
                        act.wait_ge(agg_ps, g + 1)
                        wait_for(act, tr_ps, g - 1)
                        act.activation(agg_sb[:, b, 0:S0], aps[b][:, 0:S0], ACT.Copy)
                        act.activation(agg_sb[0:WIN, b, S0:F], aps[b][0:WIN, S0:F], ACT.Copy)
                        for k in range(1, 4):
                            last = pack_component(act, agg_sb[:, b, :], aps[b], k, slice(k * WIN, (k + 1) * WIN))
                        last.then_inc(agg_done, 1)

                    def transposed(i, j):
                        g = QUAD * i + j
                        act.wait_ge(tr_ps, g + 1)
                        if j == 0:
                            wait_for(act, sum_ps, i)
                        last = act.activation(T1[0:L.k1, :, j, :], tps[0:L.k1, 0:P].rearrange("p (k w) -> p k w", k=4), ACT.Copy)
                        if n == 0:
                            last = act.activation(T2[0:2 * V1, j, :], tps[0:2 * V1, P:P + WIN], ACT.Copy)
                        else:
                            for k in range(4):
                                last = act.activation(T2[k * V1:(k + 1) * V1, j, :], tps[0:V1, P + k * WIN:P + (k + 1) * WIN], ACT.Copy)
                        last.then_inc(tr_done, 1)

                    def window_sums(i):
                        act.wait_ge(sum_ps, i + 1)
                        for j in range(QUAD):
                            wait_for(act, sum_out[j], 16 * i)
                        act.activation(sums[:, :], sums_ps(), ACT.Copy).then_inc(sum_done, 1)

                    def quad(i):
                        for j in range(QUAD):
                            g = QUAD * i + j
                            if not within(g, 0, NSUP):
                                break
                            if n == 0 and within(g + 2, 0, NSUP):
                                silu(g + 2, j % 2)
                            pack(g, j % 2)
                            if j == 1 and within(i - 1, 0, NQUAD):
                                window_sums(i - 1)
                            if within(g - 1, 0, NSUP):
                                transposed(i - 1 if j == 0 else i, (j - 1) % QUAD)

                    def chunk(m):
                        if n == 0:
                            act.wait_ge(c_hid_ps, m + 1)
                            act.activation(hid[:, 0, 0:P], hps[0:RN, 0:P], ACT.Silu, scale=NEF ** -0.5).then_inc(c_hid, 1)
                        act.wait_ge(c_agg_ps, m + 1)
                        every = slice(0, P)
                        act.activation(g_agg[:, 0, :], aps[0][:, 0:F], ACT.Copy)
                        for k in range(1, 4):
                            at = aps[k // 2][:, 256 * (k % 2):256 * (k % 2) + 256]
                            act.activation(g_agg[:, k, 0:S0], at[:, 0:S0], ACT.Copy)
                            last = pack_component(act, g_agg[:, k, :], at, k, every)
                        last.then_inc(c_agg, 1)
                        act.wait_ge(c_tr_ps, m + 1)
                        for k in range(4):
                            last = act.activation(T1[0:L.k1, k, :, :].rearrange("p q w -> p (q w)"), wps[1][0:L.k1, k // 2, P * (k % 2):P * (k % 2) + P], ACT.Copy)
                        if n == 0:
                            last = act.activation(T2[0:2 * V1, :, :].rearrange("p q w -> p (q w)"), wps[1][0:2 * V1, 2, 0:P], ACT.Copy)
                        else:
                            for k in range(4):
                                last = act.activation(T2[k * V1:(k + 1) * V1, :, :].rearrange("p q w -> p (q w)"),
                                                      wps[1][0:V1, 2 + k // 2, P * (k % 2):P * (k % 2) + P], ACT.Copy)
                        last.then_inc(c_tr, 1)
                        act.wait_ge(c_sum_ps, m + 1)
                        act.activation(sums[:, :], sums_ps(), ACT.Copy).then_inc(c_sum, 1)

                    with act.If(is_windowed(act)):
                        if n == 0:
                            silu(0, 0)
                            silu(1, 1)
                        rolled(act, NQUAD, quad, tail=2)
                        if LAST == 1:
                            window_sums(NQUAD - 2)
                        transposed(NQUAD - 1, LAST - 1)
                        window_sums(NQUAD - 1)
                    with act.Else():
                        with act.Fori(0, NCH) as m:
                            chunk(m)

                @block.vector
                def _(dve):
                    def select(i, j):
                        g = QUAD * i + j
                        wait_for(dve, S_done, g - 1)
                        dve.tensor_tensor(eq[:, j % 2, :, :], win[:, :].unsqueeze(1).broadcast_to([P, CHUNKS, WIN]),
                                          meta_sb[:, bass.ds(g * CHUNKS, CHUNKS), 0:1].broadcast_to([P, CHUNKS, WIN]), ALU.is_equal).then_inc(eq_done, 1)

                    def scale(g, j):
                        dve.wait_ge(eq_done, g + 1)
                        wait_for(dve, agg_ps, g - 1)
                        shape = [P, CHUNKS, 4, WIN]
                        dve.tensor_tensor(S[:, j % 2, :, :, :], eq[:, j % 2, :, :].unsqueeze(2).broadcast_to(shape),
                                          meta_sb[:, bass.ds(g * CHUNKS, CHUNKS), 1:5].unsqueeze(3).broadcast_to(shape), ALU.mult).then_inc(S_done, 1)

                    def multiply(i, j):
                        g = QUAD * i + j
                        dve.wait_ge(w_ps, g + 1)
                        dve.wait_ge(gathered[j], 16 * CHUNKS * (i + 1))
                        wait_for(dve, agg_ps, g - 1)
                        products(dve, Pr[:, j % 2, :, :], wps[j % 2][:, 0:CHUNKS, :], G[:, j, :, :], CHUNKS).then_inc(P_done, 1)

                    def indices(g, j):
                        dve.tensor_copy(idx[:, j, :], src_sb[:, bass.ds(g * CHUNKS, CHUNKS)]).then_inc(idx_done, 1)

                    def quad(i):
                        for j in range(QUAD):
                            g = QUAD * i + j
                            if not within(g, 0, NSUP):
                                break
                            more = within(g + 1, 0, NSUP)
                            if more:
                                select(i + (j + 1) // QUAD, (j + 1) % QUAD)
                            multiply(i, j)
                            if within(g + QUAD, 0, NSUP):
                                indices(g + QUAD, j)
                            if more:
                                scale(g + 1, (j + 1) % QUAD)

                    DUP_OPS = 8

                    def chunk(m):
                        s = [0]

                        def link(ins):
                            s[0] += 1
                            ins.then_inc(c_dve, 1)
                            dve.wait_ge(c_dve, DUP_OPS * m + s[0])
                        dve.wait_ge(c_in, loads_per_chunk * (m + 1))
                        link(dve.tensor_copy(g_dstf[:, :], g_dst[:, :]))
                        link(dve.tensor_copy(g_rowf[:, :], g_row[:, :]))
                        link(dve.tensor_scalar(g_eq[:, :], g_rowf[:, :], g_dstf[:, 0:1], None, ALU.is_equal))
                        shape = [P, 4, P]
                        dve.tensor_tensor(g_S[:, :, :], g_eq[:, :].unsqueeze(1).broadcast_to(shape), g_y[:, :].unsqueeze(2).broadcast_to(shape), ALU.mult)
                        link(dve.tensor_tensor(g_tmp[:, :], g_eq[:, :], g_low[:, :], ALU.mult))
                        link(dve.tensor_reduce(out=g_dup[:, 0:1], in_=g_tmp[:, :], op=ALU.max, axis=AX.X))
                        link(dve.tensor_tensor(g_dup[:, 1:2], g_dead[:, :], g_dstf[:, :], ALU.subtract))
                        link(dve.scalar_tensor_tensor(out=g_dup[:, 1:2], in0=g_dup[:, 1:2], scalar=g_dup[:, 0:1], in1=g_dstf[:, :], op0=ALU.mult, op1=ALU.add))
                        link(dve.tensor_copy(g_to[:, :], g_dup[:, 1:2]))
                        assert s[0] == DUP_OPS
                        dve.wait_ge(c_w, m + 1)
                        dve.wait_ge(c_gathered, 16 * (m + 1))
                        products(dve, Pr[:, 0, 0:1, :], wps[0][:, 0:1, :], G[:, 0, 0:1, :], 1).then_inc(c_ready, 1)

                    with dve.If(is_windowed(dve)):
                        for j in range(QUAD):
                            indices(j, j)
                        select(0, 0)
                        scale(0, 0)
                        rolled(dve, NQUAD, quad, tail=2)
                    with dve.Else():
                        with dve.Fori(0, NCH) as m:
                            chunk(m)

        def output_phase():
            SLOTS = 4
            acc_in = [sem(f"out_in{b}") for b in range(SLOTS)]
            added = sem("added")
            out_done = [sem(f"out_done{b}") for b in range(SLOTS)]
            with nc.sbuf_tensor("accout", [P, SLOTS, 2, BATCH, F], F32) as accout, nc.Block() as block:
                @block.sync
                def _(sp):
                    for q in range(NBATCH):
                        b = q % SLOTS
                        if q >= SLOTS:
                            sp.wait_ge(out_done[b], 16 * (q // SLOTS))
                        for h in range(2):
                            src = acc[1][h, q * BATCH * P:(q + 1) * BATCH * P, :].rearrange("(t p) f -> p t f", p=P)
                            sp.dma_start(accout[:, b, h, :, :], src).then_inc(acc_in[b], 16)

                @block.scalar
                def _(act):
                    for q in range(NBATCH):
                        b = q % SLOTS
                        act.wait_ge(added, 2 * q + 2)
                        act.dma_start(out[q * BATCH * P:(q + 1) * BATCH * P, :].rearrange("(t p) f -> p t f", p=P), accout[:, b, 1, :, :]).then_inc(out_done[b], 16)
                    for b in range(SLOTS):
                        act.wait_ge(out_done[b], 16 * len(range(b, NBATCH, SLOTS)))

                @block.vector
                def _(dve):
                    for q in range(NBATCH):
                        b = q % SLOTS
                        dve.wait_ge(acc_in[b], 32 * (q // SLOTS + 1))
                        dve.tensor_tensor(accout[:, b, 0, :, :], accout[:, b, 0, :, :], accout[:, b, 1, :, :], ALU.add).then_inc(added, 1)
                        dve.wait_ge(added, 2 * q + 1)
                        x_b = X[:, q * BATCH * F:(q + 1) * BATCH * F].rearrange("p (t f) -> p t f", f=F)
                        dve.tensor_tensor(accout[:, b, 1, :, :], accout[:, b, 0, :, :], x_b, ALU.add).then_inc(added, 1)

        first_phase()
        edge_phase(L0)
        node_phase(1, None)
        edge_phase(L1)
        output_phase()


def kernel(x, src, dst, edge_attr_12, edge_attr_4, edge_attr_64, node_vec1,
           L0_gnn_W_sc0, L0_gnn_W_sc1, L0_gnn_W_l1_0, L0_gnn_W_l1_1, L0_gnn_W_fc1, L0_gnn_W_fc2, L0_gnn_W_l2_0, L0_gnn_W_l2_1,
           L1_gnn_si_w0, L1_gnn_si_w1, L1_gnn_lin1_w0, L1_gnn_lin1_w1, L1_gnn_tp_weight, L1_gnn_lin2_w0, L1_gnn_lin2_w1):
    import concourse.bacc as bacc
    from concourse.bass_utils import run_bass_kernel_spmd

    def pad(a, rows, mode="constant"):
        a = np.asarray(a)
        return np.pad(a, [(0, rows - a.shape[0])] + [(0, 0)] * (a.ndim - 1), mode=mode)

    def by_chunk(a):
        a = a.reshape((-1, P) + a.shape[1:])
        return np.ascontiguousarray(np.moveaxis(a, 0, 1).reshape(P, -1))

    dst_pad = pad(dst, EPAD, "edge")
    dst_pad[NSUP * SUP:] = np.repeat(np.arange(N, N + ALLSUP - NSUP, dtype=dst_pad.dtype), SUP)
    base = np.concatenate([dst_pad[::SUP], np.full(2, NPAD - 1, dst_pad.dtype)]).reshape(1, -1)
    arrays = {
        "x": pad(x, NPAD),
        "z_t": np.ascontiguousarray(pad(node_vec1, NPAD).reshape(NT, P).T),
        "src_t": by_chunk(pad(src, EPAD)),
        "dst_t": by_chunk(dst_pad),
        "dst_flat": dst_pad,
        "base_row": base,
        "y_t": by_chunk(pad(edge_attr_4, EPAD)),
        "rad_t": np.ascontiguousarray(pad(edge_attr_12, EPAD).T),
        "query_t": np.ascontiguousarray(pad(edge_attr_64, EPAD).T),
        "w_sc0": L0_gnn_W_sc0, "w_sc1": L0_gnn_W_sc1, "w_l10": L0_gnn_W_l1_0, "w_l11": L0_gnn_W_l1_1,
        "w_fc1": L0_gnn_W_fc1, "w_fc2": L0_gnn_W_fc2, "w_l20": L0_gnn_W_l2_0, "w_l21": L0_gnn_W_l2_1,
        "si_w0": L1_gnn_si_w0, "si_w1": L1_gnn_si_w1, "lin1_w0": L1_gnn_lin1_w0, "lin1_w1": L1_gnn_lin1_w1,
        "tp_w": L1_gnn_tp_weight, "lin2_w0": L1_gnn_lin2_w0, "lin2_w1": L1_gnn_lin2_w1,
    }
    arrays = {k: np.ascontiguousarray(v) for k, v in arrays.items()}
    nc = bacc.Bacc("TRN2", target_bir_lowering=False, num_devices=1)
    aps = {k: nc.dram_tensor(k, v.shape, mybir.dt.from_np(v.dtype), kind="ExternalInput").ap() for k, v in arrays.items()}
    out = nc.dram_tensor("out", (NPAD, F), F32, kind="ExternalOutput").ap()
    gnn_kernel(nc, out=out, **aps)
    r = run_bass_kernel_spmd(nc, [arrays], core_ids=[0])
    return r.results[0]["out"][:N]
```

```python
import math
from contextlib import ExitStack

import numpy as np

import concourse.bass as bass
from concourse import mybir

F32 = mybir.dt.float32
BF16 = mybir.dt.bfloat16
I32 = mybir.dt.int32
ALU = mybir.AluOpType
ACT = mybir.ActivationFunctionType
AX = mybir.AxisListType

P = 128
N, E = 6250, 106250
S0, V1 = 64, 32
F = S0 + 3 * V1
NEF, RN, DK = 12, 100, 64
EPS = 1e-5

WIN = 32
CHUNKS = 3
SUP = CHUNKS * P
QUAD = 4
NSUP = -(-E // SUP)
NCH = NSUP * CHUNKS
NQUAD = -(-NSUP // QUAD)
LAST = NSUP - (NQUAD - 1) * QUAD
ALLSUP = NQUAD * QUAD
EPAD = ALLSUP * SUP

BATCH = 5
NT = 2 * BATCH * -(-N // (2 * BATCH * P))
NBATCH = NT // BATCH
NPAD = NT * P
ROWS = NPAD + P
FG = NQUAD

PARTS = 3
KST = PARTS * PARTS * NEF
SPLIT = P // NEF
while QUAD * SUP % SPLIT:
    SPLIT -= 1
SPLIT_P = NEF * SPLIT
SPLIT_W = QUAD * SUP // SPLIT

C_S, C_X = math.sin(math.pi / 8), math.cos(math.pi / 8)


class Layer:
    PK0 = F

    def __init__(self, n):
        self.n = n
        self.wcols = 2 * S0 + (2 + n) * V1
        self.kin = RN if n == 0 else DK
        self.pcols = 2 * F + n * 3 * V1
        self.d_col = 2 * S0 + V1 * (1 + n)
        self.agg = self.pcols - F
        self.k1 = S0 + V1 if n == 0 else P
        self.k2 = 2 * V1 if n == 0 else P


L0, L1 = Layer(0), Layer(1)


def other_two(c):
    return [a for a in range(3) if a != c]


def wait_for(eng, sem, value):
    if not isinstance(value, int) or value > 0:
        eng.wait_ge(sem, value)


def waits_alone(eng, sem, value, least, *more):
    pairs = [(sem, value), *more]
    if isinstance(value, int):
        for s, v in pairs:
            wait_for(eng, s, v)
    else:
        pairs = [(s, eng.to_reg(v)) for s, v in pairs]
        eng.wait_ge(sem, least)
        for s, v in pairs:
            eng.wait_ge(s, v)


def within(step, first, last):
    return not isinstance(step, int) or first <= step < last


def rolled(eng, count, body, tail=1):
    body(0)
    with eng.Fori(1, count - tail) as i:
        body(i)
    for i in range(count - tail, count):
        body(i)


def gnn_kernel(nc, x, z_t, src_t, dst_t, dst_flat, base_row, y_t, rad_t, rad_q, query_t,
               w_sc0, w_sc1, w_l10, w_l11, w_fc1, w_fc2, w_l20, w_l21,
               si_w0, si_w1, lin1_w0, lin1_w1, tp_w, lin2_w0, lin2_w1, out):
    ctx = ExitStack()
    with ctx:
        ctx.enter_context(nc.allow_non_contiguous_dma(reason="per-edge columns and per-channel weights, a few bytes per partition"))

        def sb(name, shape, dt=F32):
            return ctx.enter_context(nc.sbuf_tensor(name, shape, dt))

        def sem(name):
            return ctx.enter_context(nc.semaphore(name))

        def dram(name, shape, dt=F32):
            return nc.dram_tensor(name, shape, dt, kind="Internal").ap()

        table = [dram(f"table{n}", (NPAD, F)) for n in range(2)]
        acc = [dram(f"acc{n}", (2, ROWS, F)) for n in range(2)]

        split_d = dram("split_d", (NQUAD * PARTS * NEF, QUAD * SUP), BF16)

        X = sb("X", [P, NT * F])
        z_sb = sb("z_sb", [P, NT])
        ident = sb("ident", [P, P])
        win_i = sb("win_i", [P, WIN], I32)
        win = sb("win", [P, WIN])
        flag = sb("flag", [1, 1], I32)
        zero = sb("zero", [P, F])
        src_sb = sb("src_sb", [P, NCH], I32)
        meta_sb = sb("meta_sb", [P, NCH, 5])
        stats = sb("stats", [P, NT * 6])
        mean = sb("mean", [P, NT])
        rstd = sb("rstd", [P, NT])
        shift = sb("shift", [P, NT])
        base_sb = sb("base_sb", [1, ALLSUP + 2], I32)
        u0 = [sb(f"u0_{n}", [P, S0]) for n in range(2)]
        u1 = [sb(f"u1_{n}", [P, V1]) for n in range(2)]
        v1 = [sb(f"v1_{n}", [P, V1]) for n in range(2)]
        ra = [sb(f"ra{n}", [S0, 2 * S0]) for n in range(2)]
        rb = [sb(f"rb{n}", [3 * V1, 6 * V1]) for n in range(2)]
        r1 = [sb(f"r1_{n}", [P, 4, F]) for n in range(2)]
        r2 = [sb(f"r2_{n}", [P, F]) for n in range(2)]
        fc1_sb = sb("fc1_sb", [NEF, RN])
        fc1_st = sb("fc1_st", [KST, RN], BF16)
        fc2_sb = sb("fc2_sb", [RN, L0.wcols])
        tp_sb = sb("tp_sb", [DK, L1.wcols])
        hn = sb("hn", [P, 2, F])
        hT = sb("hT", [P, 2, 2, P])
        rows2 = sb("rows2", [P, 2, BATCH, F])
        idx = sb("idx", [P, QUAD, CHUNKS], I32)
        rad = sb("rad", [KST, 2, 2 * SUP], BF16)
        rad_f = sb("rad_f", [SPLIT_P, SPLIT_W])
        rad_r = sb("rad_r", [SPLIT_P, SPLIT_W])
        rad_p = sb("rad_p", [SPLIT_P, PARTS, SPLIT_W], BF16)
        query = sb("query", [DK, 2, 2 * SUP])
        G = sb("G", [P, QUAD, CHUNKS, F])
        hid = sb("hid", [RN, 2, SUP])
        eq = sb("eq", [P, 2, CHUNKS, WIN])
        S = sb("S", [P, 2, CHUNKS, 4, WIN])
        Pr = sb("Pr", [P, 2, CHUNKS, L1.pcols])
        agg_sb = sb("agg_sb", [P, 2, F])
        T1 = sb("T1", [P, 4, QUAD, WIN])
        T2 = sb("T2", [P, QUAD, WIN])
        sums = sb("sums", [P, F])
        g_dst = sb("g_dst", [P, 1], I32)
        g_row = sb("g_row", [P, P], I32)
        g_dstf = sb("g_dstf", [P, 1])
        g_rowf = sb("g_rowf", [P, P])
        g_rad = sb("g_rad", [NEF, P])
        g_y = sb("g_y", [P, 4])
        g_eq = sb("g_eq", [P, P])
        g_low = sb("g_low", [P, P])
        g_dead = sb("g_dead", [P, 1])
        g_deadi = sb("g_deadi", [P, 1], I32)
        g_tmp = sb("g_tmp", [P, P])
        g_dup = sb("g_dup", [P, 2])
        g_to = sb("g_to", [P, 1], I32)
        g_S = sb("g_S", [P, 4, P])
        g_agg = sb("g_agg", [P, 4, F])

        wps = [ctx.enter_context(nc.psum_tensor(f"wps{b}", [P, 4, 256], F32)) for b in range(2)]
        aps = [ctx.enter_context(nc.psum_tensor(f"aps{b}", [P, 512], F32)) for b in range(2)]
        hps = ctx.enter_context(nc.psum_tensor("hps", [P, 512], F32))
        tps = ctx.enter_context(nc.psum_tensor("tps", [P, 512], F32))

        x_loaded = sem("x_loaded")

        def keep_clock(count):
            for _ in range(count):
                nc.tensor.matmul(tps[:, 0:P], ident[:, :], ident[:, :], start=True, stop=True)

        def x_tile(t):
            return X[:, bass.ds(t * F, F)]

        def node_and_output_weights(n):
            return ((w_l10, w_sc0, w_l11, w_sc1, w_l20, w_l21),
                    (lin1_w0, si_w0, lin1_w1, si_w1, lin2_w0, lin2_w1))[n]

        NODE_LOADS, OUTPUT_LOADS = 8, 7

        def load_node_weights(eng, n, w_in):
            a0, b0, a1, b1, _, _ = node_and_output_weights(n)
            eng.dma_start(ra[n][:, 0:S0], a0).then_inc(w_in, 16)
            eng.dma_start(ra[n][:, S0:2 * S0], b0).then_inc(w_in, 16)
            for c in range(3):
                rows = slice(c, 3 * (V1 - 1) + c + 1, 3)
                eng.dma_start(rb[n][rows, c * V1:(c + 1) * V1], a1).then_inc(w_in, 16)
                eng.dma_start(rb[n][rows, (3 + c) * V1:(4 + c) * V1], b1).then_inc(w_in, 16)

        def load_output_weights(eng, n, u_in):
            c0, c1 = node_and_output_weights(n)[4:]
            eng.dma_start(u0[n][0:S0 + V1, :], c0).then_inc(u_in, 16)
            eng.dma_start(u1[n][0:S0 + V1, :], c1).then_inc(u_in, 16)
            eng.dma_start(u1[n][S0 + V1:P, :], c1[S0:S0 + V1, :]).then_inc(u_in, 16)
            for q in range(4):
                eng.dma_start(v1[n][q * V1:(q + 1) * V1, :], c1[S0:S0 + V1, :]).then_inc(u_in, 16)

        def scale_node_weights(dve, n):
            skip = C_S if n == 0 else 1.0
            dve.tensor_scalar_mul(ra[n][:, 0:S0], ra[n][:, 0:S0], S0 ** -0.5)
            dve.tensor_scalar_mul(ra[n][:, S0:], ra[n][:, S0:], skip * S0 ** -0.5)
            dve.tensor_scalar_mul(rb[n][:, 0:3 * V1], rb[n][:, 0:3 * V1], V1 ** -0.5)
            return dve.tensor_scalar_mul(rb[n][:, 3 * V1:], rb[n][:, 3 * V1:], skip * V1 ** -0.5)

        def scale_output_weights(dve, n):
            f = (C_X * RN ** -0.5 * 8.0 ** -0.5 if n == 0 else 0.1) * (S0 + V1) ** -0.5
            fv = f if n == 0 else f * 2.0 ** -0.5
            o_s = r1[n][:, :, 0:S0]
            o_v = r1[n][:, :, S0:].rearrange("p k (v c) -> p k v c", c=3)
            q_v = r2[n][:, S0:].rearrange("p (v c) -> p v c", c=3)
            sr, vr, cr = slice(0, S0), slice(S0, S0 + V1), slice(S0 + V1, P)
            dve.tensor_scalar_mul(o_s[sr, 0, :], u0[n][sr, :], f)
            dve.tensor_scalar_mul(o_v[vr, 0, :, 0], u1[n][vr, :], fv)
            if n == 0:
                dve.tensor_scalar_mul(q_v[0:V1, :, 1], v1[n][0:V1, :], fv)
                dve.tensor_scalar_mul(q_v[V1:2 * V1, :, 2], v1[n][V1:2 * V1, :], fv)
            else:
                dve.tensor_scalar_mul(o_v[cr, 0, :, 1], u1[n][cr, :], fv)
                dve.tensor_scalar_mul(q_v[0:V1, :, 2], v1[n][0:V1, :], fv)
            for c in range(3):
                k = c + 1
                last = dve.tensor_scalar_mul(o_v[sr, k, :, c], u1[n][sr, :], f)
                last = dve.tensor_scalar_mul(o_s[vr, k, :], u0[n][vr, :], f * 3.0 ** -0.5)
                if n == 1:
                    for part, m in enumerate(other_two(c)):
                        to = 3 - c - m
                        g = 0.5 * f * (1.0 if (c - m) % 3 == 1 else -1.0)
                        if part == 0:
                            last = dve.tensor_scalar_mul(o_v[cr, k, :, to], u1[n][cr, :], g)
                        else:
                            rr = slice(k * V1, (k + 1) * V1)
                            last = dve.tensor_scalar_mul(q_v[rr, :, to], v1[n][rr, :], g)
            return last

        def first_phase():
            setup_ctx = ExitStack()
            with setup_ctx:
                def tmp(name, shape, dt=F32):
                    return setup_ctx.enter_context(nc.sbuf_tensor(name, shape, dt))

                dst_i = tmp("dst_i", [P, ALLSUP * CHUNKS], I32)
                dst_f = tmp("dst_f", [P, NCH])
                base_bc = tmp("base_bc", [P, NSUP], I32)
                base_f = tmp("base_f", [P, NSUP])
                y_sb = tmp("y_sb", [P, NCH * 4])
                by_sup = tmp("by_sup", [FG, QUAD * SUP], I32)
                by_sup_f = tmp("by_sup_f", [FG, QUAD, SUP])
                b_i = tmp("b_i", [FG, 2, QUAD], I32)
                b_f = tmp("b_f", [FG, 2, QUAD])
                ext = tmp("ext", [FG, 5, QUAD])
                worst = tmp("worst", [FG, 1])
                worst1 = tmp("worst1", [1, 1])

                w12r = tmp("w12r", [NEF, RN])
                w12p = tmp("w12p", [NEF, PARTS, RN], BF16)

                w_split = sem("w_split")
                fc1_in = sem("fc1_in")
                f_in = sem("f_in")
                small_in = sem("small_in")
                big_in = sem("big_in")
                consts = sem("consts")
                zeroed = sem("zeroed")
                w_in = [sem("w_in0"), sem("w_in1")]
                u_in = [sem("u_in0"), sem("u_in1")]
                chk_in = sem("chk_in")
                chk = sem("chk")
                chk_t = sem("chk_t")
                p_chain = sem("p_chain")
                d_chain = sem("d_chain")

                def sync_setup(sp):
                    sp.wait_ge(zeroed, 1)
                    load_node_weights(sp, 0, w_in[0])

                def sync_next(sp):
                    sp.dma_start(fc1_sb[:, :], w_fc1).then_inc(f_in, 16)
                    sp.dma_start(fc2_sb[:, :], w_fc2).then_inc(f_in, 16)
                    sp.dma_start(tp_sb[:, :], tp_w).then_inc(f_in, 16)
                    load_output_weights(sp, 0, u_in[0])
                    sp.wait_ge(zeroed, 7)
                    load_node_weights(sp, 1, w_in[1])
                    load_output_weights(sp, 1, u_in[1])

                def sync_end(sp):
                    sp.wait_ge(w_in[1], 16 * NODE_LOADS)
                    sp.wait_ge(u_in[1], 16 * OUTPUT_LOADS)

                def gpsimd_setup(pool):
                    pool.memset(ident[:, :], 0.0).then_inc(consts, 1)
                    pool.memset(g_low[:, :], 1.0).then_inc(consts, 1)
                    pool.iota(win_i[:, :], [[1, WIN]], base=0, channel_multiplier=0).then_inc(consts, 1)
                    pool.iota(g_deadi[:, :], [[0, 1]], base=NPAD, channel_multiplier=1).then_inc(consts, 1)
                    pool.wait_ge(consts, 4)
                    pool.affine_select(out=ident[:, :], in_=ident[:, :], compare_op=ALU.not_equal, fill=1.0,
                                       base=0, pattern=[[-1, P]], channel_multiplier=1).then_inc(consts, 1)
                    pool.affine_select(out=g_low[:, :], in_=g_low[:, :], compare_op=ALU.is_gt, fill=0.0,
                                       base=0, pattern=[[-1, P]], channel_multiplier=1).then_inc(consts, 1)
                    pool.dma_start(by_sup[:, :], dst_flat.rearrange("(g e) -> g e", g=FG)).then_inc(small_in, 16)
                    pool.dma_start(b_i[:, 0, :], base_row[0, 0:ALLSUP].rearrange("(g q) -> g q", q=QUAD)).then_inc(small_in, 16)
                    pool.dma_start(b_i[:, 1, :], base_row[0, 2:ALLSUP + 2].rearrange("(g q) -> g q", q=QUAD)).then_inc(small_in, 16)
                    pool.dma_start(dst_i[:, :], dst_t).then_inc(big_in, 16)
                    pool.dma_start(base_bc[:, :], base_row[0, 0:NSUP].partition_broadcast(P)).then_inc(big_in, 16)
                    pool.dma_start(y_sb[:, :], y_t[:, 0:NCH * 4]).then_inc(big_in, 16)
                    pool.dma_start(base_sb[:, :], base_row).then_inc(big_in, 16)
                    pool.dma_start(src_sb[:, :], src_t[:, 0:NCH]).then_inc(big_in, 16)
                    pool.wait_ge(small_in, 48)
                    pool.tensor_copy(b_f[:, :, :], b_i[:, :, :])
                    pool.tensor_copy(by_sup_f[:, :, :], by_sup[:, :].rearrange("g (q e) -> g q e", q=QUAD)).then_inc(p_chain, 1)
                    pool.wait_ge(big_in, 80)
                    pool.tensor_copy(dst_f[:, :], dst_i[:, 0:NCH])
                    pool.tensor_copy(base_f[:, :], base_bc[:, :]).then_inc(p_chain, 1)
                    pool.tensor_copy(meta_sb[:, :, 1:5], y_sb[:, :].rearrange("p (c k) -> p c k", k=4))
                    pool.wait_ge(p_chain, 2)
                    pool.tensor_tensor(meta_sb[:, :, 0].rearrange("p (g c) -> p g c", c=CHUNKS),
                                       dst_f[:, :].rearrange("p (g c) -> p g c", c=CHUNKS),
                                       base_f[:, :].unsqueeze(2).broadcast_to([P, NSUP, CHUNKS]), ALU.subtract).then_inc(chk_in, 1)
                    pool.wait_ge(w_split, 1)
                    for wp in range(PARTS):
                        for xp in range(PARTS):
                            r0 = (wp * PARTS + xp) * NEF
                            pool.dma_start(fc1_st[r0:r0 + NEF, :], w12p[:, wp, :]).then_inc(fc1_in, 16)
                    pool.wait_ge(zeroed, 7)

                def gpsimd_end(pool):
                    pool.wait_ge(fc1_in, 16 * PARTS * PARTS)

                def tensor_setup(pe):
                    pe.wait_ge(consts, 6)
                    pe.wait_ge(zeroed, 8)

                def tensor_end(pe):
                    pe.wait_ge(chk, 1)
                    nc.tensor.transpose(tps[0:1, 0:FG], worst[:, :], ident[0:FG, 0:FG]).then_inc(chk_t, 1)

                def vector_setup(dve):
                    for n in range(2):
                        dve.memset(rb[n][:, :], 0.0).then_inc(zeroed, 1)
                        dve.memset(r1[n][:, :, :], 0.0).then_inc(zeroed, 1)
                        dve.memset(r2[n][:, :], 0.0).then_inc(zeroed, 1)
                    dve.memset(zero[:, :], 0.0).then_inc(zeroed, 1)

                def vector_weights(dve):
                    dve.wait_ge(w_in[0], 16 * NODE_LOADS)
                    scale_node_weights(dve, 0).then_inc(zeroed, 1)

                def radial_weight_parts(dve):
                    dve.wait_ge(f_in, 48)
                    dve.tensor_copy(w12p[:, 0, :], fc1_sb[:, :]).then_inc(d_chain, 1)
                    dve.wait_ge(d_chain, 1)
                    dve.tensor_tensor(w12r[:, :], fc1_sb[:, :], w12p[:, 0, :], ALU.subtract).then_inc(d_chain, 1)
                    dve.wait_ge(d_chain, 2)
                    dve.tensor_copy(w12p[:, 1, :], w12r[:, :]).then_inc(d_chain, 1)
                    dve.wait_ge(d_chain, 3)
                    dve.tensor_tensor(w12p[:, 2, :], w12r[:, :], w12p[:, 1, :], ALU.subtract).then_inc(w_split, 1)

                def output_weights_0(dve):
                    dve.wait_ge(u_in[0], 16 * OUTPUT_LOADS)
                    scale_output_weights(dve, 0)

                def output_weights_1(dve):
                    dve.wait_ge(u_in[1], 16 * OUTPUT_LOADS)
                    scale_output_weights(dve, 1)

                def smallest_dst(dve):
                    dve.wait_ge(chk_in, 1)
                    dve.tensor_reduce(out=ext[:, 0, :], in_=by_sup_f[:, :, :], op=ALU.min, axis=AX.X).then_inc(d_chain, 1)

                def largest_dst(dve):
                    dve.tensor_reduce(out=ext[:, 1, :], in_=by_sup_f[:, :, :], op=ALU.max, axis=AX.X).then_inc(d_chain, 1)
                    dve.wait_ge(d_chain, 5)

                def window_check(dve):
                    dve.tensor_copy(win[:, :], win_i[:, :])
                    dve.tensor_copy(g_dead[:, :], g_deadi[:, :])
                    dve.tensor_tensor(ext[:, 2, :], b_f[:, 0, :], ext[:, 0, :], ALU.subtract)
                    dve.scalar_tensor_tensor(out=ext[:, 3, :], in0=ext[:, 1, :], scalar=float(1 - WIN), in1=b_f[:, 0, :], op0=ALU.add, op1=ALU.subtract)
                    dve.scalar_tensor_tensor(out=ext[:, 4, :], in0=ext[:, 1, :], scalar=1.0, in1=b_f[:, 1, :], op0=ALU.add, op1=ALU.subtract).then_inc(d_chain, 1)
                    dve.wait_ge(d_chain, 6)
                    dve.tensor_reduce(out=worst[:, :], in_=ext[:, 2:5, :], op=ALU.max, axis=AX.XY).then_inc(chk, 1)

                vector_late = [output_weights_0, output_weights_1, smallest_dst, largest_dst, window_check]

                def vector_end(dve):
                    dve.wait_ge(chk_t, 1)
                    dve.tensor_reduce(out=worst1[:, :], in_=tps[0:1, 0:FG], op=ALU.max, axis=AX.X).then_inc(chk, 1)
                    dve.wait_ge(chk, 2)
                    dve.tensor_scalar(flag[:, :], worst1[:, :], 0.0, None, ALU.is_le)

                node_phase(0, {"gpsimd": gpsimd_setup, "tensor": tensor_setup, "tensor_end": tensor_end,
                               "vector": vector_setup, "vector_weights": vector_weights, "vector_end": vector_end,
                               "vector_early": radial_weight_parts, "vector_late": vector_late,
                               "sync": sync_setup, "sync_next": sync_next, "sync_end": sync_end, "gpsimd_end": gpsimd_end})

        def node_phase(n, beside):
            loaded = [sem(f"loaded{n}{b}") for b in range(2)]
            paired = sem(f"paired{n}")
            summed = sem(f"summed{n}")
            scaled = sem(f"scaled{n}")
            stats_done = sem(f"stats_done{n}")
            moments = sem(f"moments{n}")
            var_eps = sem(f"var_eps{n}")
            std_done = sem(f"std_done{n}")
            shift_done = sem(f"shift_done{n}")
            norm_done = sem(f"norm_done{n}")
            t_ps = sem(f"t_ps{n}")
            hT_done = sem(f"hT_done{n}")
            o_ps = sem(f"o_ps{n}")
            row_done = sem(f"row_done{n}")
            skip_done = sem(f"skip_done{n}")
            rows_out = [sem(f"rows_out{n}{b}") for b in range(2)]
            z_in = sem(f"z_in{n}")
            x_more = sem(f"x_more{n}")
            sums_zero = sem(f"sums_zero{n}")
            MOMENTS = 3

            def projected(r):
                bank = hps[:, :] if r == 4 else wps[r // 2][:, 2 * (r % 2):2 * (r % 2) + 2, :].rearrange("p a c -> p (a c)")
                return bank[:, 0:2 * F]

            def steps(i):
                for b in range(2):
                    for r in range(BATCH):
                        u = b * BATCH + r
                        yield b, r, 2 * BATCH * i + u, u % 2

            phase_ctx = ExitStack()
            if n == 1:
                accin = phase_ctx.enter_context(nc.sbuf_tensor("accin", [P, 2, 2, BATCH, F], F32))
            with phase_ctx, nc.Block() as block:
                @block.sync
                def _(sp):
                    def load_x(first, last, done):
                        sp.dma_start(X[:, first * BATCH * F:last * BATCH * F].rearrange("p (t f) -> p t f", f=F),
                                     x[first * BATCH * P:last * BATCH * P, :].rearrange("(t p) f -> p t f", p=P)).then_inc(done, 16)

                    def load(i, b):
                        q = 2 * i + b
                        wait_for(sp, summed, BATCH * (q - 1))
                        for h in range(2):
                            sp.dma_start(accin[:, b, h, :, :], acc[0][h, bass.ds(q * BATCH * P, BATCH * P), :].rearrange("(t p) f -> p t f", p=P)).then_inc(loaded[b], 16)

                    if n == 0:
                        load_x(0, 1, loaded[0])
                        beside["sync"](sp)
                        load_x(1, 2, loaded[1])
                        sp.dma_start(z_sb[:, :], z_t).then_inc(z_in, 16)
                        load_x(2, 4, x_more)
                        load_x(4, NBATCH, x_loaded)
                        beside["sync_next"](sp)
                    else:
                        load(0, 0)
                        load(0, 1)
                        load(1, 0)
                        load(1, 1)

                    def batches(i):
                        for b in range(2):
                            q = 2 * i + b
                            if n == 1 and within(i + 2, 0, NBATCH // 2):
                                load(i + 2, b)
                            sp.wait_ge(row_done, (q + 1) * BATCH)
                            sp.dma_start(table[n][bass.ds(q * BATCH * P, BATCH * P), :].rearrange("(t p) f -> p t f", p=P), rows2[:, b, :, :]).then_inc(rows_out[b], 16)
                    rolled(sp, NBATCH // 2, batches, tail=2)
                    for b in range(2):
                        sp.wait_ge(rows_out[b], 8 * NBATCH)
                    if n == 0:
                        beside["sync_end"](sp)

                @block.gpsimd
                def _(pool):
                    def zero_sums(q):
                        for h in range(2):
                            pool.dma_start(acc[n][h, bass.ds(q * BATCH * P, BATCH * P), :].rearrange("(t p) f -> p t f", p=P),
                                           zero[:, :].unsqueeze(1).broadcast_to([P, BATCH, F])).then_inc(sums_zero, 16)

                    def pair(i):
                        for b in range(2):
                            pool.wait_ge(loaded[b], 32 * i + 32)
                            pool.tensor_tensor(accin[:, b, 0, :, :], accin[:, b, 0, :, :], accin[:, b, 1, :, :], ALU.add).then_inc(paired, 1)
                            zero_sums(2 * i + b)

                    if n == 0:
                        beside["gpsimd"](pool)
                        pool.wait_ge(x_loaded, 16)
                        with pool.Fori(0, NBATCH) as q:
                            pool.wait_ge(row_done, q * BATCH + 1)
                            zero_sums(q)
                    else:
                        rolled(pool, NBATCH // 2, pair)
                    for h in range(2):
                        pool.dma_start(acc[n][h, NPAD:ROWS, :], zero[:, :]).then_inc(sums_zero, 16)
                    if n == 0:
                        beside["gpsimd_end"](pool)
                    pool.wait_ge(sums_zero, 32 * (NBATCH + 1))

                @block.vector
                def _(dve):
                    def add_sums(i, b, tiles):
                        q = 2 * i + b
                        if tiles[0] == 0:
                            dve.wait_ge(paired, q + 1)
                        for r in tiles:
                            t = q * BATCH + r
                            dve.scalar_tensor_tensor(out=x_tile(t), in0=accin[:, b, 0, r, :], scalar=z_sb[:, bass.ds(t, 1)], in1=x_tile(t), op0=ALU.mult, op1=ALU.add).then_inc(summed, 1)

                    def per_tile(a, q):
                        return a[:, bass.ds(q * BATCH, BATCH)]

                    def statistics(i, b, tiles):
                        q = 2 * i + b
                        if n == 0 and isinstance(i, int) and i == 1:
                            dve.wait_ge(x_more, 16)
                        elif n == 0 and within(i, 2, NBATCH):
                            dve.wait_ge(x_loaded, 16)
                        elif n == 0:
                            dve.wait_ge(loaded[b], 16)
                        else:
                            waits_alone(dve, summed, q * BATCH + tiles[-1] + 1, 1)
                        for r in tiles:
                            t = q * BATCH + r
                            last = dve.bn_stats(stats[:, bass.ds(t * 6, 6)], x_tile(t))
                        if tiles[-1] == BATCH - 1:
                            last.then_inc(stats_done, 1)

                    def moments_sums(q):
                        st = stats[:, bass.ds(q * BATCH * 6, BATCH * 6)].rearrange("p (t s) -> p t s", s=6)
                        dve.wait_ge(stats_done, q + 1)
                        dve.tensor_tensor(per_tile(mean, q), st[:, :, 1], st[:, :, 4], ALU.add)
                        dve.tensor_tensor(per_tile(shift, q), st[:, :, 1], st[:, :, 4], ALU.subtract)
                        dve.tensor_tensor(per_tile(rstd, q), st[:, :, 2], st[:, :, 5], ALU.add).then_inc(moments, 1)

                    def moments_scaled(q):
                        rstd_q, shift_q = per_tile(rstd, q), per_tile(shift, q)
                        dve.wait_ge(moments, MOMENTS * q + 1)
                        dve.tensor_scalar(rstd_q, rstd_q, 1.0 / F, EPS, ALU.mult, ALU.add)
                        dve.scalar_tensor_tensor(out=shift_q, in0=shift_q, scalar=0.25, in1=shift_q, op0=ALU.mult, op1=ALU.mult).then_inc(moments, 1)

                    def variance(q):
                        dve.wait_ge(moments, MOMENTS * q + 2)
                        dve.tensor_tensor(per_tile(rstd, q), per_tile(rstd, q), per_tile(shift, q), ALU.add).then_inc(var_eps, 1)

                    def scale_shift(q):
                        waits_alone(dve, std_done, q + 1, 1)
                        dve.reciprocal(per_tile(rstd, q), per_tile(rstd, q)).then_inc(moments, 1)
                        dve.wait_ge(moments, MOMENTS * (q + 1))
                        dve.scalar_tensor_tensor(out=per_tile(shift, q), in0=per_tile(mean, q), scalar=-0.5, in1=per_tile(rstd, q), op0=ALU.mult, op1=ALU.mult).then_inc(shift_done, 1)

                    def add_skip(t, r):
                        dve.wait_ge(o_ps, t + 1)
                        o = projected(r)
                        x_s, x_v = X[:, bass.ds(t * F, S0)], X[:, bass.ds(t * F + S0, 3 * V1)].rearrange("p (v c) -> p v c", c=3)
                        k_s, k_v = o[:, F:F + S0], o[:, F + S0:2 * F].rearrange("p (c v) -> p v c", c=3)
                        if n == 0:
                            zc = z_sb[:, bass.ds(t, 1)]
                            dve.scalar_tensor_tensor(out=x_s, in0=k_s, scalar=zc, in1=x_s, op0=ALU.mult, op1=ALU.add)
                            dve.scalar_tensor_tensor(out=x_v, in0=k_v, scalar=zc, in1=x_v, op0=ALU.mult, op1=ALU.add).then_inc(skip_done, 1)
                        else:
                            dve.tensor_tensor(x_s, k_s, x_s, ALU.add)
                            dve.tensor_tensor(x_v, k_v, x_v, ALU.add).then_inc(skip_done, 1)

                    if n == 0:
                        beside["vector"](dve)
                    else:
                        scale_node_weights(dve, 1).then_inc(scaled, 1)
                        add_sums(0, 0, range(BATCH))
                    statistics(0, 0, range(BATCH))
                    moments_sums(0)
                    moments_scaled(0)
                    variance(0)
                    scale_shift(0)
                    if n == 0:
                        beside["vector_weights"](dve)
                    else:
                        add_sums(0, 1, range(BATCH))
                    statistics(0, 1, range(BATCH))
                    if n == 0:
                        dve.wait_ge(z_in, 16)

                    def batches(i):
                        for b, r, t, s in steps(i):
                            q = 2 * i + b
                            if within(q + 1, 0, NBATCH) and r < 3:
                                (moments_sums, variance, scale_shift)[r](q + 1)
                            add_skip(t, r)
                            if within(q + 1, 0, NBATCH) and r == 0:
                                moments_scaled(q + 1)
                            if within(q + 2, 0, NBATCH):
                                if r >= 1:
                                    statistics(i + 1, b, range(r - 1, r) if r < BATCH - 1 else range(r - 1, BATCH))
                                if n == 1 and r < BATCH - 1:
                                    add_sums(i + 1, b, range(r, r + 1) if r < BATCH - 2 else range(r, BATCH))
                            if n == 0 and isinstance(i, int) and t == 2 * BATCH - 1:
                                beside["vector_early"](dve)
                            if n == 0 and isinstance(i, int) and i > 0 and t % (2 * BATCH) < len(beside["vector_late"]):
                                beside["vector_late"][t % (2 * BATCH)](dve)
                    rolled(dve, NBATCH // 2, batches)
                    if n == 0:
                        beside["vector_end"](dve)

                @block.tensor
                def _(pe):
                    def transposes(t, s):
                        pe.wait_ge(norm_done, t + 1)
                        wait_for(pe, hT_done, t - 1)
                        nc.tensor.transpose(aps[s][0:3 * V1, P:2 * P], hn[:, s, S0:F], ident[:, :])
                        nc.tensor.transpose(aps[s][0:S0, 0:P], hn[:, s, 0:S0], ident[:, :]).then_inc(t_ps, 1)

                    def project(t, s, r):
                        pe.wait_ge(hT_done, t + 1)
                        wait_for(pe, row_done, t - BATCH + 1)
                        o = projected(r).rearrange("p (h f) -> p h f", h=2)
                        nc.tensor.matmul(o[:, :, 0:S0], hT[0:S0, s, 0, :], ra[n][:, :].rearrange("p (h f) -> p h f", h=2), start=True, stop=True)
                        nc.tensor.matmul(o[:, :, S0:F], hT[0:3 * V1, s, 1, :], rb[n][:, :].rearrange("p (h f) -> p h f", h=2), start=True, stop=True).then_inc(o_ps, 1)

                    if n == 0:
                        beside["tensor"](pe)
                    else:
                        pe.wait_ge(scaled, 1)
                    transposes(0, 0)

                    def batches(i):
                        for b, r, t, s in steps(i):
                            if within(t + 1, 0, NT):
                                transposes(t + 1, 1 - s)
                            keep_clock(1)
                            project(t, s, r)
                    rolled(pe, NBATCH // 2, batches)
                    if n == 0:
                        beside["tensor_end"](pe)

                @block.scalar
                def _(act):
                    def std(q):
                        act.wait_ge(var_eps, q + 1)
                        r = rstd[:, bass.ds(q * BATCH, BATCH)]
                        act.activation(r, r, ACT.Sqrt).then_inc(std_done, 1)

                    def norm(q, t, s):
                        act.wait_ge(shift_done, q + 1)
                        wait_for(act, t_ps, t - 1)
                        act.activation(hn[:, s, :], x_tile(t), ACT.Relu, scale=rstd[:, bass.ds(t, 1)], bias=shift[:, bass.ds(t, 1)]).then_inc(norm_done, 1)

                    def transposed(t, s):
                        act.wait_ge(t_ps, t + 1)
                        wait_for(act, o_ps, t - 1)
                        act.activation(hT[0:S0, s, 0, :], aps[s][0:S0, 0:P], ACT.Copy)
                        act.activation(hT[0:3 * V1, s, 1, :], aps[s][0:3 * V1, P:2 * P], ACT.Copy).then_inc(hT_done, 1)

                    def table_row(i, b, r, t):
                        act.wait_ge(skip_done, t + 1)
                        if r == 0:
                            wait_for(act, rows_out[b], 16 * i)
                        o = projected(r)[:, 0:F]
                        if n == 0:
                            act.activation(rows2[:, b, r, :], o, ACT.Copy, scale=z_sb[:, bass.ds(t, 1)]).then_inc(row_done, 1)
                        else:
                            act.activation(rows2[:, b, r, :], o, ACT.Copy).then_inc(row_done, 1)

                    std(0)
                    norm(0, 0, 0)
                    norm(0, 1, 1)
                    transposed(0, 0)

                    def batches(i):
                        for b, r, t, s in steps(i):
                            q = 2 * i + b
                            if within(t + 2, 0, NT):
                                norm(q + (r + 2) // BATCH, t + 2, s)
                            if within(t + 1, 0, NT):
                                transposed(t + 1, 1 - s)
                            if within(t - 2, 0, NT):
                                if r >= 2:
                                    table_row(i, b, r - 2, t - 2)
                                else:
                                    table_row(i if b == 1 else i - 1, 1 - b, r - 2 + BATCH, t - 2)
                            if r == 1 and within(q + 1, 0, NBATCH):
                                std(q + 1)
                    rolled(act, NBATCH // 2, batches)
                    for t in (NT - 2, NT - 1):
                        table_row(NBATCH // 2 - 1, 1, t % BATCH, t)

        def edge_phase(L):
            n = L.n
            idx_done = sem(f"idx_done{n}")
            edge_in = [sem(f"edge_in{n}{h}") for h in range(2)]
            gathered = [sem(f"gathered{n}{j}") for j in range(QUAD)]
            hid_ps, hid_done = sem(f"hid_ps{n}"), sem(f"hid_done{n}")
            w_ps = sem(f"w_ps{n}")
            eq_done, S_done, P_done = sem(f"eq_done{n}"), sem(f"S_done{n}"), sem(f"P_done{n}")
            agg_ps, agg_done = sem(f"agg_ps{n}"), sem(f"agg_done{n}")
            tr_ps, tr_done = sem(f"tr_ps{n}"), sem(f"tr_done{n}")
            sum_ps, sum_done = sem(f"sum_ps{n}"), sem(f"sum_done{n}")
            sum_out = [sem(f"sum_out{n}{j}") for j in range(QUAD)]
            split_in, split_hi, split_rest = sem(f"split_in{n}"), sem(f"split_hi{n}"), sem(f"split_rest{n}")
            split_mid, split_lo, split_out = sem(f"split_mid{n}"), sem(f"split_lo{n}"), sem(f"split_out{n}")
            c_in, c_gathered, c_added = sem(f"c_in{n}"), sem(f"c_gathered{n}"), sem(f"c_added{n}")
            c_hid_ps, c_hid, c_w = sem(f"c_hid_ps{n}"), sem(f"c_hid{n}"), sem(f"c_w{n}")
            c_dve, c_ready = sem(f"c_dve{n}"), sem(f"c_ready{n}")
            c_agg_ps, c_agg, c_tr_ps, c_tr = sem(f"c_agg_ps{n}"), sem(f"c_agg{n}"), sem(f"c_tr_ps{n}"), sem(f"c_tr{n}")
            c_sum_ps, c_sum = sem(f"c_sum_ps{n}"), sem(f"c_sum{n}")

            def is_windowed(eng):
                return eng.value_load(flag[0:1, 0:1], min_val=0, max_val=1) == 1

            def radial_matmul(out_ap, lhs_slot, e0, w):
                return nc.tensor.matmul(out_ap, fc1_st[:, :], rad[:, lhs_slot, e0:e0 + w], start=True, stop=True)

            def weight_matmul(out_ap, j, c):
                if n == 0:
                    return nc.tensor.matmul(out_ap, hid[:, j % 2, c * P:(c + 1) * P], fc2_sb[:, :], start=True, stop=True)
                e0 = j % 2 * SUP + c * P
                return nc.tensor.matmul(out_ap, query[:, j // 2, e0:e0 + P], tp_sb[:, :], start=True, stop=True)

            def products(dve, out_p, w, g, m):
                h1 = g[:, :, S0:F].rearrange("p c (d v) -> p c d v", d=3)

                def vec(col, w_col):
                    return dve.tensor_tensor(out_p[:, :, col:col + 3 * V1].rearrange("p c (d v) -> p c d v", d=3),
                                             w[:, :, w_col:w_col + V1].unsqueeze(2).broadcast_to([P, m, 3, V1]), h1, ALU.mult)
                dve.tensor_tensor(out_p[:, :, 0:2 * F].rearrange("p c (h f) -> p c h f", h=2)[:, :, :, 0:S0],
                                  w[:, :, 0:2 * S0].rearrange("p c (h f) -> p c h f", h=2),
                                  g[:, :, 0:S0].unsqueeze(2).broadcast_to([P, m, 2, S0]), ALU.mult)
                vec(S0, 2 * S0)
                if n == 1:
                    vec(2 * F, 2 * S0 + V1)
                return vec(F + S0, L.d_col)

            def aggregate_matmul(out_ap, s_ap, p_ap, k, start, stop, tile):
                cols = slice(0, F) if k == 0 else slice(F, L.pcols)
                return nc.tensor.matmul(out_ap, s_ap, p_ap[:, cols], start=start, stop=stop, tile_position=tile)

            def pack_component(act, dst, src, k, rows):
                c = k - 1
                last = act.activation(dst[rows, S0:S0 + V1], src[rows, S0 + c * V1:S0 + (c + 1) * V1], ACT.Copy)
                if n == 1:
                    m0, m1 = other_two(c)
                    b0 = S0 + 3 * V1
                    pair = src[rows, b0:b0 + 3 * V1].rearrange("p (m v) -> p m v", m=3)[:, m0:m1 + 1:m1 - m0, :]
                    last = act.activation(dst[rows, S0 + V1:F].rearrange("p (m v) -> p m v", m=2), pair, ACT.Copy)
                return last

            def sums_ps():
                return tps[:, 2 * P:2 * P + F]

            def output_matmuls():
                for k in range(4):
                    nc.tensor.matmul(sums_ps(), T1[0:L.k1, k, :, :].rearrange("p q w -> p (q w)"), r1[n][0:L.k1, k, :], start=(k == 0), stop=False)
                return nc.tensor.matmul(sums_ps(), T2[0:L.k2, :, :].rearrange("p q w -> p (q w)"), r2[n][0:L.k2, :], start=False, stop=True)

            with nc.Block() as block:
                @block.sync
                def _(sp):
                    def load_edges(i, h):
                        e0 = bass.ds(i * QUAD * SUP + h * 2 * SUP, 2 * SUP)
                        wait_for(sp, hid_ps if n == 0 else w_ps, QUAD * (i - 1) + 2 * h + 2)
                        if n == 0:
                            sp.wait_ge(split_out, 16 * (i + 1))
                            for a in range(PARTS):
                                r0 = a * PARTS * NEF
                                sp.dma_start(rad[r0:r0 + PARTS * NEF, h, :],
                                             split_d[bass.ds(i * PARTS * NEF, PARTS * NEF), h * 2 * SUP:(h + 1) * 2 * SUP]).then_inc(edge_in[h], 16)
                        else:
                            sp.dma_start(query[:, h, :], query_t[:, e0]).then_inc(edge_in[h], 16)

                    def store_sums(i, j):
                        before = 2 * (j // 2) + j % 2 - 2 if j >= 2 else j + 2
                        start = sp.value_load(base_sb[0:1, bass.ds(QUAD * i + j, 1)], min_val=0, max_val=NPAD - WIN)
                        to = acc[n][j % 2, bass.ds(start, WIN), :]
                        waits_alone(sp, sum_done, i + 1, 1)
                        waits_alone(sp, sum_out[before], 16 * (i + 1) if j >= 2 else 16 * i, 16)
                        sp.dma_start(to, sums[j * WIN:(j + 1) * WIN, :]).then_inc(sum_out[j], 16)

                    def load_split(q):
                        wait_for(sp, split_rest, q)
                        sp.dma_start(rad_f[:, :], rad_q[bass.ds(q * SPLIT_P, SPLIT_P), :]).then_inc(split_in, 16)

                    def store_split(q):
                        sp.wait_ge(split_lo, q + 1)
                        to = split_d[bass.ds(q * PARTS * NEF, PARTS * NEF), :].rearrange("(a i) (s f) -> (i s) a f", a=PARTS, s=SPLIT)
                        sp.dma_start(to, rad_p[:, :, :]).then_inc(split_out, 16)

                    def quad(i):
                        if within(i + 1, 0, NQUAD):
                            load_edges(i + 1, 0)
                            if not isinstance(i, int) or (i + 1) * QUAD + 2 < NSUP:
                                load_edges(i + 1, 1)
                        if n == 0 and within(i + 3, 0, NQUAD):
                            load_split(i + 3)
                        if n == 0 and within(i + 2, 0, NQUAD):
                            store_split(i + 2)
                        if within(i - 1, 0, NQUAD):
                            for j in range(QUAD):
                                store_sums(i - 1, j)

                    def drain():
                        for j in range(LAST):
                            store_sums(NQUAD - 1, j)
                        for j in range(QUAD):
                            sp.wait_ge(sum_out[j], 16 * (NQUAD if j < LAST else NQUAD - 1))

                    def chunk(m):
                        waits_alone(sp, c_added, 16 * m, 16)
                        e0 = bass.ds(m * P, P)
                        sp.dma_start(idx[:, 0, 0:1], src_t[:, bass.ds(m, 1)]).then_inc(c_in, 16)
                        sp.dma_start(g_dst[:, :], dst_t[:, bass.ds(m, 1)]).then_inc(c_in, 16)
                        sp.dma_start(g_row[:, :], dst_flat[e0].partition_broadcast(P)).then_inc(c_in, 16)
                        sp.dma_start(g_y[:, :], y_t[:, bass.ds(4 * m, 4)]).then_inc(c_in, 16)
                        if n == 0:
                            sp.dma_start(g_rad[:, :], rad_t[:, e0]).then_inc(c_in, 16)
                        else:
                            sp.dma_start(query[:, 0, 0:P], query_t[:, e0]).then_inc(c_in, 16)

                    with sp.If(is_windowed(sp)):
                        if n == 0:
                            load_split(0)
                            load_split(1)
                            store_split(0)
                        load_edges(0, 0)
                        load_edges(0, 1)
                        if n == 0:
                            load_split(2)
                            store_split(1)
                        quad(0)
                        quad(1)
                        with sp.Fori(2, NQUAD - 3) as i:
                            quad(i)
                        quad(NQUAD - 3)
                        quad(NQUAD - 2)
                        quad(NQUAD - 1)
                        drain()
                    with sp.Else():
                        chunk(0)
                        with sp.Fori(1, NCH) as m:
                            chunk(m)
                        sp.wait_ge(c_added, 16 * NCH)

                loads_per_chunk = 16 * 5
                edge_loads = 16 * (PARTS if n == 0 else 1)

                @block.gpsimd
                def _(pool):
                    def gather(i, j):
                        g = QUAD * i + j
                        waits_alone(pool, idx_done, g + 1, 1)
                        for c in range(CHUNKS):
                            pool.indirect_dma_start(out=G[:, j, c, :], out_offset=None, in_=table[n][:, :],
                                                    in_offset=bass.IndirectOffsetOnAxis(ap=idx[:, j, c:c + 1], axis=0)).then_inc(gathered[j], 16)

                    def quad(i):
                        for j in range(QUAD):
                            if within(QUAD * i + j, 0, NSUP):
                                gather(i, j)

                    def chunk(m):
                        waits_alone(pool, c_in, loads_per_chunk * (m + 1), loads_per_chunk)
                        pool.indirect_dma_start(out=G[:, 0, 0, :], out_offset=None, in_=table[n][:, :],
                                                in_offset=bass.IndirectOffsetOnAxis(ap=idx[:, 0, 0:1], axis=0)).then_inc(c_gathered, 16)
                        waits_alone(pool, c_ready, m + 1, 1)
                        pool.wait_ge(c_sum, m + 1)
                        pool.indirect_dma_start(out=acc[n][0], out_offset=bass.IndirectOffsetOnAxis(ap=g_to[:, 0:1], axis=0),
                                                in_=sums[:, :], in_offset=None, compute_op=ALU.add).then_inc(c_added, 16)

                    with pool.If(is_windowed(pool)):
                        rolled(pool, NQUAD, quad)
                    with pool.Else():
                        with pool.Fori(0, NCH) as m:
                            chunk(m)

                @block.tensor
                def _(pe):
                    def hidden(i, j):
                        g = QUAD * i + j
                        pe.wait_ge(edge_in[j // 2], edge_loads * (i + 1))
                        wait_for(pe, hid_done, g)
                        radial_matmul(hps[0:RN, 0:SUP], j // 2, j % 2 * SUP, SUP).then_inc(hid_ps, 1)

                    def radial_weights(i, j):
                        g = QUAD * i + j
                        if n == 0:
                            pe.wait_ge(hid_done, g + 1)
                        else:
                            pe.wait_ge(edge_in[j // 2], edge_loads * (i + 1))
                        wait_for(pe, P_done, g - 1)
                        for c in range(CHUNKS):
                            last = weight_matmul(wps[j % 2][:, c, 0:L.wcols], j, c)
                        last.then_inc(w_ps, 1)

                    def aggregate(i, j):
                        g = QUAD * i + j
                        b = j % 2
                        pe.wait_ge(S_done, g + 1)
                        pe.wait_ge(P_done, g + 1)
                        wait_for(pe, agg_done, g - 1)
                        for c in range(CHUNKS):
                            for k in range(4):
                                width = F if k == 0 else L.agg
                                last = aggregate_matmul(aps[b][k * WIN:(k + 1) * WIN, 0:width], S[:, b, c, k, :], Pr[:, b, c, :],
                                                        k, c == 0, c == CHUNKS - 1, (0, k * WIN))
                        last.then_inc(agg_ps, 1)

                    def transposes(g, b, quads_out=None):
                        pe.wait_ge(agg_done, g + 1)
                        if quads_out is not None:
                            wait_for(pe, sum_done, quads_out)
                        wait_for(pe, tr_done, g)
                        nc.tensor.transpose(tps[0:L.k1, 0:P], agg_sb[:, b, 0:L.k1], ident[:, :])
                        if n == 0:
                            last = nc.tensor.transpose(tps[0:2 * V1, P:P + WIN], agg_sb[0:WIN, b, L.k1:F], ident[0:WIN, 0:WIN])
                        else:
                            last = nc.tensor.transpose(tps[0:V1, P:2 * P], agg_sb[:, b, L.k1:F], ident[:, :])
                        last.then_inc(tr_ps, 1)

                    def output(i):
                        pe.wait_ge(tr_done, min(NSUP, QUAD * (i + 1)) if isinstance(i, int) else QUAD * (i + 1))
                        wait_for(pe, sum_done, i)
                        output_matmuls().then_inc(sum_ps, 1)

                    def quad(i):
                        for j in range(QUAD):
                            g = QUAD * i + j
                            if not within(g, 0, NSUP):
                                break
                            if n == 0 and within(g + 2, 0, NSUP):
                                hidden(i + (j + 2) // QUAD, (j + 2) % QUAD)
                            if within(g + 1, 0, NSUP):
                                radial_weights(i + (j + 1) // QUAD, (j + 1) % QUAD)
                            aggregate(i, j)
                            if j == 1 and within(i - 1, 0, NQUAD):
                                output(i - 1)
                            if within(g - 1, 0, NSUP):
                                transposes(g - 1, (j - 1) % 2, i if j == 1 else None)

                    def chunk(m):
                        pe.wait_ge(c_in, loads_per_chunk * (m + 1))
                        if n == 0:
                            nc.tensor.matmul(hps[0:RN, 0:P], fc1_sb[:, :], g_rad[:, :], start=True, stop=True).then_inc(c_hid_ps, 1)
                            pe.wait_ge(c_hid, m + 1)
                        weight_matmul(wps[0][:, 0, 0:L.wcols], 0, 0).then_inc(c_w, 1)
                        pe.wait_ge(c_ready, m + 1)
                        for k in range(4):
                            width = F if k == 0 else L.agg
                            last = aggregate_matmul(aps[k // 2][:, 256 * (k % 2):256 * (k % 2) + width], g_S[:, k, :], Pr[:, 0, 0, :], k, True, True, None)
                        last.then_inc(c_agg_ps, 1)
                        pe.wait_ge(c_agg, m + 1)
                        for k in range(4):
                            last = nc.tensor.transpose(wps[1][0:L.k1, k // 2, P * (k % 2):P * (k % 2) + P], g_agg[:, k, 0:L.k1], ident[:, :])
                        if n == 0:
                            last = nc.tensor.transpose(wps[1][0:2 * V1, 2, 0:P], g_agg[:, 0, L.k1:F], ident[:, :])
                        else:
                            for k in range(4):
                                last = nc.tensor.transpose(wps[1][0:V1, 2 + k // 2, P * (k % 2):P * (k % 2) + P], g_agg[:, k, L.k1:F], ident[:, :])
                        last.then_inc(c_tr_ps, 1)
                        pe.wait_ge(c_tr, m + 1)
                        output_matmuls().then_inc(c_sum_ps, 1)

                    with pe.If(is_windowed(pe)):
                        keep_clock(16)
                        if n == 0:
                            hidden(0, 0)
                            hidden(0, 1)
                        radial_weights(0, 0)
                        rolled(pe, NQUAD, quad, tail=2)
                        if LAST == 1:
                            output(NQUAD - 2)
                        transposes(NSUP - 1, (NSUP - 1) % 2, NQUAD - 1)
                        output(NQUAD - 1)
                    with pe.Else():
                        with pe.Fori(0, NCH) as m:
                            chunk(m)

                @block.scalar
                def _(act):
                    def silu(g, b):
                        act.wait_ge(hid_ps, g + 1)
                        wait_for(act, w_ps, g - 1)
                        act.activation(hid[:, b, :], hps[0:RN, 0:SUP], ACT.Silu, scale=NEF ** -0.5).then_inc(hid_done, 1)

                    def split_high(q):
                        act.wait_ge(split_in, 16 * (q + 1))
                        wait_for(act, split_out, 16 * q)
                        act.activation(rad_p[:, 0, :], rad_f[:, :], ACT.Copy).then_inc(split_hi, 1)

                    def split_middle(q):
                        act.wait_ge(split_rest, q + 1)
                        act.activation(rad_p[:, 1, :], rad_r[:, :], ACT.Copy).then_inc(split_mid, 1)

                    def pack(g, b):
                        act.wait_ge(agg_ps, g + 1)
                        wait_for(act, tr_ps, g - 1)
                        act.activation(agg_sb[:, b, 0:S0], aps[b][:, 0:S0], ACT.Copy)
                        act.activation(agg_sb[0:WIN, b, S0:F], aps[b][0:WIN, S0:F], ACT.Copy)
                        for k in range(1, 4):
                            last = pack_component(act, agg_sb[:, b, :], aps[b], k, slice(k * WIN, (k + 1) * WIN))
                        last.then_inc(agg_done, 1)

                    def transposed(i, j):
                        g = QUAD * i + j
                        act.wait_ge(tr_ps, g + 1)
                        if j == 0:
                            wait_for(act, sum_ps, i)
                        last = act.activation(T1[0:L.k1, :, j, :], tps[0:L.k1, 0:P].rearrange("p (k w) -> p k w", k=4), ACT.Copy)
                        if n == 0:
                            last = act.activation(T2[0:2 * V1, j, :], tps[0:2 * V1, P:P + WIN], ACT.Copy)
                        else:
                            for k in range(4):
                                last = act.activation(T2[k * V1:(k + 1) * V1, j, :], tps[0:V1, P + k * WIN:P + (k + 1) * WIN], ACT.Copy)
                        last.then_inc(tr_done, 1)

                    def window_sums(i):
                        act.wait_ge(sum_ps, i + 1)
                        for j in range(QUAD):
                            wait_for(act, sum_out[j], 16 * i)
                        act.activation(sums[:, :], sums_ps(), ACT.Copy).then_inc(sum_done, 1)

                    def quad(i):
                        for j in range(QUAD):
                            g = QUAD * i + j
                            if not within(g, 0, NSUP):
                                break
                            if n == 0 and within(g + 2, 0, NSUP):
                                silu(g + 2, j % 2)
                            if n == 0 and j < 2 and within(i + 2, 0, NQUAD):
                                (split_high, split_middle)[j](i + 2)
                            pack(g, j % 2)
                            if j == 1 and within(i - 1, 0, NQUAD):
                                window_sums(i - 1)
                            if within(g - 1, 0, NSUP):
                                transposed(i - 1 if j == 0 else i, (j - 1) % QUAD)

                    def chunk(m):
                        if n == 0:
                            act.wait_ge(c_hid_ps, m + 1)
                            act.activation(hid[:, 0, 0:P], hps[0:RN, 0:P], ACT.Silu, scale=NEF ** -0.5).then_inc(c_hid, 1)
                        act.wait_ge(c_agg_ps, m + 1)
                        every = slice(0, P)
                        act.activation(g_agg[:, 0, :], aps[0][:, 0:F], ACT.Copy)
                        for k in range(1, 4):
                            at = aps[k // 2][:, 256 * (k % 2):256 * (k % 2) + 256]
                            act.activation(g_agg[:, k, 0:S0], at[:, 0:S0], ACT.Copy)
                            last = pack_component(act, g_agg[:, k, :], at, k, every)
                        last.then_inc(c_agg, 1)
                        act.wait_ge(c_tr_ps, m + 1)
                        for k in range(4):
                            last = act.activation(T1[0:L.k1, k, :, :].rearrange("p q w -> p (q w)"), wps[1][0:L.k1, k // 2, P * (k % 2):P * (k % 2) + P], ACT.Copy)
                        if n == 0:
                            last = act.activation(T2[0:2 * V1, :, :].rearrange("p q w -> p (q w)"), wps[1][0:2 * V1, 2, 0:P], ACT.Copy)
                        else:
                            for k in range(4):
                                last = act.activation(T2[k * V1:(k + 1) * V1, :, :].rearrange("p q w -> p (q w)"),
                                                      wps[1][0:V1, 2 + k // 2, P * (k % 2):P * (k % 2) + P], ACT.Copy)
                        last.then_inc(c_tr, 1)
                        act.wait_ge(c_sum_ps, m + 1)
                        act.activation(sums[:, :], sums_ps(), ACT.Copy).then_inc(c_sum, 1)

                    with act.If(is_windowed(act)):
                        if n == 0:
                            for q in range(2):
                                split_high(q)
                                split_middle(q)
                            silu(0, 0)
                            silu(1, 1)
                        rolled(act, NQUAD, quad, tail=2)
                        if LAST == 1:
                            window_sums(NQUAD - 2)
                        transposed(NQUAD - 1, LAST - 1)
                        window_sums(NQUAD - 1)
                    with act.Else():
                        with act.Fori(0, NCH) as m:
                            chunk(m)

                @block.vector
                def _(dve):
                    def select(i, j):
                        g = QUAD * i + j
                        wait_for(dve, S_done, g - 1)
                        dve.tensor_tensor(eq[:, j % 2, :, :], win[:, :].unsqueeze(1).broadcast_to([P, CHUNKS, WIN]),
                                          meta_sb[:, bass.ds(g * CHUNKS, CHUNKS), 0:1].broadcast_to([P, CHUNKS, WIN]), ALU.is_equal).then_inc(eq_done, 1)

                    def scale(g, j):
                        dve.wait_ge(eq_done, g + 1)
                        wait_for(dve, agg_ps, g - 1)
                        shape = [P, CHUNKS, 4, WIN]
                        dve.tensor_tensor(S[:, j % 2, :, :, :], eq[:, j % 2, :, :].unsqueeze(2).broadcast_to(shape),
                                          meta_sb[:, bass.ds(g * CHUNKS, CHUNKS), 1:5].unsqueeze(3).broadcast_to(shape), ALU.mult).then_inc(S_done, 1)

                    def multiply(i, j):
                        g = QUAD * i + j
                        dve.wait_ge(w_ps, g + 1)
                        dve.wait_ge(gathered[j], 16 * CHUNKS * (i + 1))
                        wait_for(dve, agg_ps, g - 1)
                        products(dve, Pr[:, j % 2, :, :], wps[j % 2][:, 0:CHUNKS, :], G[:, j, :, :], CHUNKS).then_inc(P_done, 1)

                    def indices(g, j):
                        dve.tensor_copy(idx[:, j, :], src_sb[:, bass.ds(g * CHUNKS, CHUNKS)]).then_inc(idx_done, 1)

                    def split_remainder(q):
                        dve.wait_ge(split_hi, q + 1)
                        wait_for(dve, split_mid, q)
                        dve.tensor_tensor(rad_r[:, :], rad_f[:, :], rad_p[:, 0, :], ALU.subtract).then_inc(split_rest, 1)

                    def split_low(q):
                        dve.wait_ge(split_mid, q + 1)
                        dve.tensor_tensor(rad_p[:, 2, :], rad_r[:, :], rad_p[:, 1, :], ALU.subtract).then_inc(split_lo, 1)

                    def quad(i):
                        for j in range(QUAD):
                            g = QUAD * i + j
                            if not within(g, 0, NSUP):
                                break
                            if n == 0 and j in (1, 2) and within(i + 2, 0, NQUAD):
                                (split_remainder, split_low)[j - 1](i + 2)
                            more = within(g + 1, 0, NSUP)
                            if more:
                                select(i + (j + 1) // QUAD, (j + 1) % QUAD)
                            multiply(i, j)
                            if within(g + QUAD, 0, NSUP):
                                indices(g + QUAD, j)
                            if more:
                                scale(g + 1, (j + 1) % QUAD)

                    DUP_OPS = 8

                    def chunk(m):
                        s = [0]

                        def link(ins):
                            s[0] += 1
                            ins.then_inc(c_dve, 1)
                            dve.wait_ge(c_dve, DUP_OPS * m + s[0])
                        dve.wait_ge(c_in, loads_per_chunk * (m + 1))
                        link(dve.tensor_copy(g_dstf[:, :], g_dst[:, :]))
                        link(dve.tensor_copy(g_rowf[:, :], g_row[:, :]))
                        link(dve.tensor_scalar(g_eq[:, :], g_rowf[:, :], g_dstf[:, 0:1], None, ALU.is_equal))
                        shape = [P, 4, P]
                        dve.tensor_tensor(g_S[:, :, :], g_eq[:, :].unsqueeze(1).broadcast_to(shape), g_y[:, :].unsqueeze(2).broadcast_to(shape), ALU.mult)
                        link(dve.tensor_tensor(g_tmp[:, :], g_eq[:, :], g_low[:, :], ALU.mult))
                        link(dve.tensor_reduce(out=g_dup[:, 0:1], in_=g_tmp[:, :], op=ALU.max, axis=AX.X))
                        link(dve.tensor_tensor(g_dup[:, 1:2], g_dead[:, :], g_dstf[:, :], ALU.subtract))
                        link(dve.scalar_tensor_tensor(out=g_dup[:, 1:2], in0=g_dup[:, 1:2], scalar=g_dup[:, 0:1], in1=g_dstf[:, :], op0=ALU.mult, op1=ALU.add))
                        link(dve.tensor_copy(g_to[:, :], g_dup[:, 1:2]))
                        assert s[0] == DUP_OPS
                        dve.wait_ge(c_w, m + 1)
                        dve.wait_ge(c_gathered, 16 * (m + 1))
                        products(dve, Pr[:, 0, 0:1, :], wps[0][:, 0:1, :], G[:, 0, 0:1, :], 1).then_inc(c_ready, 1)

                    with dve.If(is_windowed(dve)):
                        for j in range(QUAD):
                            indices(j, j)
                        if n == 0:
                            for q in range(2):
                                split_remainder(q)
                                split_low(q)
                        select(0, 0)
                        scale(0, 0)
                        rolled(dve, NQUAD, quad, tail=2)
                    with dve.Else():
                        with dve.Fori(0, NCH) as m:
                            chunk(m)

        def output_phase():
            SLOTS = 4
            acc_in = [sem(f"out_in{b}") for b in range(SLOTS)]
            added = sem("added")
            out_done = [sem(f"out_done{b}") for b in range(SLOTS)]
            with nc.sbuf_tensor("accout", [P, SLOTS, 2, BATCH, F], F32) as accout, nc.Block() as block:
                @block.sync
                def _(sp):
                    for q in range(NBATCH):
                        b = q % SLOTS
                        if q >= SLOTS:
                            sp.wait_ge(out_done[b], 16 * (q // SLOTS))
                        for h in range(2):
                            src = acc[1][h, q * BATCH * P:(q + 1) * BATCH * P, :].rearrange("(t p) f -> p t f", p=P)
                            sp.dma_start(accout[:, b, h, :, :], src).then_inc(acc_in[b], 16)

                @block.scalar
                def _(act):
                    for q in range(NBATCH):
                        b = q % SLOTS
                        act.wait_ge(added, 2 * q + 2)
                        act.dma_start(out[q * BATCH * P:(q + 1) * BATCH * P, :].rearrange("(t p) f -> p t f", p=P), accout[:, b, 1, :, :]).then_inc(out_done[b], 16)
                    for b in range(SLOTS):
                        act.wait_ge(out_done[b], 16 * len(range(b, NBATCH, SLOTS)))

                @block.vector
                def _(dve):
                    for q in range(NBATCH):
                        b = q % SLOTS
                        dve.wait_ge(acc_in[b], 32 * (q // SLOTS + 1))
                        dve.tensor_tensor(accout[:, b, 0, :, :], accout[:, b, 0, :, :], accout[:, b, 1, :, :], ALU.add).then_inc(added, 1)
                        dve.wait_ge(added, 2 * q + 1)
                        x_b = X[:, q * BATCH * F:(q + 1) * BATCH * F].rearrange("p (t f) -> p t f", f=F)
                        dve.tensor_tensor(accout[:, b, 1, :, :], accout[:, b, 0, :, :], x_b, ALU.add).then_inc(added, 1)

        first_phase()
        edge_phase(L0)
        node_phase(1, None)
        edge_phase(L1)
        output_phase()


def kernel(x, src, dst, edge_attr_12, edge_attr_4, edge_attr_64, node_vec1,
           L0_gnn_W_sc0, L0_gnn_W_sc1, L0_gnn_W_l1_0, L0_gnn_W_l1_1, L0_gnn_W_fc1, L0_gnn_W_fc2, L0_gnn_W_l2_0, L0_gnn_W_l2_1,
           L1_gnn_si_w0, L1_gnn_si_w1, L1_gnn_lin1_w0, L1_gnn_lin1_w1, L1_gnn_tp_weight, L1_gnn_lin2_w0, L1_gnn_lin2_w1):
    import concourse.bacc as bacc
    from concourse.bass_utils import run_bass_kernel_spmd

    def pad(a, rows, mode="constant"):
        a = np.asarray(a)
        return np.pad(a, [(0, rows - a.shape[0])] + [(0, 0)] * (a.ndim - 1), mode=mode)

    def by_chunk(a):
        a = a.reshape((-1, P) + a.shape[1:])
        return np.ascontiguousarray(np.moveaxis(a, 0, 1).reshape(P, -1))

    dst_pad = pad(dst, EPAD, "edge")
    dst_pad[NSUP * SUP:] = np.repeat(np.arange(N, N + ALLSUP - NSUP, dtype=dst_pad.dtype), SUP)
    base = np.concatenate([dst_pad[::SUP], np.full(2, NPAD - 1, dst_pad.dtype)]).reshape(1, -1)
    arrays = {
        "x": pad(x, NPAD),
        "z_t": np.ascontiguousarray(pad(node_vec1, NPAD).reshape(NT, P).T),
        "src_t": by_chunk(pad(src, EPAD)),
        "dst_t": by_chunk(dst_pad),
        "dst_flat": dst_pad,
        "base_row": base,
        "y_t": by_chunk(pad(edge_attr_4, EPAD)),
        "rad_t": np.ascontiguousarray(pad(edge_attr_12, EPAD).T),
        "rad_q": np.ascontiguousarray(pad(edge_attr_12, EPAD).reshape(NQUAD, QUAD * SUP, NEF).transpose(0, 2, 1)).reshape(NQUAD * SPLIT_P, SPLIT_W),
        "query_t": np.ascontiguousarray(pad(edge_attr_64, EPAD).T),
        "w_sc0": L0_gnn_W_sc0, "w_sc1": L0_gnn_W_sc1, "w_l10": L0_gnn_W_l1_0, "w_l11": L0_gnn_W_l1_1,
        "w_fc1": L0_gnn_W_fc1, "w_fc2": L0_gnn_W_fc2, "w_l20": L0_gnn_W_l2_0, "w_l21": L0_gnn_W_l2_1,
        "si_w0": L1_gnn_si_w0, "si_w1": L1_gnn_si_w1, "lin1_w0": L1_gnn_lin1_w0, "lin1_w1": L1_gnn_lin1_w1,
        "tp_w": L1_gnn_tp_weight, "lin2_w0": L1_gnn_lin2_w0, "lin2_w1": L1_gnn_lin2_w1,
    }
    arrays = {k: np.ascontiguousarray(v) for k, v in arrays.items()}
    nc = bacc.Bacc("TRN2", target_bir_lowering=False, num_devices=1)
    aps = {k: nc.dram_tensor(k, v.shape, mybir.dt.from_np(v.dtype), kind="ExternalInput").ap() for k, v in arrays.items()}
    out = nc.dram_tensor("out", (NPAD, F), F32, kind="ExternalOutput").ap()
    gnn_kernel(nc, out=out, **aps)
    r = run_bass_kernel_spmd(nc, [arrays], core_ids=[0])
    return r.results[0]["out"][:N]
```
